# Optimizing a Trainium2 kernel written in Bass

```python
import numpy as np
import jax
import jax.numpy as jnp

def _softmax(x, axis=-1):
    return jax.nn.softmax(x, axis=axis)

def _gelu(x):
    return jax.nn.gelu(x, approximate=True)

def _silu(x):
    return jax.nn.silu(x)

def _sigmoid(x):
    return jax.nn.sigmoid(x)

def _layernorm(x, axis=-1, eps=1e-05):
    m = jnp.mean(x, axis=axis, keepdims=True)
    v = jnp.var(x, axis=axis, keepdims=True)
    return (x - m) / jnp.sqrt(v + eps)

def _scatter_add(tgt, idx, src, axis=0):
    return tgt.at[idx].add(src)

def _segment_sum(src, seg, n):
    return jax.ops.segment_sum(src, seg, n)
kernel_name = 'mk_cond_seq_d4_seqx_r4_2d3fc2'

def setup_inputs(seed: int=0):
    np.random.seed(seed)
    _w = jnp.asarray

    def _rec_inputs():
        import jax
        import jax.numpy as jnp
        _rk = jax.random.key(seed)
        x = -0.0003929 + 0.9999 * jax.random.normal(jax.random.fold_in(_rk, 1), (8, 512, 256), jnp.float32)
        _lenS = 512 - jax.random.randint(jax.random.fold_in(_rk, 7), (8,), 0, max(1, 512 // 4) + 1, jnp.int32)
        _lenS2 = 512 - jax.random.randint(jax.random.fold_in(_rk, 8), (8,), 0, max(1, 512 // 4) + 1, jnp.int32)
        cond_2048 = 0.00782532 + 1.00527 * jax.random.normal(jax.random.fold_in(_rk, 11), (8, 512), jnp.float32)
        itok_S_0_1023 = jax.random.randint(jax.random.fold_in(_rk, 13), (512,), 0, 256, jnp.int32)
        _validS = jnp.arange(512)[None, :] < _lenS[:, None]
        _validS2 = jnp.arange(512)[None, :] < _lenS2[:, None]
        _causal = jnp.tril(jnp.ones((512, 512), dtype=bool))
        mask_BxS_ik0 = jnp.where(jnp.broadcast_to(_validS[:, :], (8, 512)), 0, 1).astype(jnp.int32)
        mask_BxSx1_fk1 = jnp.where(jnp.ones((8, 512, 1), dtype=bool), 1.0, 0.0).astype(jnp.float32)
        return (x, cond_2048, itok_S_0_1023, mask_BxS_ik0, mask_BxSx1_fk1)
    x, cond_2048, itok_S_0_1023, mask_BxS_ik0, mask_BxSx1_fk1 = _rec_inputs()

    def _L0_cond_setup():
        import jax, jax.numpy as jnp
        import numpy as np
        H = 16
        LN_EPS = 1e-05

        def _layernorm(x, scale, bias):
            mu = jnp.mean(x, axis=-1, keepdims=True)
            var = jnp.var(x, axis=-1, keepdims=True)
            return (x - mu) * jax.lax.rsqrt(var + LN_EPS) * scale + bias
        key = jax.random.key(seed)
        ks = jax.random.split(key, 8)
        B, T, D, E = (4, 1024, 256, 512)
        s = 0.02
        return {'x': jax.random.normal(ks[0], (B, T, D), jnp.float32), 'emb': jax.random.normal(ks[1], (B, E), jnp.float32), 'src_mask': jax.random.randint(ks[2], (B, T), 0, 2).astype(jnp.int32), 'norm_scale': jnp.ones((D,), jnp.float32), 'norm_bias': jnp.zeros((D,), jnp.float32), 'Wq': jax.random.normal(ks[3], (D, D), jnp.float32) * s, 'bq': jnp.zeros((D,), jnp.float32), 'Wk': jax.random.normal(ks[4], (D, D), jnp.float32) * s, 'bk': jnp.zeros((D,), jnp.float32), 'Wv': jax.random.normal(ks[5], (D, D), jnp.float32) * s, 'bv': jnp.zeros((D,), jnp.float32), 'film_emb_W': jax.random.normal(ks[6], (E, 2 * D), jnp.float32) * s, 'film_emb_b': jnp.zeros((2 * D,), jnp.float32), 'film_norm_scale': jnp.ones((D,), jnp.float32), 'film_norm_bias': jnp.zeros((D,), jnp.float32), 'film_out_W': jax.random.normal(ks[7], (D, D), jnp.float32) * s, 'film_out_b': jnp.zeros((D,), jnp.float32)}
    _L0_cond_all = _L0_cond_setup()
    _L0_cond_in = {k: v for k, v in _L0_cond_all.items() if k in ('norm_scale', 'norm_bias', 'Wq', 'bq', 'Wk', 'bk', 'Wv', 'bv', 'film_emb_W', 'film_emb_b', 'film_norm_scale', 'film_norm_bias', 'film_out_W', 'film_out_b')}
    del _L0_cond_all

    def _L1_cond_setup():
        import jax, jax.numpy as jnp
        import numpy as np
        D = 256
        DI = 512
        N = 16
        DT_RANK = 64
        D_CONV = 4
        EPS = 1e-05

        def _layernorm(x, g, b):
            mu = jnp.mean(x, axis=-1, keepdims=True)
            var = jnp.mean((x - mu) ** 2, axis=-1, keepdims=True)
            return (x - mu) * jax.lax.rsqrt(var + EPS) * g + b

        def _mamba(xn, in_proj_w, conv_w, conv_b, x_proj_w, dt_proj_w, dt_proj_b, A_log, D_param, out_proj_w):
            b, sl, _ = xn.shape
            xz = jnp.einsum('bsd,ed->bse', xn, in_proj_w)
            x_in, z = jnp.split(xz, 2, axis=-1)
            xt = jnp.transpose(x_in, (0, 2, 1))
            u = jax.lax.conv_general_dilated(xt, conv_w[:, None, :], (1,), [(D_CONV - 1, 0)], feature_group_count=DI, dimension_numbers=('NCH', 'OIH', 'NCH')) + conv_b[None, :, None]
            u = jax.nn.silu(jnp.transpose(u, (0, 2, 1)))
            x_dbl = jnp.einsum('bsd,ed->bse', u, x_proj_w)
            dt_r, B, C = jnp.split(x_dbl, [DT_RANK, DT_RANK + N], axis=-1)
            dt = jax.nn.softplus(jnp.einsum('bsr,dr->bsd', dt_r, dt_proj_w) + dt_proj_b)
            A = -jnp.exp(A_log)

            def step(h, inp):
                dt_t, B_t, C_t, u_t = inp
                dA = jnp.exp(dt_t[:, :, None] * A)
                h = h * dA + (dt_t * u_t)[:, :, None] * B_t[:, None, :]
                y = jnp.einsum('bdn,bn->bd', h, C_t)
                return (h, y)
            seq = (jnp.transpose(dt, (1, 0, 2)), jnp.transpose(B, (1, 0, 2)), jnp.transpose(C, (1, 0, 2)), jnp.transpose(u, (1, 0, 2)))
            h0 = jnp.zeros((b, DI, N), xn.dtype)
            _, ys = jax.lax.scan(step, h0, seq)
            y = jnp.transpose(ys, (1, 0, 2)) + u * D_param
            y = y * jax.nn.silu(z)
            return jnp.einsum('bsd,ed->bse', y, out_proj_w)
        key = jax.random.key(seed)
        ks = jax.random.split(key, 16)
        s = lambda fan: 1.0 / np.sqrt(fan)
        inp = {'x': jax.random.normal(ks[0], (2, 512, D), jnp.float32), 'c': jax.random.normal(ks[1], (2, 2 * D), jnp.float32), 'ln_g': jnp.ones((D,), jnp.float32), 'ln_b': jnp.zeros((D,), jnp.float32), 'ada_w': jax.random.normal(ks[2], (3 * D, 2 * D), jnp.float32) * s(2 * D), 'ada_b': jnp.zeros((3 * D,), jnp.float32), 'in_proj_w': jax.random.normal(ks[3], (2 * DI, D), jnp.float32) * s(D), 'conv_w': jax.random.normal(ks[4], (DI, D_CONV), jnp.float32) * s(D_CONV), 'conv_b': jnp.zeros((DI,), jnp.float32), 'x_proj_w': jax.random.normal(ks[5], (DT_RANK + 2 * N, DI), jnp.float32) * s(DI), 'dt_proj_w': jax.random.normal(ks[6], (DI, DT_RANK), jnp.float32) * s(DT_RANK), 'dt_proj_b': jax.random.uniform(ks[7], (DI,), jnp.float32, -4.0, -2.0), 'A_log': jnp.tile(jnp.log(jnp.arange(1, N + 1, dtype=jnp.float32)), (DI, 1)), 'D_param': jnp.ones((DI,), jnp.float32), 'out_proj_w': jax.random.normal(ks[8], (D, DI), jnp.float32) * s(DI)}
        return inp
    _L1_cond_all = _L1_cond_setup()
    _L1_cond_in = {k: v for k, v in _L1_cond_all.items() if k in ('ln_g', 'ln_b', 'ada_w', 'ada_b', 'in_proj_w', 'conv_w', 'conv_b', 'x_proj_w', 'dt_proj_w', 'dt_proj_b', 'A_log', 'D_param', 'out_proj_w')}
    del _L1_cond_all

    def _L2_cond_setup():
        import jax, jax.numpy as jnp
        import numpy as np
        B_SZ, S, D = (4, 256, 256)
        DI, DS, DTR, DC = (512, 16, 64, 4)
        EPS = 1e-05

        def _layernorm(x, g, b):
            m = jnp.mean(x, axis=-1, keepdims=True)
            v = jnp.var(x, axis=-1, keepdims=True)
            return (x - m) * jax.lax.rsqrt(v + EPS) * g + b

        def _mamba(h, W_in, conv_w, conv_b, W_xp, W_dt, b_dt, A_log, D_param, W_out):
            bsz = h.shape[0]
            xz = h @ W_in
            xm, z = jnp.split(xz, 2, axis=-1)
            xc = jnp.transpose(xm, (0, 2, 1))
            xc = jax.lax.conv_general_dilated(xc, conv_w, (1,), [(DC - 1, 0)], feature_group_count=DI, dimension_numbers=('NCH', 'OIH', 'NCH'))
            xc = xc + conv_b[None, :, None]
            xm = jax.nn.silu(jnp.transpose(xc, (0, 2, 1)))
            xdbl = xm @ W_xp
            dtr, Bm, Cm = jnp.split(xdbl, [DTR, DTR + DS], axis=-1)
            dt = jax.nn.softplus(dtr @ W_dt + b_dt)
            A = -jnp.exp(A_log)

            def step(hst, inp):
                dt_t, B_t, C_t, x_t = inp
                dA = jnp.exp(dt_t[:, :, None] * A)
                hst = hst * dA + (dt_t * x_t)[:, :, None] * B_t[:, None, :]
                y = jnp.einsum('bds,bs->bd', hst, C_t)
                return (hst, y)
            inputs = (jnp.transpose(dt, (1, 0, 2)), jnp.transpose(Bm, (1, 0, 2)), jnp.transpose(Cm, (1, 0, 2)), jnp.transpose(xm, (1, 0, 2)))
            h0 = jnp.zeros((bsz, DI, DS), dt.dtype)
            _, ys = jax.lax.scan(step, h0, inputs)
            y = jnp.transpose(ys, (1, 0, 2)) + xm * D_param
            y = y * jax.nn.silu(z)
            return y @ W_out
        key = jax.random.key(seed)
        ks = jax.random.split(key, 12)

        def w(k, shape, scale=0.02):
            return jax.random.normal(k, shape, jnp.float32) * scale
        x = jax.random.normal(ks[0], (B_SZ, S, D), jnp.float32)
        c = jax.random.normal(ks[1], (B_SZ, 2 * D), jnp.float32)
        W_ada = w(ks[2], (2 * D, 3 * D))
        b_ada = jnp.zeros((3 * D,), jnp.float32)
        gamma = jnp.ones((D,), jnp.float32)
        beta = jnp.zeros((D,), jnp.float32)
        W_in = w(ks[3], (D, 2 * DI))
        conv_w = w(ks[4], (DI, 1, DC), 0.1)
        conv_b = jnp.zeros((DI,), jnp.float32)
        W_xp = w(ks[5], (DI, DTR + 2 * DS))
        W_dt = w(ks[6], (DTR, DI))
        b_dt = jnp.full((DI,), jnp.log(jnp.expm1(jnp.float32(0.01))), jnp.float32)
        A_log = jnp.log(jnp.broadcast_to(jnp.arange(1, DS + 1, dtype=jnp.float32), (DI, DS)))
        D_param = jnp.ones((DI,), jnp.float32)
        W_out = w(ks[7], (DI, D))
        perm = jax.random.permutation(ks[8], S)
        inv_perm = jnp.argsort(perm)
        return dict(x=x, c=c, W_ada=W_ada, b_ada=b_ada, gamma=gamma, beta=beta, W_in=W_in, conv_w=conv_w, conv_b=conv_b, W_xp=W_xp, W_dt=W_dt, b_dt=b_dt, A_log=A_log, D_param=D_param, W_out=W_out, perm=perm, inv_perm=inv_perm)
    _L2_cond_all = _L2_cond_setup()
    _L2_cond_in = {k: v for k, v in _L2_cond_all.items() if k in ('W_ada', 'b_ada', 'gamma', 'beta', 'W_in', 'conv_w', 'conv_b', 'W_xp', 'W_dt', 'b_dt', 'A_log', 'D_param', 'W_out')}
    del _L2_cond_all

    def _L3_cond_setup():
        import jax, jax.numpy as jnp
        import numpy as np
        B, T, D, H, TE = (4, 512, 256, 8, 512)
        EPS = 1e-05

        def _ln(x, w, b):
            m = jnp.mean(x, axis=-1, keepdims=True)
            v = jnp.mean((x - m) ** 2, axis=-1, keepdims=True)
            return (x - m) * jax.lax.rsqrt(v + EPS) * w + b
        key = jax.random.key(seed)
        ks = jax.random.split(key, 16)
        s = 0.02
        inp = {'x': jax.random.normal(ks[0], (B, T, D), jnp.float32), 'emb': jax.random.normal(ks[1], (B, TE), jnp.float32), 'src_mask': (jax.random.uniform(ks[2], (B, T, 1)) > 0.2).astype(jnp.float32), 'num_head': H, 'ln_w': jnp.ones((D,), jnp.float32), 'ln_b': jnp.zeros((D,), jnp.float32), 'Wq': jax.random.normal(ks[3], (D, D), jnp.float32) * s, 'bq': jnp.zeros((D,), jnp.float32), 'Wk': jax.random.normal(ks[4], (D, D), jnp.float32) * s, 'bk': jnp.zeros((D,), jnp.float32), 'Wv': jax.random.normal(ks[5], (D, D), jnp.float32) * s, 'bv': jnp.zeros((D,), jnp.float32), 'W_emb': jax.random.normal(ks[6], (TE, 2 * D), jnp.float32) * s, 'b_emb': jnp.zeros((2 * D,), jnp.float32), 'ln2_w': jnp.ones((D,), jnp.float32), 'ln2_b': jnp.zeros((D,), jnp.float32), 'W_out': jax.random.normal(ks[7], (D, D), jnp.float32) * s, 'b_out': jnp.zeros((D,), jnp.float32)}
        return inp
    _L3_cond_all = _L3_cond_setup()
    _L3_cond_in = {k: v for k, v in _L3_cond_all.items() if k in ('ln_w', 'ln_b', 'Wq', 'bq', 'Wk', 'bk', 'Wv', 'bv', 'W_emb', 'b_emb', 'ln2_w', 'ln2_b', 'W_out', 'b_out')}
    del _L3_cond_all
    return {'x': x, 'cond_2048': cond_2048, 'itok_S_0_1023': itok_S_0_1023, 'mask_BxS_ik0': mask_BxS_ik0, 'mask_BxSx1_fk1': mask_BxSx1_fk1, 'L0_cond_norm_scale': _L0_cond_in['norm_scale'], 'L0_cond_norm_bias': _L0_cond_in['norm_bias'], 'L0_cond_Wq': _L0_cond_in['Wq'], 'L0_cond_bq': _L0_cond_in['bq'], 'L0_cond_Wk': _L0_cond_in['Wk'], 'L0_cond_bk': _L0_cond_in['bk'], 'L0_cond_Wv': _L0_cond_in['Wv'], 'L0_cond_bv': _L0_cond_in['bv'], 'L0_cond_film_emb_W': _L0_cond_in['film_emb_W'], 'L0_cond_film_emb_b': _L0_cond_in['film_emb_b'], 'L0_cond_film_norm_scale': _L0_cond_in['film_norm_scale'], 'L0_cond_film_norm_bias': _L0_cond_in['film_norm_bias'], 'L0_cond_film_out_W': _L0_cond_in['film_out_W'], 'L0_cond_film_out_b': _L0_cond_in['film_out_b'], 'L1_cond_ln_g': _L1_cond_in['ln_g'], 'L1_cond_ln_b': _L1_cond_in['ln_b'], 'L1_cond_ada_w': _L1_cond_in['ada_w'], 'L1_cond_ada_b': _L1_cond_in['ada_b'], 'L1_cond_in_proj_w': _L1_cond_in['in_proj_w'], 'L1_cond_conv_w': _L1_cond_in['conv_w'], 'L1_cond_conv_b': _L1_cond_in['conv_b'], 'L1_cond_x_proj_w': _L1_cond_in['x_proj_w'], 'L1_cond_dt_proj_w': _L1_cond_in['dt_proj_w'], 'L1_cond_dt_proj_b': _L1_cond_in['dt_proj_b'], 'L1_cond_A_log': _L1_cond_in['A_log'], 'L1_cond_D_param': _L1_cond_in['D_param'], 'L1_cond_out_proj_w': _L1_cond_in['out_proj_w'], 'L2_cond_W_ada': _L2_cond_in['W_ada'], 'L2_cond_b_ada': _L2_cond_in['b_ada'], 'L2_cond_gamma': _L2_cond_in['gamma'], 'L2_cond_beta': _L2_cond_in['beta'], 'L2_cond_W_in': _L2_cond_in['W_in'], 'L2_cond_conv_w': _L2_cond_in['conv_w'], 'L2_cond_conv_b': _L2_cond_in['conv_b'], 'L2_cond_W_xp': _L2_cond_in['W_xp'], 'L2_cond_W_dt': _L2_cond_in['W_dt'], 'L2_cond_b_dt': _L2_cond_in['b_dt'], 'L2_cond_A_log': _L2_cond_in['A_log'], 'L2_cond_D_param': _L2_cond_in['D_param'], 'L2_cond_W_out': _L2_cond_in['W_out'], 'L3_cond_ln_w': _L3_cond_in['ln_w'], 'L3_cond_ln_b': _L3_cond_in['ln_b'], 'L3_cond_Wq': _L3_cond_in['Wq'], 'L3_cond_bq': _L3_cond_in['bq'], 'L3_cond_Wk': _L3_cond_in['Wk'], 'L3_cond_bk': _L3_cond_in['bk'], 'L3_cond_Wv': _L3_cond_in['Wv'], 'L3_cond_bv': _L3_cond_in['bv'], 'L3_cond_W_emb': _L3_cond_in['W_emb'], 'L3_cond_b_emb': _L3_cond_in['b_emb'], 'L3_cond_ln2_w': _L3_cond_in['ln2_w'], 'L3_cond_ln2_b': _L3_cond_in['ln2_b'], 'L3_cond_W_out': _L3_cond_in['W_out'], 'L3_cond_b_out': _L3_cond_in['b_out']}

def reference(x, cond_2048, itok_S_0_1023, mask_BxS_ik0, mask_BxSx1_fk1, L0_cond_norm_scale, L0_cond_norm_bias, L0_cond_Wq, L0_cond_bq, L0_cond_Wk, L0_cond_bk, L0_cond_Wv, L0_cond_bv, L0_cond_film_emb_W, L0_cond_film_emb_b, L0_cond_film_norm_scale, L0_cond_film_norm_bias, L0_cond_film_out_W, L0_cond_film_out_b, L1_cond_ln_g, L1_cond_ln_b, L1_cond_ada_w, L1_cond_ada_b, L1_cond_in_proj_w, L1_cond_conv_w, L1_cond_conv_b, L1_cond_x_proj_w, L1_cond_dt_proj_w, L1_cond_dt_proj_b, L1_cond_A_log, L1_cond_D_param, L1_cond_out_proj_w, L2_cond_W_ada, L2_cond_b_ada, L2_cond_gamma, L2_cond_beta, L2_cond_W_in, L2_cond_conv_w, L2_cond_conv_b, L2_cond_W_xp, L2_cond_W_dt, L2_cond_b_dt, L2_cond_A_log, L2_cond_D_param, L2_cond_W_out, L3_cond_ln_w, L3_cond_ln_b, L3_cond_Wq, L3_cond_bq, L3_cond_Wk, L3_cond_bk, L3_cond_Wv, L3_cond_bv, L3_cond_W_emb, L3_cond_b_emb, L3_cond_ln2_w, L3_cond_ln2_b, L3_cond_W_out, L3_cond_b_out):
    import jax
    import jax.numpy as jnp

    def _L0_cond_ref(x, emb, src_mask, norm_scale, norm_bias, Wq, bq, Wk, bk, Wv, bv, film_emb_W, film_emb_b, film_norm_scale, film_norm_bias, film_out_W, film_out_b):
        import jax, jax.numpy as jnp
        import numpy as np
        H = 16
        LN_EPS = 1e-05

        def _layernorm(x, scale, bias):
            mu = jnp.mean(x, axis=-1, keepdims=True)
            var = jnp.var(x, axis=-1, keepdims=True)
            return (x - mu) * jax.lax.rsqrt(var + LN_EPS) * scale + bias
        B, T, D = x.shape
        dh = D // H
        xn = _layernorm(x, norm_scale, norm_bias)
        q = xn @ Wq + bq
        k = xn @ Wk + bk
        v = xn @ Wv + bv
        mask = (src_mask == 1)[:, :, None]
        k = jnp.where(mask, -jnp.inf, k)
        v = jnp.where(mask, 0.0, v)
        q = q.reshape(B, T, H, dh).transpose(0, 2, 1, 3)
        k = k.reshape(B, T, H, dh).transpose(0, 2, 1, 3)
        v = v.reshape(B, T, H, dh).transpose(0, 2, 1, 3)
        q = jax.nn.softmax(q, axis=-1)
        k = jax.nn.softmax(k, axis=2)
        attn = jnp.einsum('bhse,bhsd->bhed', k, v)
        y = jnp.einsum('bhtd,bhed->bhte', q, attn)
        y = y.transpose(0, 2, 1, 3).reshape(B, T, D)
        emb_out = jax.nn.silu(emb) @ film_emb_W + film_emb_b
        scale, shift = jnp.split(emb_out, 2, axis=-1)
        h = _layernorm(y, film_norm_scale, film_norm_bias) * (1.0 + scale[:, None, :]) + shift[:, None, :]
        h = jax.nn.silu(h) @ film_out_W + film_out_b
        return x + h

    def _L1_cond_ref(x, c, ln_g, ln_b, ada_w, ada_b, in_proj_w, conv_w, conv_b, x_proj_w, dt_proj_w, dt_proj_b, A_log, D_param, out_proj_w):
        import jax, jax.numpy as jnp
        import numpy as np
        D = 256
        DI = 512
        N = 16
        DT_RANK = 64
        D_CONV = 4
        EPS = 1e-05

        def _layernorm(x, g, b):
            mu = jnp.mean(x, axis=-1, keepdims=True)
            var = jnp.mean((x - mu) ** 2, axis=-1, keepdims=True)
            return (x - mu) * jax.lax.rsqrt(var + EPS) * g + b

        def _mamba(xn, in_proj_w, conv_w, conv_b, x_proj_w, dt_proj_w, dt_proj_b, A_log, D_param, out_proj_w):
            b, sl, _ = xn.shape
            xz = jnp.einsum('bsd,ed->bse', xn, in_proj_w)
            x_in, z = jnp.split(xz, 2, axis=-1)
            xt = jnp.transpose(x_in, (0, 2, 1))
            u = jax.lax.conv_general_dilated(xt, conv_w[:, None, :], (1,), [(D_CONV - 1, 0)], feature_group_count=DI, dimension_numbers=('NCH', 'OIH', 'NCH')) + conv_b[None, :, None]
            u = jax.nn.silu(jnp.transpose(u, (0, 2, 1)))
            x_dbl = jnp.einsum('bsd,ed->bse', u, x_proj_w)
            dt_r, B, C = jnp.split(x_dbl, [DT_RANK, DT_RANK + N], axis=-1)
            dt = jax.nn.softplus(jnp.einsum('bsr,dr->bsd', dt_r, dt_proj_w) + dt_proj_b)
            A = -jnp.exp(A_log)

            def step(h, inp):
                dt_t, B_t, C_t, u_t = inp
                dA = jnp.exp(dt_t[:, :, None] * A)
                h = h * dA + (dt_t * u_t)[:, :, None] * B_t[:, None, :]
                y = jnp.einsum('bdn,bn->bd', h, C_t)
                return (h, y)
            seq = (jnp.transpose(dt, (1, 0, 2)), jnp.transpose(B, (1, 0, 2)), jnp.transpose(C, (1, 0, 2)), jnp.transpose(u, (1, 0, 2)))
            h0 = jnp.zeros((b, DI, N), xn.dtype)
            _, ys = jax.lax.scan(step, h0, seq)
            y = jnp.transpose(ys, (1, 0, 2)) + u * D_param
            y = y * jax.nn.silu(z)
            return jnp.einsum('bsd,ed->bse', y, out_proj_w)
        ada = jnp.einsum('bc,ec->be', jax.nn.silu(c), ada_w) + ada_b
        shift, scale, gate = jnp.split(ada, 3, axis=1)
        xn = _layernorm(x, ln_g, ln_b)
        xn = xn * (1.0 + scale[:, None, :]) + shift[:, None, :]
        x_ssm = _mamba(xn, in_proj_w, conv_w, conv_b, x_proj_w, dt_proj_w, dt_proj_b, A_log, D_param, out_proj_w)
        return x + gate[:, None, :] * x_ssm

    def _L2_cond_ref(x, c, W_ada, b_ada, gamma, beta, W_in, conv_w, conv_b, W_xp, W_dt, b_dt, A_log, D_param, W_out, perm, inv_perm):
        import jax, jax.numpy as jnp
        import numpy as np
        B_SZ, S, D = (4, 256, 256)
        DI, DS, DTR, DC = (512, 16, 64, 4)
        EPS = 1e-05

        def _layernorm(x, g, b):
            m = jnp.mean(x, axis=-1, keepdims=True)
            v = jnp.var(x, axis=-1, keepdims=True)
            return (x - m) * jax.lax.rsqrt(v + EPS) * g + b

        def _mamba(h, W_in, conv_w, conv_b, W_xp, W_dt, b_dt, A_log, D_param, W_out):
            bsz = h.shape[0]
            xz = h @ W_in
            xm, z = jnp.split(xz, 2, axis=-1)
            xc = jnp.transpose(xm, (0, 2, 1))
            xc = jax.lax.conv_general_dilated(xc, conv_w, (1,), [(DC - 1, 0)], feature_group_count=DI, dimension_numbers=('NCH', 'OIH', 'NCH'))
            xc = xc + conv_b[None, :, None]
            xm = jax.nn.silu(jnp.transpose(xc, (0, 2, 1)))
            xdbl = xm @ W_xp
            dtr, Bm, Cm = jnp.split(xdbl, [DTR, DTR + DS], axis=-1)
            dt = jax.nn.softplus(dtr @ W_dt + b_dt)
            A = -jnp.exp(A_log)

            def step(hst, inp):
                dt_t, B_t, C_t, x_t = inp
                dA = jnp.exp(dt_t[:, :, None] * A)
                hst = hst * dA + (dt_t * x_t)[:, :, None] * B_t[:, None, :]
                y = jnp.einsum('bds,bs->bd', hst, C_t)
                return (hst, y)
            inputs = (jnp.transpose(dt, (1, 0, 2)), jnp.transpose(Bm, (1, 0, 2)), jnp.transpose(Cm, (1, 0, 2)), jnp.transpose(xm, (1, 0, 2)))
            h0 = jnp.zeros((bsz, DI, DS), dt.dtype)
            _, ys = jax.lax.scan(step, h0, inputs)
            y = jnp.transpose(ys, (1, 0, 2)) + xm * D_param
            y = y * jax.nn.silu(z)
            return y @ W_out
        mod = jax.nn.silu(c) @ W_ada + b_ada
        shift, scale, gate = jnp.split(mod, 3, axis=1)
        h = _layernorm(x, gamma, beta)
        h = h * (1.0 + scale[:, None, :]) + shift[:, None, :]
        h = h[:, perm]
        y = _mamba(h, W_in, conv_w, conv_b, W_xp, W_dt, b_dt, A_log, D_param, W_out)
        y = y[:, inv_perm]
        return x + gate[:, None, :] * y

    def _L3_cond_ref(x, emb, src_mask, num_head, ln_w, ln_b, Wq, bq, Wk, bk, Wv, bv, W_emb, b_emb, ln2_w, ln2_b, W_out, b_out):
        import jax, jax.numpy as jnp
        import numpy as np
        B, T, D, H, TE = (4, 512, 256, 8, 512)
        EPS = 1e-05

        def _ln(x, w, b):
            m = jnp.mean(x, axis=-1, keepdims=True)
            v = jnp.mean((x - m) ** 2, axis=-1, keepdims=True)
            return (x - m) * jax.lax.rsqrt(v + EPS) * w + b
        b, t, d = x.shape
        h = num_head
        dh = d // h
        xn = _ln(x, ln_w, ln_b)
        q = xn @ Wq + bq
        k = xn @ Wk + bk + (1.0 - src_mask) * -1000000.0
        q = jax.nn.softmax(q.reshape(b, t, h, dh), axis=-1)
        k = jax.nn.softmax(k.reshape(b, t, h, dh), axis=1)
        v = ((xn @ Wv + bv) * src_mask).reshape(b, t, h, dh)
        att = jnp.einsum('bnhd,bnhl->bhdl', k, v)
        y = jnp.einsum('bnhd,bhdl->bnhl', q, att).reshape(b, t, d)
        emb_out = (jax.nn.silu(emb) @ W_emb + b_emb)[:, None, :]
        scale, shift = jnp.split(emb_out, 2, axis=2)
        hh = _ln(y, ln2_w, ln2_b) * (1.0 + scale) + shift
        hh = jax.nn.silu(hh) @ W_out + b_out
        return x + hh
    x = _L0_cond_ref(x, cond_2048, mask_BxS_ik0, L0_cond_norm_scale, L0_cond_norm_bias, L0_cond_Wq, L0_cond_bq, L0_cond_Wk, L0_cond_bk, L0_cond_Wv, L0_cond_bv, L0_cond_film_emb_W, L0_cond_film_emb_b, L0_cond_film_norm_scale, L0_cond_film_norm_bias, L0_cond_film_out_W, L0_cond_film_out_b)
    x = _L1_cond_ref(x, cond_2048, L1_cond_ln_g, L1_cond_ln_b, L1_cond_ada_w, L1_cond_ada_b, L1_cond_in_proj_w, L1_cond_conv_w, L1_cond_conv_b, L1_cond_x_proj_w, L1_cond_dt_proj_w, L1_cond_dt_proj_b, L1_cond_A_log, L1_cond_D_param, L1_cond_out_proj_w)
    x = _L2_cond_ref(x, cond_2048, L2_cond_W_ada, L2_cond_b_ada, L2_cond_gamma, L2_cond_beta, L2_cond_W_in, L2_cond_conv_w, L2_cond_conv_b, L2_cond_W_xp, L2_cond_W_dt, L2_cond_b_dt, L2_cond_A_log, L2_cond_D_param, L2_cond_W_out, itok_S_0_1023, itok_S_0_1023)
    x = _L3_cond_ref(x, cond_2048, mask_BxSx1_fk1, 8, L3_cond_ln_w, L3_cond_ln_b, L3_cond_Wq, L3_cond_bq, L3_cond_Wk, L3_cond_bk, L3_cond_Wv, L3_cond_bv, L3_cond_W_emb, L3_cond_b_emb, L3_cond_ln2_w, L3_cond_ln2_b, L3_cond_W_out, L3_cond_b_out)
    return x

_drawn_inputs = setup_inputs


def setup_inputs(seed=0):
    import zlib

    import numpy as np

    out = dict(_drawn_inputs(seed))
    spreads = {'L0_cond_norm_scale': (1.0, 0.2),
     'L0_cond_norm_bias': (0.0, 0.1),
     'L0_cond_bq': (0.0, 0.1),
     'L0_cond_bk': (0.0, 0.1),
     'L0_cond_bv': (0.0, 0.1),
     'L0_cond_film_emb_b': (0.0, 0.1),
     'L0_cond_film_norm_scale': (1.0, 0.2),
     'L0_cond_film_norm_bias': (0.0, 0.1),
     'L0_cond_film_out_b': (0.0, 0.1),
     'L1_cond_ln_g': (1.0, 0.2),
     'L1_cond_ln_b': (0.0, 0.1),
     'L1_cond_ada_b': (0.0, 0.1),
     'L1_cond_conv_b': (0.0, 0.1),
     'L1_cond_D_param': (1.0, 0.2),
     'L2_cond_b_ada': (0.0, 0.1),
     'L2_cond_gamma': (1.0, 0.2),
     'L2_cond_beta': (0.0, 0.1),
     'L2_cond_conv_b': (0.0, 0.1),
     'L2_cond_b_dt': (-4.600166320800781, 0.2),
     'L2_cond_D_param': (1.0, 0.2),
     'L3_cond_ln_w': (1.0, 0.2),
     'L3_cond_ln_b': (0.0, 0.1),
     'L3_cond_bq': (0.0, 0.1),
     'L3_cond_bk': (0.0, 0.1),
     'L3_cond_bv': (0.0, 0.1),
     'L3_cond_b_emb': (0.0, 0.1),
     'L3_cond_ln2_w': (1.0, 0.2),
     'L3_cond_ln2_b': (0.0, 0.1),
     'L3_cond_b_out': (0.0, 0.1)}
    factors = {}
    for name, (base, spread) in spreads.items():
        noise = np.random.default_rng([zlib.crc32(name.encode()), seed]).standard_normal(out[name].shape)
        drawn = base * np.exp(spread * noise) if base else spread * noise
        out[name] = jnp.asarray(drawn.astype(out[name].dtype))
    for name, factor in factors.items():
        out[name] = (out[name] * factor).astype(out[name].dtype)
    return out
```

```python
from contextlib import ExitStack

import concourse.bass as bass
from concourse import mybir

P = 128
B, T, D = 8, 512, 256
TT, DC = T // P, D // P
DI, CH, N = 512, 4, 16
DTR, TAPS = 64, 4
E = 512
EC = E // P
NB = 2 * N
EPS = 1e-5
MASKED = -1e30
HEADS = (16, 8)
ATT, SSM = (0, 3), (1, 2)
SLOTS = 3

ALU = mybir.AluOpType
ACT = mybir.ActivationFunctionType
AX = mybir.AxisListType.X
F32, BF16, I32 = mybir.dt.float32, mybir.dt.bfloat16, mybir.dt.int32

ATT_PACK = (("wq", DC * D), ("wk", DC * D), ("wv", DC * D), ("wo", DC * D), ("bk", DC),
            ("norm_g", DC), ("norm_b", DC), ("film_g", DC), ("film_b", DC), ("emb_b", 2 * DC), ("heads", P))
SSM_PACK = (("w_in", DC * 2 * DI), ("w_x", CH * (DTR + 3 * NB)), ("w_dt", DI), ("w_out", CH * D),
            ("conv_w", CH * TAPS), ("conv_b", CH), ("dt_b", CH), ("a_log", CH * N), ("d_skip", CH),
            ("norm_g", DC), ("norm_b", DC), ("ada_b", 3 * DC))
CONST_PACK = (("ident", P), ("token", TT), ("cond", EC * B), ("keep3", B * TT), ("ones", P))


def columns(pack):
    at, out = 0, {}
    for name, n in pack:
        out[name] = (at, at + n)
        at += n
    return out, at


MOD_SCALE = {layer: 2 * DC * layer for layer in range(4)}
MOD_SHIFT = {layer: 2 * DC * layer + DC for layer in range(4)}
MOD_KEEP = {0: 8 * DC, 3: 8 * DC + TT}
MOD_PICK = 8 * DC + 2 * TT
MODS = MOD_PICK + 1

ATT_DVE_LINKS, SSM_DVE_LINKS = 12, 11


def bass_cond_seq(nc, x, out, mask_cols, mask_rows0, mask_rows3, order, const_pack, sel, att_packs, ssm_packs,
                  film_w, ada_w, att_rows, gate_rows):
    ctx = ExitStack()
    with ctx:
        def sb(name, shape, dt=F32):
            return ctx.enter_context(nc.sbuf_tensor(name, shape, dt))

        def sem(name):
            return ctx.enter_context(nc.semaphore(name))

        bank = [ctx.enter_context(nc.psum_tensor(f"bank{k}", [P, 512], F32)) for k in range(8)]

        catt, n_att = columns(ATT_PACK)
        cssm, n_ssm = columns(SSM_PACK)
        cconst, n_const = columns(CONST_PACK)
        att_sb = {layer: sb(f"att_pack{layer}", [P, n_att]) for layer in ATT}
        ssm_sb = {layer: sb(f"ssm_pack{layer}", [P, n_ssm]) for layer in SSM}
        const_sb = sb("const_sb", [P, n_const])
        sel_sb = sb("sel_sb", [3 * NB, NB * P], BF16)

        def aw(layer, name):
            return att_sb[layer][:, catt[name][0]:catt[name][1]]

        def sw(layer, name):
            return ssm_sb[layer][:, cssm[name][0]:cssm[name][1]]

        def cw(name):
            return const_sb[:, cconst[name][0]:cconst[name][1]]

        ident = cw("ident")
        ones_row, ones_row8 = cw("ones")[0:1, :], cw("ones")[0:B, :]
        att_bias = {layer: sb(f"att_bias{layer}", [P, 3, D]) for layer in ATT}
        permute = sb("permute", [P, TT, T])
        mask_i = sb("mask_i", [P, B * TT], I32)
        neg_half = sb("neg_half", [P, TT])
        mod_all = sb("mod_all", [P, B, MODS])
        mod_raw = sb("mod_raw", [P, 3 * DC, B])
        mod = sb("mod", [P, MODS])
        gate_row = sb("gate_row", [B, 2 * D])
        gate = sb("gate", [P, 2, D])
        gate_nat = sb("gate_nat", [B, 2, D])
        silu_c = sb("silu_c", [P, EC, B])
        half_w = {layer: sb(f"half_w{layer}", [P, CH * TAPS]) for layer in SSM}
        half_cb = {layer: sb(f"half_cb{layer}", [P, CH]) for layer in SSM}
        neg_a = {layer: sb(f"neg_a{layer}", [P, CH * N]) for layer in SSM}

        x_in = sb("x_in", [P, TT, D])
        x_res = sb("x_res", [P, TT, D])
        x_bias = sb("x_bias", [P, TT, D])
        x_out = x_bias
        mrow_i = sb("mrow_i", [1, T], I32)
        mrow3 = sb("mrow3", [1, T])
        stats = sb("stats", [P, TT, 6])
        mv = sb("mv", [P, TT, 2])
        var_eps = sb("var_eps", [P, TT])
        rstd = sb("rstd", [P, TT])
        xn = sb("xn", [P, TT, D])
        xnT = sb("xnT", [P, DC, T])

        kmax = sb("kmax", [P, DC])
        kshift = sb("kshift", [P, DC])
        ksum = sb("ksum", [P, DC])
        krec = sb("krec", [P, DC])
        kexp = sb("kexp", [P, DC, T])
        mask_row = kexp[0:1, 0, :]
        knat = sb("knat", [P, TT, D])
        gate_bias = knat[0:B, 0:2, :]
        qstat = sb("qstat", [P, TT * 16])
        qT = sb("qT", [P, DC, T])
        order_i = qT[:, 0, :].bitcast(I32)
        att = sb("att", [P, DC, P])

        xpad = sb("xpad", [P, CH, T + TAPS - 1])
        u = sb("u", [P, CH, T])
        zh = sb("zh", [P, CH, T])
        q, v = (zh[:, 2 * h:2 * h + 2, :].rearrange("p c (t d) -> p (c t) d", d=D) for h in range(2))
        dt = sb("dt", [P, CH, T])
        dtu = sb("dtu", [P, CH, T])
        dtr = xpad[0:DTR, 0, 0:T]
        bc_rest = xpad[0:3 * NB, 1, 0:T]
        bc_parts = sb("bc_parts", [3 * NB, T], BF16)
        decay = sb("decay", [P, 2, CH, T])
        state = sb("state", [P, SLOTS, CH, T])
        b_rows = sb("b_rows", [P, 2, T])
        zt = state[:, SLOTS - 1]

        film_sb = {0: decay[:, 0], 3: decay[:, 1]}
        ada_flat = state[:].rearrange("p s c t -> p (s c t)")
        ada_sb = {1: ada_flat[:, 0:EC * 3 * D].rearrange("p (k n) -> p k n", k=EC),
                  2: ada_flat[:, EC * 3 * D:2 * EC * 3 * D].rearrange("p (k n) -> p k n", k=EC)}

        s_const, s_att_w, s_ssm_w, s_cond_w, s_rows = (sem(n) for n in (
            "const_loaded", "att_weights_loaded", "ssm_weights_loaded", "cond_weights_loaded", "rows_loaded"))
        s_silu_t, s_silu, s_cond_pe, s_cond_ev, s_gate_nat, s_gate_pe, s_gate_ev, s_pro, s_neg_a, s_setup, s_zero = (
            sem(n) for n in ("cond_tanh", "cond_silu", "mod_product", "mod_evacuated", "gate_rows_ready",
                             "gate_spread", "gate_evacuated", "setup_links", "neg_a_exp", "setup_done", "zeroed"))
        s_x, s_mrow, s_mod, s_out_ready, s_out = (sem(n) for n in (
            "x_loaded", "mask_rows_loaded", "mod_ready", "x_out_ready", "x_out_stored"))
        s_var, s_rstd, s_xn, s_xT, s_xnT = (sem(n) for n in (
            "variance_ready", "rstd_ready", "xn_ready", "xn_turned", "xnT_ready"))
        a_links, a_mask, a_k, a_q, a_v, a_kshift, a_kexp, a_kn, a_kT, a_knat, a_qev, a_qsub, a_qexp, a_qn, a_qT, \
            a_qTs, a_vadd, a_vs, a_att, a_atts, a_y, a_yT, a_hid, a_tanh, a_act, a_o, a_xb = (sem("a_" + n) for n in (
                "links", "mask_row", "k_product", "q_product", "v_product", "kshift_ready", "k_exp", "k_normed",
                "k_turned", "k_natural", "q_evacuated", "q_shifted", "q_exp", "q_normed", "q_turned", "qT_ready",
                "v_biased", "v_ready", "att_product", "att_ready", "y_product", "y_turned", "hidden_half",
                "hidden_tanh", "hidden_ready", "out_product", "x_biased"))
        m_links, m_in, m_xpad, m_z, m_conv, m_ut, m_u, m_x, m_dtr, m_parts, m_dtp, m_abs, m_relu, m_ln, m_lnl, m_dt, \
            m_dtu, m_sz, m_bps, m_brow, m_cps, m_decay, m_inject, m_scan, m_prod, m_sum, m_gated, m_o, m_og, m_g = (
                sem("m_" + n) for n in (
                    "links", "in_product", "conv_input", "gate_in", "conv", "u_tanh", "u_ready", "x_product",
                    "dtr_ready", "bc_parts", "dt_product", "dt_abs", "dt_relu", "dt_log", "dt_log_links", "dt_ready",
                    "dtu_ready", "silu_z", "b_spread", "b_rows", "c_spread", "decay_ready", "inject_ready", "scanned",
                    "weighted", "summed", "gated", "out_product", "out_gated", "gathered"))

        block = ctx.enter_context(nc.Block())

        @block.sync
        def _(sp):
            sp.dma_start(const_sb[:], const_pack).then_inc(s_const, 16)
            sp.dma_start(mask_i[:], mask_cols).then_inc(s_const, 16)
            sp.dma_start(order_i, order.partition_broadcast(P)).then_inc(s_const, 16)
            sp.dma_start(film_sb[0], film_w[0].rearrange("(k p) n -> p k n", p=P)).then_inc(s_cond_w, 16)
            sp.dma_start(att_sb[0][:], att_packs[0]).then_inc(s_att_w, 16)
            sp.dma_start(ada_sb[1], ada_w[1].rearrange("(k p) n -> p k n", p=P)).then_inc(s_cond_w, 16)
            sp.dma_start(ssm_sb[1][:], ssm_packs[1]).then_inc(s_ssm_w, 16)
            sp.dma_start(ssm_sb[2][:], ssm_packs[2]).then_inc(s_ssm_w, 16)
            sp.dma_start(sel_sb[:], sel).then_inc(s_const, 16)

            def load(i):
                sp.dma_start(x_in[:], x[i].rearrange("(t p) d -> p t d", p=P)).then_inc(s_x, 16)
                sp.dma_start(mrow_i[:], mask_rows0[bass.ds(i, 1), :]).then_inc(s_mrow, 16)
                sp.dma_start(mrow3[:], mask_rows3[bass.ds(i, 1), :]).then_inc(s_mrow, 16)

            def store(i):
                sp.wait_ge(s_out_ready, i + 1)
                sp.dma_start(out[i].rearrange("(t p) d -> p t d", p=P), x_out[:]).then_inc(s_out, 16)

            load(0)
            with sp.Fori(0, B - 1) as i:
                store(i)
                load(i + 1)
            store(B - 1)
            sp.wait_ge(s_out, 16 * B)

        @block.gpsimd
        def _(pool):
            pool.memset(neg_half[:], -0.5).then_inc(s_zero, 1)
            pool.memset(xpad[:, :, 0:TAPS - 1], 0.0).then_inc(s_zero, 1)
            pool.wait_ge(s_rows, 16 * 8)
            pool.wait_ge(s_zero, 2)
            pool.wait_ge(s_cond_pe, 4)
            pool.wait_ge(s_gate_nat, 2)
            pool.memset(decay[:, :, :, 0:1], 0.0).then_inc(s_zero, 1)
            pool.wait_ge(s_setup, 1)

            def reciprocal_root(k):
                pool.wait_ge(s_var, k)
                pool.tensor_tensor(rstd[:], var_eps[:], neg_half[:], ALU.pow).then_inc(s_rstd, 1)

            def attention(i, j, layer):
                ai = 2 * i + j
                reciprocal_root(6 * i + 4 * j + 1)
                src = x_in if layer == 0 else x_res
                ins = pool.tensor_tensor(x_bias[:], src[:],
                                         att_bias[layer][:, 2:3, :].broadcast_to([P, TT, D]), ALU.add)
                ins.then_inc(a_xb, 1)
                reciprocal_root(6 * i + 4 * j + 2)

            def state_space(i, j, layer):
                mi = 2 * i + j
                reciprocal_root(6 * i + 3 + j)
                pool.wait_ge(m_ln, mi + 1)
                pool.wait_ge(m_relu, mi * CH + CH)
                pool.tensor_tensor(dt[:], dt[:], dtu[:], ALU.add).then_inc(m_dt, 1)
                pool.wait_ge(m_dt, mi + 1)
                pool.wait_ge(m_u, mi * CH + CH)
                pool.tensor_tensor(dtu[:], dt[:], u[:], ALU.mult).then_inc(m_dtu, 1)
                pool.wait_ge(m_dtu, mi + 1)
                for n in range(N):
                    pool.wait_ge(m_brow, mi * N + n + 1)
                    if n == SLOTS - 1:
                        pool.wait_ge(m_sz, mi + 1)
                    if n >= SLOTS:
                        pool.wait_ge(m_sum, mi * N + n - SLOTS + 1)
                    pool.tensor_tensor(state[:, n % SLOTS], dtu[:],
                                       b_rows[:, n % 2:n % 2 + 1, :].broadcast_to([P, CH, T]),
                                       ALU.mult).then_inc(m_inject, 1)

            with pool.Fori(0, B) as i:
                pool.tensor_copy(mod[:], mod_all[:, bass.ds(i, 1), :].rearrange("p b m -> p (b m)")).then_inc(s_mod, 1)
                pool.wait_ge(s_mod, 2 * i + 1)
                pool.tensor_tensor(gate_row[:], gate_nat[:].rearrange("b l d -> b (l d)"),
                                   mod[0:B, MOD_PICK:MOD_PICK + 1].broadcast_to([B, 2 * D]), ALU.mult).then_inc(s_mod, 1)
                pool.wait_ge(s_x, 16 * i + 16)
                attention(i, 0, 0)
                state_space(i, 0, 1)
                state_space(i, 1, 2)
                attention(i, 1, 3)
                pool.wait_ge(s_out, 16 * i + 16)

        @block.scalar
        def _(act):
            act.dma_start(film_sb[3], film_w[3].rearrange("(k p) n -> p k n", p=P)).then_inc(s_cond_w, 16)
            act.dma_start(ada_sb[2], ada_w[2].rearrange("(k p) n -> p k n", p=P)).then_inc(s_cond_w, 16)
            act.dma_start(att_sb[3][:], att_packs[3]).then_inc(s_att_w, 16)
            for layer in ATT:
                for r in range(3):
                    act.dma_start(att_bias[layer][:, r], att_rows[layer][r].partition_broadcast(P)).then_inc(s_rows, 16)
            for n in range(2):
                act.dma_start(gate_bias[:, n], gate_rows[n].partition_broadcast(B)).then_inc(s_rows, 16)
            act.wait_ge(s_const, 64)
            act.activation(silu_c[:].rearrange("p k b -> p (k b)"), cw("cond"), ACT.Tanh, scale=0.5).then_inc(s_silu_t, 1)
            act.wait_ge(s_ssm_w, 32)
            for layer in SSM:
                act.activation(neg_a[layer][:], sw(layer, "a_log"), ACT.Exp).then_inc(s_neg_a, 1)
            act.wait_ge(s_setup, 1)

            def turned_norm(i, k, layer, scale, shift):
                for c in range(DC):
                    act.wait_ge(s_xT, (4 * i + k) * DC + c + 1)
                    act.activation(xnT[:, c, :], bank[c][:], ACT.Identity, scale=scale[:, c:c + 1],
                                   bias=shift[:, c:c + 1]).then_inc(s_xnT, 1)

            def attention(i, j, layer):
                ai = 2 * i + j
                turned_norm(i, 3 * j, layer, aw(layer, "norm_g"), aw(layer, "norm_b"))
                for c in range(DC):
                    act.wait_ge(a_kshift, ai + 1)
                    act.activation(kexp[:, c, :], bank[4 + c][:], ACT.Exp, bias=kshift[:, c:c + 1],
                                   accum_out=ksum[:, c:c + 1]).then_inc(a_kexp, 1)
                act.wait_ge(a_qsub, ai + 1)
                act.activation(q, q, ACT.Exp).then_inc(a_qexp, 1)
                act.wait_ge(a_vadd, ai + 1)
                for t in range(TT):
                    act.activation(v[:, t, :], v[:, t, :], ACT.Copy,
                                   scale=mod[:, MOD_KEEP[layer] + t:MOD_KEEP[layer] + t + 1]).then_inc(a_vs, 1)
                for h in range(2):
                    act.wait_ge(a_kT, ai * 2 + h + 1)
                    act.activation(knat[:, 2 * h:2 * h + 2, :].rearrange("p t d -> p (t d)"), bank[2 + h][:],
                                   ACT.Copy).then_inc(a_knat, 1)
                for c in range(DC):
                    act.wait_ge(a_qT, ai * DC + c + 1)
                    act.activation(qT[:, c, :], bank[c][:], ACT.Copy).then_inc(a_qTs, 1)
                for c in range(DC):
                    act.wait_ge(a_yT, ai * DC + c + 1)
                    args = dict(scale=mod[:, MOD_SCALE[layer] + c:MOD_SCALE[layer] + c + 1],
                                bias=mod[:, MOD_SHIFT[layer] + c:MOD_SHIFT[layer] + c + 1])
                    act.activation(kexp[:, c, :], bank[c][:], ACT.Identity, **args).then_inc(a_hid, 1)
                    act.activation(qT[:, c, :], bank[c][:], ACT.Tanh, **args).then_inc(a_tanh, 1)

            def state_space(i, j, layer):
                mi = 2 * i + j
                turned_norm(i, 1 + j, layer, mod[:, MOD_SCALE[layer]:], mod[:, MOD_SHIFT[layer]:])
                for c in range(CH):
                    act.wait_ge(m_in, mi * 2 * CH + c + 1)
                    act.activation(xpad[:, c, TAPS - 1:], bank[2 + c][:], ACT.Copy).then_inc(m_xpad, 1)
                for c in range(CH):
                    act.wait_ge(m_in, mi * 2 * CH + CH + c + 1)
                    z = bank[(6 + c) % 8]
                    act.activation(zh[:, c, :], z[:], ACT.Copy, scale=0.5).then_inc(m_z, 1)
                    act.activation(zt[:, c, :], z[:], ACT.Tanh, scale=0.5).then_inc(m_z, 1)
                for c in range(CH):
                    act.wait_ge(m_conv, mi * CH + c + 1)
                    act.activation(dt[:, c, :], u[:, c, :], ACT.Tanh).then_inc(m_ut, 1)
                act.wait_ge(m_x, mi * 2 + 1)
                act.activation(dtr, bank[2][0:DTR, :], ACT.Copy).then_inc(m_dtr, 1)
                for c in range(CH):
                    act.wait_ge(m_dtp, mi * CH + c + 1)
                    if c == 0:
                        act.wait_ge(m_u, mi * CH + CH)
                    act.activation(dt[:, c, :], bank[4 + c][:], ACT.Abs, bias=sw(layer, "dt_b")[:, c:c + 1]).then_inc(m_abs, 1)
                act.wait_ge(m_abs, mi * CH + CH)
                act.activation(dt[:], dt[:], ACT.Exp, scale=-1.0).then_inc(m_lnl, 1)
                act.wait_ge(m_lnl, mi + 1)
                act.activation(dt[:], dt[:], ACT.Ln, bias=1.0).then_inc(m_ln, 1)
                for n in range(N):
                    act.wait_ge(m_bps, mi * N + n + 1)
                    if n >= 2:
                        act.wait_ge(m_inject, mi * N + n - 1)
                    act.activation(b_rows[:, n % 2, :], bank[4 + n % 2][:], ACT.Copy).then_inc(m_brow, 1)
                    if n == 0:
                        act.wait_ge(m_dt, mi + 1)
                    if n >= 2:
                        act.wait_ge(m_scan, mi * N + n - 1)
                    for c in range(CH):
                        act.activation(decay[:, n % 2, c, 1:], dt[:, c, 1:], ACT.Exp,
                                       scale=neg_a[layer][:, c * N + n:c * N + n + 1]).then_inc(m_decay, 1)

            with act.Fori(0, B) as i:
                act.wait_ge(s_mod, 2 * i + 2)
                act.wait_ge(s_gate_pe, i + 1)
                act.activation(gate[:].rearrange("p l d -> p (l d)"), bank[7][:], ACT.Copy).then_inc(s_gate_ev, 1)
                attention(i, 0, 0)
                state_space(i, 0, 1)
                state_space(i, 1, 2)
                attention(i, 1, 3)

        @block.vector
        def _(dve):
            pro = [0]

            def setup_link(ins):
                pro[0] += 1
                ins.then_inc(s_pro, 1)
                dve.wait_ge(s_pro, pro[0])

            dve.wait_ge(s_const, 64)
            dve.wait_ge(s_silu_t, 1)
            flat_c = silu_c[:].rearrange("p k b -> p (k b)")
            setup_link(dve.scalar_tensor_tensor(flat_c, flat_c, 1.0, cw("cond"), ALU.add, ALU.mult))
            dve.tensor_scalar(flat_c, flat_c, 0.5, None, ALU.mult).then_inc(s_silu, 1)
            keep0 = mod_all[:, :, MOD_KEEP[0]:MOD_KEEP[0] + TT]
            setup_link(dve.tensor_scalar(keep0, mask_i[:].rearrange("p (b t) -> p b t", t=TT), 1.0, None, ALU.is_equal))
            setup_link(dve.tensor_scalar(keep0, keep0, -1.0, 1.0, ALU.mult, ALU.add))
            setup_link(dve.tensor_copy(mod_all[:, :, MOD_KEEP[3]:MOD_KEEP[3] + TT],
                                       cw("keep3").rearrange("p (b t) -> p b t", t=TT)))
            setup_link(dve.tensor_copy(mod_all[:, :, MOD_PICK], ident[:, 0:B]))
            ordf = xn[:].rearrange("p t d -> p (t d)")[:, 0:T]
            setup_link(dve.tensor_copy(ordf, order_i))
            for t in range(TT):
                dve.tensor_scalar(permute[:, t, :], ordf, cw("token")[:, t:t + 1], None, ALU.is_equal)
            dve.wait_ge(s_ssm_w, 32)
            for n, layer in enumerate(SSM):
                dve.tensor_scalar(half_w[layer][:], sw(layer, "conv_w"), 0.5, None, ALU.mult)
                dve.tensor_scalar(half_cb[layer][:], sw(layer, "conv_b"), 0.5, None, ALU.mult)
                dve.wait_ge(s_neg_a, n + 1)
                setup_link(dve.tensor_scalar(neg_a[layer][:], neg_a[layer][:], -1.0, None, ALU.mult))
            dve.wait_ge(s_rows, 16 * 8)
            dve.wait_ge(s_att_w, 32)

            for n, layer in enumerate((0, 1, 2, 3)):
                dve.wait_ge(s_cond_pe, n + 1)
                is_att = layer in ATT
                m = 2 * DC if is_att else 3 * DC
                bias = aw(layer, "emb_b") if is_att else sw(layer, "ada_b")
                g, b = ((aw(layer, "film_g"), aw(layer, "film_b")) if is_att
                        else (sw(layer, "norm_g"), sw(layer, "norm_b")))
                raw = mod_raw[:, 0:m, :]
                setup_link(dve.tensor_tensor(raw, bank[n][:, 0:m * B].rearrange("p (m b) -> p m b", b=B),
                                             bias.unsqueeze(2).broadcast_to([P, m, B]), ALU.add))
                at_scale, at_shift = (0, DC) if is_att else (DC, 0)
                for c in range(DC):
                    sc, sh = raw[:, at_scale + c, :], raw[:, at_shift + c, :]
                    to_s = mod_all[:, :, MOD_SCALE[layer] + c]
                    to_h = mod_all[:, :, MOD_SHIFT[layer] + c]
                    setup_link(dve.tensor_scalar(to_s, sc, 1.0, g[:, c:c + 1], ALU.add, ALU.mult))
                    setup_link(dve.tensor_scalar(to_h, sc, 1.0, b[:, c:c + 1], ALU.add, ALU.mult))
                    setup_link(dve.tensor_tensor(to_h, to_h, sh, ALU.add))
                if is_att:
                    both = mod_all[:, :, MOD_SCALE[layer]:MOD_SHIFT[layer] + DC]
                    setup_link(dve.tensor_scalar(both, both, 0.5, None, ALU.mult))
            for n in range(2):
                dve.wait_ge(s_cond_pe, 5 + n)
                dve.tensor_tensor(gate_nat[:, n, :], bank[4 + n][0:B, 0:D], gate_bias[:, n, :], ALU.add).then_inc(s_gate_nat, 1)
            dve.wait_ge(s_gate_nat, 2)
            dve.wait_ge(s_zero, 3)
            dve.memset(stats[:], 0.0).then_inc(s_setup, 1)
            dve.wait_ge(s_setup, 1)

            def moments(src, k, link):
                for t in range(TT):
                    ins = dve.bn_stats(stats[:, t, :], src(t))
                link(ins)
                dve.tensor_copy(var_eps[:], stats[:, :, 2])
                for t in range(TT):
                    ins = dve.bn_aggr(mv[:, t, :], stats[:, t, :])
                link(ins)
                dve.tensor_scalar(var_eps[:], mv[:, :, 1], EPS, None, ALU.add).then_inc(s_var, 1)
                dve.wait_ge(s_rstd, k)

            def normed(src, k):
                for t in range(TT):
                    dve.tensor_scalar(xn[:, t, :], src(t), mv[:, t, 0:1], rstd[:, t:t + 1], ALU.subtract,
                                      ALU.mult).then_inc(s_xn, 1)

            def attention(i, j, layer):
                ai = 2 * i + j
                heads = HEADS[j]
                width = D // heads
                links = [0]

                def link(ins):
                    links[0] += 1
                    ins.then_inc(a_links, 1)
                    dve.wait_ge(a_links, ai * ATT_DVE_LINKS + links[0])

                src = x_in if layer == 0 else x_res
                if layer == 0:
                    dve.wait_ge(s_mrow, 32 * i + 32)
                    link(dve.tensor_scalar(mask_row, mrow_i[:], 1.0, None, ALU.is_equal))
                    dve.tensor_scalar(mask_row, mask_row, MASKED, None, ALU.mult).then_inc(a_mask, 1)
                else:
                    link(dve.tensor_scalar(mask_row, mrow3[:], -1.0, 1.0, ALU.mult, ALU.add))
                    dve.tensor_scalar(mask_row, mask_row, -1000000.0, None, ALU.mult).then_inc(a_mask, 1)
                if layer == 0:
                    dve.wait_ge(s_x, 16 * i + 16)
                moments(lambda t: src[:, t, :], 6 * i + 4 * j + 1, link)
                normed(lambda t: src[:, t, :], 6 * i + 4 * j + 1)
                for c in range(DC):
                    dve.wait_ge(a_k, ai * DC + c + 1)
                    ins = dve.tensor_reduce(kmax[:, c:c + 1], bank[4 + c][:], AX, ALU.max)
                link(ins)
                link(dve.tensor_tensor(kmax[:], kmax[:], aw(layer, "bk"), ALU.add))
                dve.tensor_tensor(kshift[:], aw(layer, "bk"), kmax[:], ALU.subtract).then_inc(a_kshift, 1)
                for h in range(2):
                    dve.wait_ge(a_q, ai * 2 + h + 1)
                    dve.tensor_tensor(q[:, 2 * h:2 * h + 2, :], bank[2 + h][:].rearrange("p (t d) -> p t d", d=D),
                                      att_bias[layer][:, 0:1, :].broadcast_to([P, 2, D]), ALU.add).then_inc(a_qev, 1)
                dve.wait_ge(a_qev, ai * 2 + 2)
                qh = q.rearrange("p t (h w) -> p (t h) w", w=width)
                qs = qstat[:, 0:TT * heads]
                qsb = qs.unsqueeze(2).broadcast_to([P, TT * heads, width])
                link(dve.tensor_reduce(qs, qh, AX, ALU.max))
                dve.tensor_tensor(qh, qh, qsb, ALU.subtract).then_inc(a_qsub, 1)
                for h in range(2):
                    dve.wait_ge(a_v, ai * 2 + h + 1)
                    ins = dve.tensor_tensor(v[:, 2 * h:2 * h + 2, :], bank[6 + h][:].rearrange("p (t d) -> p t d", d=D),
                                            att_bias[layer][:, 1:2, :].broadcast_to([P, 2, D]), ALU.add)
                ins.then_inc(a_vadd, 1)
                dve.wait_ge(a_kexp, ai * DC + DC)
                link(dve.reciprocal(krec[:], ksum[:]))
                for c in range(DC):
                    dve.tensor_scalar(kexp[:, c, :], kexp[:, c, :], krec[:, c:c + 1], None, ALU.mult).then_inc(a_kn, 1)
                dve.wait_ge(a_qexp, ai + 1)
                link(dve.tensor_reduce(qs, qh, AX, ALU.add))
                link(dve.reciprocal(qs, qs))
                dve.tensor_tensor(qh, qh, qsb, ALU.mult).then_inc(a_qn, 1)
                for c in range(DC):
                    dve.wait_ge(a_att, ai * DC + c + 1)
                    dve.tensor_tensor(att[:, c, :], bank[4 + c][:, 0:P], aw(layer, "heads"), ALU.mult).then_inc(a_atts, 1)
                dve.wait_ge(a_y, ai * TT + TT)
                ysrc = lambda t: bank[6 + t // 2][:, (t % 2) * D:(t % 2 + 1) * D]
                moments(ysrc, 6 * i + 4 * j + 2, link)
                normed(ysrc, 6 * i + 4 * j + 2)
                for c in range(DC):
                    dve.wait_ge(a_hid, ai * DC + c + 1)
                    dve.wait_ge(a_tanh, ai * DC + c + 1)
                    dve.scalar_tensor_tensor(xnT[:, c, :], qT[:, c, :], 1.0, kexp[:, c, :], ALU.add,
                                             ALU.mult).then_inc(a_act, 1)
                dst = x_res if layer == 0 else x_out
                dve.wait_ge(a_xb, ai + 1)
                for h in range(2):
                    dve.wait_ge(a_o, ai * 2 + h + 1)
                    ins = dve.tensor_tensor(dst[:, 2 * h:2 * h + 2, :], bank[2 + h][:].rearrange("p (t d) -> p t d", d=D),
                                            x_bias[:, 2 * h:2 * h + 2, :], ALU.add)
                link(ins)
                if layer == 3:
                    dve.sem_inc(s_out_ready, 1)
                assert links[0] == ATT_DVE_LINKS, links

            def state_space(i, j, layer):
                mi = 2 * i + j
                links = [0]

                def link(ins):
                    links[0] += 1
                    ins.then_inc(m_links, 1)
                    dve.wait_ge(m_links, mi * SSM_DVE_LINKS + links[0])

                moments(lambda t: x_res[:, t, :], 6 * i + 3 + j, link)
                normed(lambda t: x_res[:, t, :], 6 * i + 3 + j)
                for k in range(TAPS):
                    for c in range(CH):
                        w = half_w[layer][:, c * TAPS + k:c * TAPS + k + 1]
                        if k == 0:
                            dve.wait_ge(m_xpad, mi * CH + c + 1)
                            ins = dve.tensor_scalar(u[:, c, :], xpad[:, c, 0:T], w, half_cb[layer][:, c:c + 1],
                                                    ALU.mult, ALU.add)
                        else:
                            ins = dve.scalar_tensor_tensor(u[:, c, :], xpad[:, c, k:k + T], w, u[:, c, :], ALU.mult,
                                                           ALU.add)
                            if k == TAPS - 1:
                                ins.then_inc(m_conv, 1)
                    if k < TAPS - 1:
                        link(ins)
                for c in range(CH):
                    dve.wait_ge(m_ut, mi * CH + c + 1)
                    dve.scalar_tensor_tensor(u[:, c, :], dt[:, c, :], 1.0, u[:, c, :], ALU.add, ALU.mult).then_inc(m_u, 1)
                dve.wait_ge(m_z, mi * 2 * CH + 2 * CH)
                dve.scalar_tensor_tensor(zh[:], zt, 1.0, zh[:], ALU.add, ALU.mult).then_inc(m_sz, 1)
                dve.wait_ge(m_x, mi * 2 + 2)
                rows = bank[3][0:3 * NB, :]
                link(dve.tensor_copy(bc_parts[:], rows))
                link(dve.tensor_tensor(bc_rest, rows, bc_parts[:], ALU.subtract))
                dve.tensor_copy(bc_parts[NB:2 * NB, :], bc_rest[NB:2 * NB, :])
                link(dve.tensor_copy(bc_parts[2 * NB:, :], bc_rest[2 * NB:, :]))
                link(dve.tensor_tensor(bc_rest[2 * NB:, :], bc_rest[2 * NB:, :], bc_parts[2 * NB:, :], ALU.subtract))
                dve.tensor_copy(bc_parts[2 * NB:, :], bc_rest[2 * NB:, :]).then_inc(m_parts, 1)
                for c in range(CH):
                    dve.wait_ge(m_abs, mi * CH + c + 1)
                    dve.tensor_scalar(dtu[:, c, :], bank[4 + c][:], sw(layer, "dt_b")[:, c:c + 1], 0.0, ALU.add,
                                      ALU.max).then_inc(m_relu, 1)

                def scan(n):
                    dve.wait_ge(m_decay, (mi * N + n) * CH + CH)
                    dve.wait_ge(m_inject, mi * N + n + 1)
                    s = state[:, n % SLOTS].rearrange("p c t -> p (c t)")
                    dve.tensor_tensor_scan(s, decay[:, n % 2].rearrange("p c t -> p (c t)"), s, 0.0, ALU.mult,
                                           ALU.add).then_inc(m_scan, 1)

                scan(0)
                for n in range(N):
                    if n + 1 < N:
                        scan(n + 1)
                    dve.wait_ge(m_scan, mi * N + n + 1)
                    dve.wait_ge(m_cps, mi * N + n + 1)
                    s = state[:, n % SLOTS]
                    dve.tensor_tensor(s, s, bank[6 + n % 2][:].unsqueeze(1).broadcast_to([P, CH, T]),
                                      ALU.mult).then_inc(m_prod, 1)
                dve.wait_ge(m_sum, mi * N + N)
                for c in range(CH):
                    ins = dve.scalar_tensor_tensor(u[:, c, :], u[:, c, :], sw(layer, "d_skip")[:, c:c + 1], bank[c][:],
                                                   ALU.mult, ALU.add)
                link(ins)
                for c in range(CH):
                    dve.tensor_tensor(u[:, c, :], u[:, c, :], zh[:, c, :], ALU.mult).then_inc(m_gated, 1)
                for h in range(2):
                    dve.wait_ge(m_o, mi * 2 + h + 1)
                    dve.tensor_tensor(xn[:, 2 * h:2 * h + 2, :], bank[4 + h][:].rearrange("p (t d) -> p t d", d=D),
                                      gate[:, j:j + 1, :].broadcast_to([P, 2, D]), ALU.mult).then_inc(m_og, 1)
                dve.wait_ge(m_og, mi * 2 + 2)
                if layer == 1:
                    ins = dve.tensor_tensor(x_res[:], x_res[:], xn[:], ALU.add)
                else:
                    for h in range(2):
                        dve.wait_ge(m_g, i * 2 + h + 1)
                        ins = dve.tensor_tensor(x_res[:, 2 * h:2 * h + 2, :],
                                                bank[6 + h][:].rearrange("p (t d) -> p t d", d=D),
                                                x_res[:, 2 * h:2 * h + 2, :], ALU.add)
                ins.then_inc(m_links, 1)
                links[0] += 1
                dve.wait_ge(m_links, mi * SSM_DVE_LINKS + links[0])
                assert links[0] == SSM_DVE_LINKS, links

            with dve.Fori(0, B) as i:
                dve.wait_ge(s_mod, 2 * i + 2)
                attention(i, 0, 0)
                state_space(i, 0, 1)
                state_space(i, 1, 2)
                attention(i, 1, 3)

        @block.tensor
        def _(pe):
            pe.wait_ge(s_const, 64)
            pe.wait_ge(s_silu, 1)
            pe.wait_ge(s_cond_w, 64)
            for n, layer in enumerate((0, 1, 2, 3)):
                w = film_sb[layer] if layer in ATT else ada_sb[layer]
                m = 2 * DC if layer in ATT else 3 * DC
                for c in range(m):
                    for k in range(EC):
                        ins = pe.matmul(bank[n][:, c * B:(c + 1) * B], w[:, k, c * P:(c + 1) * P], silu_c[:, k, :],
                                        start=(k == 0), stop=(k == EC - 1))
                ins.then_inc(s_cond_pe, 1)
            for n, layer in enumerate(SSM):
                for k in range(EC):
                    ins = pe.matmul(bank[4 + n][0:B, 0:D], silu_c[:, k, :], ada_sb[layer][:, k, 2 * D:3 * D],
                                    start=(k == 0), stop=(k == EC - 1))
                ins.then_inc(s_cond_pe, 1)
            pe.wait_ge(s_setup, 1)

            def turn(src, done):
                for c in range(DC):
                    for t in range(TT):
                        ins = pe.transpose(bank[c][:, t * P:(t + 1) * P], src[:, t, c * P:(c + 1) * P], ident)
                    ins.then_inc(done, 1)

            def attention(i, j, layer):
                ai = 2 * i + j
                pe.wait_ge(s_xn, 24 * i + 16 * j + TT)
                turn(xn, s_xT)
                w = {n: aw(layer, n).rearrange("p (c n) -> p c n", c=DC) for n in ("wq", "wk", "wv", "wo")}
                pe.wait_ge(s_xnT, (4 * i + 3 * j) * DC + DC)
                pe.wait_ge(a_mask, ai + 1)
                for e in range(DC):
                    for c in range(DC):
                        pe.matmul(bank[4 + e][:], w["wk"][:, c, e * P:(e + 1) * P], xnT[:, c, :], start=(c == 0), stop=False)
                    pe.matmul(bank[4 + e][:], ones_row, mask_row, start=False, stop=True).then_inc(a_k, 1)
                for t in range(TT):
                    for c in range(DC):
                        ins = pe.matmul(bank[2 + t // 2][:, (t % 2) * D:(t % 2 + 1) * D], xnT[:, c, t * P:(t + 1) * P],
                                        w["wq"][:, c, :], start=(c == 0), stop=(c == DC - 1))
                    if t % 2:
                        ins.then_inc(a_q, 1)
                for t in range(TT):
                    for c in range(DC):
                        ins = pe.matmul(bank[6 + t // 2][:, (t % 2) * D:(t % 2 + 1) * D], xnT[:, c, t * P:(t + 1) * P],
                                        w["wv"][:, c, :], start=(c == 0), stop=(c == DC - 1))
                    if t % 2:
                        ins.then_inc(a_v, 1)
                pe.wait_ge(a_kn, ai * DC + DC)
                pe.wait_ge(a_qev, ai * 2 + 2)
                for t in range(TT):
                    for c in range(DC):
                        ins = pe.transpose(bank[2 + t // 2][:, (t % 2) * D + c * P:(t % 2) * D + (c + 1) * P],
                                           kexp[:, c, t * P:(t + 1) * P], ident)
                    if t % 2:
                        ins.then_inc(a_kT, 1)
                pe.wait_ge(a_qn, ai + 1)
                turn(q, a_qT)
                pe.wait_ge(a_knat, ai * 2 + 2)
                pe.wait_ge(a_vs, ai * TT + TT)
                over, free = (v, knat) if layer == 0 else (knat, v)
                for c in range(DC):
                    for t in range(TT):
                        ins = pe.matmul(bank[4 + c][:, 0:P], over[:, t, c * P:(c + 1) * P], free[:, t, c * P:(c + 1) * P],
                                        start=(t == 0), stop=(t == TT - 1))
                    ins.then_inc(a_att, 1)
                pe.wait_ge(a_qTs, ai * DC + DC)
                pe.wait_ge(a_atts, ai * DC + DC)
                for t in range(TT):
                    for c in range(DC):
                        ins = pe.matmul(bank[6 + t // 2][:, (t % 2) * D + c * P:(t % 2) * D + (c + 1) * P],
                                        qT[:, c, t * P:(t + 1) * P], att[:, c, :], start=True, stop=True)
                    ins.then_inc(a_y, 1)
                pe.wait_ge(s_xn, 24 * i + 16 * j + 2 * TT)
                turn(xn, a_yT)
                pe.wait_ge(a_act, ai * DC + DC)
                for t in range(TT):
                    for c in range(DC):
                        ins = pe.matmul(bank[2 + t // 2][:, (t % 2) * D:(t % 2 + 1) * D], xnT[:, c, t * P:(t + 1) * P],
                                        w["wo"][:, c, :], start=(c == 0), stop=(c == DC - 1))
                    if t % 2:
                        ins.then_inc(a_o, 1)

            def state_space(i, j, layer):
                mi = 2 * i + j
                w_in = sw(layer, "w_in").rearrange("p (c n) -> p c n", c=DC)
                w_x = sw(layer, "w_x").rearrange("p (c n) -> p c n", c=CH)
                w_dt = sw(layer, "w_dt")[0:DTR, :]
                w_out = sw(layer, "w_out").rearrange("p (c n) -> p c n", c=CH)
                pe.wait_ge(s_xn, 24 * i + (3 + j) * TT)
                if layer == 1:
                    turn(xn, s_xT)
                else:
                    for c in range(DC):
                        for t in range(TT):
                            ins = pe.matmul(bank[c][:], xn[:, t, c * P:(c + 1) * P], permute[:, t, :],
                                            start=(t == 0), stop=(t == TT - 1))
                        ins.then_inc(s_xT, 1)
                pe.wait_ge(s_xnT, (4 * i + 1 + j) * DC + DC)
                for e in range(2 * CH):
                    for c in range(DC):
                        ins = pe.matmul(bank[(2 + e) % 8][:], w_in[:, c, e * P:(e + 1) * P], xnT[:, c, :],
                                        start=(c == 0), stop=(c == DC - 1))
                    ins.then_inc(m_in, 1)
                pe.wait_ge(m_u, mi * CH + CH)
                for c in range(CH):
                    ins = pe.matmul(bank[2][0:DTR, :], w_x[:, c, 0:DTR], u[:, c, :], start=(c == 0), stop=(c == CH - 1))
                ins.then_inc(m_x, 1)
                for c in range(CH):
                    ins = pe.matmul(bank[3][0:3 * NB, :], w_x[:, c, DTR:], u[:, c, :], start=(c == 0), stop=(c == CH - 1))
                ins.then_inc(m_x, 1)
                pe.wait_ge(m_z, mi * 2 * CH + 2 * CH)
                pe.wait_ge(m_dtr, mi + 1)
                for c in range(CH):
                    pe.matmul(bank[4 + c][:], w_dt[:, c * P:(c + 1) * P], dtr, start=True, stop=True).then_inc(m_dtp, 1)
                pe.wait_ge(m_parts, mi + 1)
                pe.wait_ge(m_abs, mi * CH + CH)
                pe.wait_ge(m_relu, mi * CH + CH)

                def spread(n):
                    if n >= 2:
                        pe.wait_ge(m_brow, mi * N + n - 1)
                    pe.matmul(bank[4 + n % 2][:], sel_sb[:, n * P:(n + 1) * P], bc_parts[:], start=True,
                              stop=True).then_inc(m_bps, 1)
                    if n >= 2:
                        pe.wait_ge(m_prod, mi * N + n - 1)
                    pe.matmul(bank[6 + n % 2][:], sel_sb[:, (N + n) * P:(N + n + 1) * P], bc_parts[:], start=True,
                              stop=True).then_inc(m_cps, 1)

                spread(0)
                spread(1)
                for n in range(N):
                    pe.wait_ge(m_prod, mi * N + n + 1)
                    if n + 2 < N:
                        spread(n + 2)
                    for c in range(CH):
                        ins = pe.matmul(bank[c][:], ident, state[:, n % SLOTS, c, :], start=(n == 0), stop=(n == N - 1))
                    ins.then_inc(m_sum, 1)
                pe.wait_ge(m_gated, mi * CH + CH)
                for t in range(TT):
                    for c in range(CH):
                        ins = pe.matmul(bank[4 + t // 2][:, (t % 2) * D:(t % 2 + 1) * D], u[:, c, t * P:(t + 1) * P],
                                        w_out[:, c, :], start=(c == 0), stop=(c == CH - 1))
                    if t % 2:
                        ins.then_inc(m_o, 1)
                if layer == 2:
                    pe.wait_ge(m_og, mi * 2 + 2)
                    for t in range(TT):
                        for s in range(TT):
                            ins = pe.matmul(bank[6 + t // 2][:, (t % 2) * D:(t % 2 + 1) * D],
                                            permute[:, s, t * P:(t + 1) * P], xn[:, s, :], start=(s == 0), stop=(s == TT - 1))
                        if t % 2:
                            ins.then_inc(m_g, 1)

            with pe.Fori(0, B) as i:
                pe.wait_ge(s_mod, 2 * i + 2)
                pe.matmul(bank[7][:], ones_row8, gate_row[:], start=True, stop=True).then_inc(s_gate_pe, 1)
                attention(i, 0, 0)
                state_space(i, 0, 1)
                state_space(i, 1, 2)
                attention(i, 1, 3)


def kernel(**inputs):
    import numpy as np
    import concourse.bacc as bacc
    from concourse import mybir as mb
    from concourse.bass_utils import run_bass_kernel_spmd as run

    a = {k: np.asarray(v) for k, v in inputs.items()}

    def chunks(w):
        c = w.shape[0] // P
        return w.reshape(c, P, -1).transpose(1, 0, 2).reshape(P, -1)

    def cols(vec):
        return vec.reshape(-1, P).T

    def rows_of(w):
        full = np.zeros((P, w.shape[1]), w.dtype)
        full[:w.shape[0]] = w
        return full

    def pack(parts, names):
        return np.ascontiguousarray(np.concatenate([parts[n] for n, _ in names], axis=1))

    arrays, args = {}, {}
    nc = bacc.Bacc("TRN2", target_bir_lowering=False, num_devices=1)

    def give(name, array):
        array = np.ascontiguousarray(array)
        arrays[name] = array
        return nc.dram_tensor(name, array.shape, mb.dt.from_np(array.dtype), kind="ExternalInput").ap()

    def heads(n):
        w = np.arange(P) // (D // n)
        return (w[:, None] == w[None, :]).astype(np.float32)

    att_packs, ssm_packs, film_w, ada_w, att_rows = {}, {}, {}, {}, {}
    for n, (layer, names) in enumerate((
            (0, ("norm_scale", "norm_bias", "film_emb_W", "film_emb_b", "film_norm_scale", "film_norm_bias",
                 "film_out_W", "film_out_b")),
            (3, ("ln_w", "ln_b", "W_emb", "b_emb", "ln2_w", "ln2_b", "W_out", "b_out")))):
        g = lambda s: a[f"L{layer}_cond_{s}"]
        ng, nb, ew, eb, fg, fb, ow, ob = (g(s) for s in names)
        parts = dict(wq=chunks(g("Wq")), wk=chunks(g("Wk")), wv=chunks(g("Wv")), wo=chunks(ow), bk=cols(g("bk")),
                     norm_g=cols(ng), norm_b=cols(nb), film_g=cols(fg), film_b=cols(fb), emb_b=cols(eb),
                     heads=heads(HEADS[n]))
        att_packs[layer] = give(f"att_pack_{layer}", pack(parts, ATT_PACK))
        film_w[layer] = give(f"film_w_{layer}", ew)
        att_rows[layer] = [give(f"att_row_{layer}_{k}", r) for k, r in enumerate((g("bq"), g("bv"), ob))]
    gate_rows = []
    for layer in SSM:
        g = lambda s: a[f"L{layer}_cond_{s}"]
        if layer == 1:
            w_in, w_x, w_dt, w_out, ada = (g(s).T for s in ("in_proj_w", "x_proj_w", "dt_proj_w", "out_proj_w", "ada_w"))
            conv, dt_b, ng, nb, ab = g("conv_w"), g("dt_proj_b"), g("ln_g"), g("ln_b"), g("ada_b")
        else:
            w_in, w_x, w_dt, w_out, ada = (g(s) for s in ("W_in", "W_xp", "W_dt", "W_out", "W_ada"))
            conv, dt_b, ng, nb, ab = g("conv_w")[:, 0, :], g("b_dt"), g("gamma"), g("beta"), g("b_ada")
        parts = dict(w_in=chunks(w_in), w_x=chunks(np.concatenate([w_x] + 2 * [w_x[:, DTR:]], axis=1)), w_dt=rows_of(w_dt), w_out=chunks(w_out), conv_w=chunks(conv),
                     conv_b=cols(g("conv_b")), dt_b=cols(dt_b), a_log=chunks(g("A_log")), d_skip=cols(g("D_param")),
                     norm_g=cols(ng), norm_b=cols(nb), ada_b=cols(ab))
        ssm_packs[layer] = give(f"ssm_pack_{layer}", pack(parts, SSM_PACK))
        ada_w[layer] = give(f"ada_w_{layer}", ada)
        gate_rows.append(give(f"gate_row_{layer}", ab[2 * D:]))
    mask = a["mask_BxSx1_fk1"].reshape(B, T)
    by_tile = lambda m: m.reshape(B, TT, P).transpose(2, 0, 1).reshape(P, B * TT)
    parts = dict(ident=np.eye(P, dtype=np.float32), token=np.arange(T, dtype=np.float32).reshape(TT, P).T,
                 cond=a["cond_2048"].T.reshape(EC, P, B).transpose(1, 0, 2).reshape(P, EC * B),
                 keep3=by_tile(mask), ones=np.ones((P, P), np.float32))
    const_pack = give("const_pack", pack(parts, CONST_PACK))
    sel = np.repeat(np.tile(np.eye(NB), (3, 1)), P, axis=1).astype(mb.dt.np(BF16))
    sel = give("sel", sel)
    order = give("order", a["itok_S_0_1023"])
    mask_cols = give("mask_cols", by_tile(a["mask_BxS_ik0"]))
    mask_rows0 = give("mask_rows0", a["mask_BxS_ik0"])
    mask_rows3 = give("mask_rows3", mask)
    x = give("x", a["x"])
    out = nc.dram_tensor("out", (B, T, D), mb.dt.float32, kind="ExternalOutput").ap()
    bass_cond_seq(nc, x, out, mask_cols, mask_rows0, mask_rows3, order, const_pack, sel, att_packs, ssm_packs,
                  film_w, ada_w, att_rows, gate_rows)
    r = run(nc, [arrays], core_ids=[0])
    return r.results[0]["out"]
```

```python
from contextlib import ExitStack

import concourse.bass as bass
from concourse import mybir

P = 128
B, T, D = 8, 512, 256
TT, DC = T // P, D // P
DI, CH, N = 512, 4, 16
DTR, TAPS = 64, 4
E = 512
EC = E // P
NB = 2 * N
EPS = 1e-5
MASKED = -1e30
HEADS = (16, 8)
ATT, SSM = (0, 3), (1, 2)
HALVES = 2
HC = CH // HALVES
UNITS = HALVES * N
STATES, DECAYS = 4, 2

ALU = mybir.AluOpType
ACT = mybir.ActivationFunctionType
AX = mybir.AxisListType.X
F32, BF16, I32 = mybir.dt.float32, mybir.dt.bfloat16, mybir.dt.int32

ATT_PACK = (("wq", DC * D), ("wk", DC * D), ("wv", DC * D), ("wo", DC * D), ("bk", DC),
            ("norm_g", DC), ("norm_b", DC), ("film_g", DC), ("film_b", DC), ("emb_b", 2 * DC), ("heads", P))
SSM_PACK = (("w_in", DC * 2 * DI), ("w_x", CH * (DTR + 3 * NB)), ("w_dt", DI), ("w_out", CH * D),
            ("conv_w", CH * TAPS), ("conv_b", CH), ("dt_b", CH), ("a_log", CH * N), ("d_skip", CH),
            ("norm_g", DC), ("norm_b", DC), ("ada_b", 3 * DC))
CONST_PACK = (("ident", P), ("token", TT), ("cond", EC * B), ("keep3", B * TT), ("ones", P))


def columns(pack):
    at, out = 0, {}
    for name, n in pack:
        out[name] = (at, at + n)
        at += n
    return out, at


MOD_AT = {0: 0, 3: 2 * DC + TT, 1: 4 * DC + 2 * TT, 2: 6 * DC + 2 * TT}
MOD_PICK = 8 * DC + 2 * TT
MODS = MOD_PICK + 1

ATT_STAGES = dict(norm=3, root=2, xn=2, turn=3, xnT=2, k=4, kmax=3, kexp=3, v=3, vkeep=4, qT=3, qTs=3, att=2, y=3,
                  ynorm=3, yroot=2, yn=2, yturn=3, hidden=3, act=2, out=4, res=2)
PREP_STAGES = dict(norm=3, root=2, xn=2, turn=4, xnT=2, in01=3, in23=3, z01=4, z23=4, u01=2, u23=4, x=6, parts=6,
                   dt01=2, dt23=3, soft=5, dt=5, dtu=5)
POST_STAGES = dict(skip=3, out=6, gate=3, gather=6, res=2)
ATT_TICKS, PREP_TICKS, POST_TICKS = (sum(d.values()) for d in (ATT_STAGES, PREP_STAGES, POST_STAGES))

ATT_LINKS, PREP_LINKS, POST_LINKS = 11, 13, 1

PAIRS = B // 2


def beside(units, work, ticks):
    done = 0
    for k, _ in enumerate(units):
        while done < ticks * (k + 1) // UNITS:
            next(work, None)
            done += 1
    for _ in work:
        pass


def one_after_another(*parts):
    for part in parts:
        yield from part


def run_batches(eng, att, prep, post, scan):
    def mid(p, s, more):
        parts = [post(4 * p + s, 1, s, 2 * p + s), prep(2 + 4 * p + s, 2, s, 2 * p + s)]
        ticks = POST_TICKS + PREP_TICKS
        if more:
            parts.append(att(2 + 4 * p + s, 0, s, 2 * p + 2 + s))
            ticks += ATT_TICKS
        return one_after_another(*parts), ticks

    def end(p, s, more):
        parts = [post(4 * p + 2 + s, 2, s, 2 * p + s), att(2 + 4 * p + (2 if more else 0) + s, 3, s, 2 * p + s)]
        ticks = POST_TICKS + ATT_TICKS
        if more:
            parts.append(prep(4 + 4 * p + s, 1, s, 2 * p + 2 + s))
            ticks += PREP_TICKS
        return one_after_another(*parts), ticks

    for _ in one_after_another(att(0, 0, 0, 0), prep(0, 1, 0, 0)):
        pass
    beside(scan(0, 1, 0), one_after_another(att(1, 0, 1, 1), prep(1, 1, 1, 1)), ATT_TICKS + PREP_TICKS)
    with eng.Fori(0, PAIRS - 1) as p:
        beside(scan(1 + 4 * p, 1, 1), *mid(p, 0, True))
        beside(scan(2 + 4 * p, 2, 0), *mid(p, 1, True))
        beside(scan(3 + 4 * p, 2, 1), *end(p, 0, True))
        beside(scan(4 + 4 * p, 1, 0), *end(p, 1, True))
    p = PAIRS - 1
    beside(scan(1 + 4 * p, 1, 1), *mid(p, 0, False))
    beside(scan(2 + 4 * p, 2, 0), *mid(p, 1, False))
    beside(scan(3 + 4 * p, 2, 1), *end(p, 0, False))
    for _ in end(p, 1, False)[0]:
        pass


def rest(ticks):
    for _ in range(ticks):
        yield


def bass_cond_seq(nc, x, out, mask_cols, mask_rows0, mask_rows3, order, const_pack, sel, att_packs, ssm_packs,
                  film_w, ada_w, att_rows, gate_rows):
    ctx = ExitStack()
    with ctx:
        def sb(name, shape, dt=F32):
            return ctx.enter_context(nc.sbuf_tensor(name, shape, dt))

        def sem(name):
            return ctx.enter_context(nc.semaphore(name))

        bank = [ctx.enter_context(nc.psum_tensor(f"bank{k}", [P, 512], F32)) for k in range(8)]
        y_banks, b_bank, c_bank = bank[0:HC], bank[2], bank[3]
        pa, pb = bank[4:6], bank[6:8]

        catt, n_att = columns(ATT_PACK)
        cssm, n_ssm = columns(SSM_PACK)
        cconst, n_const = columns(CONST_PACK)
        att_sb = {layer: sb(f"att_pack{layer}", [P, n_att]) for layer in ATT}
        ssm_sb = {layer: sb(f"ssm_pack{layer}", [P, n_ssm]) for layer in SSM}
        const_sb = sb("const_sb", [P, n_const])
        sel_sb = sb("sel_sb", [3 * NB, NB], BF16)

        def aw(layer, name):
            return att_sb[layer][:, catt[name][0]:catt[name][1]]

        def sw(layer, name):
            return ssm_sb[layer][:, cssm[name][0]:cssm[name][1]]

        def cw(name):
            return const_sb[:, cconst[name][0]:cconst[name][1]]

        ident = cw("ident")
        ones_row, ones_row8 = {0: cw("ones")[0:1, :], 3: cw("ones")[32:33, :]}, cw("ones")[0:B, :]
        out_bias = sb("out_bias", [P, 2, D])
        rows = sb("rows", [P, T])
        qv_bias = {0: rows[0:1, :], 3: rows[32:33, :]}
        mrow_i, mrow3 = rows[64:65, :].bitcast(I32), rows[96:97, :]
        permute = sb("permute", [P, TT, T])
        neg_half = sb("neg_half", [P, TT])
        mod_all = sb("mod_all", [P, B, MODS])
        mod_att = sb("mod_att", [P, 2 * DC + TT])
        mod_prep = sb("mod_prep", [P, 2 * DC])
        gate_nat = sb("gate_nat", [B, 2, D])
        gate_row = sb("gate_row", [B, D])
        gate_pick = sb("gate_pick", [P, 1])
        gate = sb("gate", [P, D])
        half_w = {layer: sb(f"half_w{layer}", [P, CH * TAPS]) for layer in SSM}
        half_cb = {layer: sb(f"half_cb{layer}", [P, CH]) for layer in SSM}
        neg_a = {layer: sb(f"neg_a{layer}", [P, CH * N]) for layer in SSM}

        kept = sb("kept", [P, 8, CH, T])
        u, zh, dt, dtu = ([kept[:, 4 * s + k] for s in range(2)] for k in range(4))
        x_next = [sb(f"x_next{s}", [P, TT, D]) for s in range(2)]
        x_res = [sb(f"x_res{s}", [P, TT, D]) for s in range(2)]
        bc_parts = [sb(f"bc_parts{s}", [3 * NB, T], BF16) for s in range(2)]

        decay = sb("decay", [P, DECAYS, HC, T])
        state = sb("state", [P, STATES, HC, T])
        b_rows = sb("b_rows", [P, 2, T])

        x_in = sb("x_in", [P, TT, D])
        stats = sb("stats", [P, TT, 6])
        mv = sb("mv", [P, TT, 2])
        var_eps = sb("var_eps", [P, TT])
        rstd = sb("rstd", [P, TT])
        xn = sb("xn", [P, TT, D])
        xnT = sb("xnT", [P, DC, T])
        kmax, kshift, ksum, krec = (sb(n, [P, DC]) for n in ("kmax", "kshift", "ksum", "krec"))
        qstat = sb("qstat", [P, TT * 16])
        kexp = sb("kexp", [P, DC, T])
        mask_row = kexp[0:1, 0, :]
        knat = xn
        qT = xnT
        att = sb("att", [P, DC, P])
        conv_in = sb("conv_in", [P, CH * (T + TAPS - 1)])
        xpad = conv_in[:].rearrange("p (c t) -> p c t", c=CH)
        q, v = (conv_in[:, k * TT * D:(k + 1) * TT * D].rearrange("p (t d) -> p t d", d=D) for k in range(2))
        zt = conv_in[:, 0:CH * T].rearrange("p (c t) -> p c t", c=CH)
        dtr, bc_rest = kexp[0:DTR, 0, :], kexp[0:3 * NB, 1, :]

        order_i = kexp[:, 0, :].bitcast(I32)
        mask_i = kexp[:, 1, 0:B * TT].bitcast(I32)
        gate_bias = state[0:B, 0, 0, :].rearrange("p (l d) -> p l d", d=D)
        silu_c = xnT[:, 0, 0:EC * B].rearrange("p (k b) -> p k b", k=EC)
        mod_raw = xnT[:, 1, 0:3 * DC * B].rearrange("p (m b) -> p m b", b=B)
        flat = kept[:].rearrange("p s c t -> p (s c t)")
        film_sb = {0: flat[:, 0:EC * 2 * D], 3: flat[:, EC * 2 * D:EC * 4 * D]}
        ada_sb = {1: flat[:, EC * 4 * D:EC * 7 * D], 2: flat[:, EC * 7 * D:EC * 10 * D]}
        film_sb, ada_sb = ({n: w.rearrange("p (k n) -> p k n", k=EC) for n, w in d.items()} for d in (film_sb, ada_sb))

        s_const, s_att_w, s_ssm_w, s_cond_w, s_rows = (sem(n) for n in (
            "const_loaded", "att_weights_loaded", "ssm_weights_loaded", "cond_weights_loaded", "rows_loaded"))
        s_silu_t, s_silu, s_cond_pe, s_gate_nat, s_links, s_neg_a, s_setup, s_zero = (sem(n) for n in (
            "cond_tanh", "cond_silu", "mod_product", "gate_rows_ready", "setup_links", "neg_a_exp", "setup_done",
            "zeroed"))
        s_x, s_mrow3, s_xfree, s_m3free, s_out_ready, s_out = (sem(n) for n in (
            "x_loaded", "mask3_loaded", "x_in_free", "mask3_free", "x_out_ready", "x_out_stored"))
        a_links, a_mod, a_var, a_rstd, a_xn, a_xT, a_xnT, a_xb, a_mask, a_k, a_q, a_v, a_kshift, a_kexp, a_kn, a_kT, \
            a_knat, a_qsub, a_qexp, a_qn, a_qT, a_qTs, a_vs, a_att, a_atts, a_y, a_yT, a_hid, a_act, a_o, a_done = (
                sem("a_" + n) for n in (
                    "links", "mod_ready", "variance", "rstd", "xn_ready", "xn_turned", "xnT_ready", "x_biased",
                    "mask_row", "k_product", "q_product", "v_product", "kshift", "k_exp", "k_normed", "k_turned",
                    "k_natural", "q_shifted", "q_exp", "q_normed", "q_turned", "qT_ready", "v_ready", "att_product",
                    "att_ready", "y_product", "y_turned", "hidden_tanh", "hidden_ready", "out_product", "done"))
        p_links, p_mod, p_pad, p_var, p_rstd, p_xn, p_xT, p_xnT, p_in, p_xpad, p_z, p_conv, p_ut, p_u, p_x, p_dtr, p_sz, \
            p_parts, p_dtp, p_abs, p_exp, p_ln, p_dt, p_dtu = (sem("p_" + n) for n in (
                "links", "mod_ready", "pad_zeroed", "variance", "rstd", "xn_ready", "xn_turned", "xnT_ready",
                "in_product", "conv_input", "z_ready", "conv", "u_tanh", "u_ready", "x_product", "dtr_ready", "silu_z",
                "bc_parts", "dt_product", "dt_abs", "dt_exp", "dt_log", "dt_ready", "dtu_ready"))
        m_bps, m_brow, m_cps, m_decay, m_inject, m_scan, m_prod, m_sum, m_skip, m_half0 = (sem("m_" + n) for n in (
            "b_spread", "b_rows", "c_spread", "decay_ready", "inject_ready", "scanned", "weighted", "summed",
            "skip_added", "first_half_gated"))
        o_links, o_pick, o_row, o_gated, o_gps, o_gate, o_o, o_og, o_g = (sem("o_" + n) for n in (
            "links", "gate_picked", "gate_row", "second_half_gated", "gate_spread", "gate_ready", "out_product",
            "out_gated", "gathered"))

        def wait_back(eng, sem_, si, k, lag, each=1):
            if not (isinstance(si, int) and si * UNITS + k < lag):
                eng.wait_ge(sem_, (si * UNITS + k + 1 - lag) * each)

        block = ctx.enter_context(nc.Block())

        @block.sync
        def _(sp):
            def load(b):
                sp.dma_start(x_in[:], x[b].rearrange("(t p) d -> p t d", p=P)).then_inc(s_x, 16)
                sp.dma_start(mrow_i, mask_rows0[bass.ds(b, 1), :]).then_inc(s_x, 16)

            def load_mask3(b):
                sp.dma_start(mrow3, mask_rows3[bass.ds(b, 1), :]).then_inc(s_mrow3, 16)

            def store(b, s):
                sp.wait_ge(s_out_ready, b + 1)
                sp.dma_start(out[b].rearrange("(t p) d -> p t d", p=P), x_res[s][:]).then_inc(s_out, 16)

            sp.dma_start(const_sb[:], const_pack).then_inc(s_const, 16)
            sp.dma_start(mask_i, mask_cols).then_inc(s_const, 16)
            sp.dma_start(order_i, order.partition_broadcast(P)).then_inc(s_const, 16)
            sp.dma_start(sel_sb[:], sel).then_inc(s_const, 16)
            sp.dma_start(film_sb[0], film_w[0].rearrange("(k p) n -> p k n", p=P)).then_inc(s_cond_w, 16)
            sp.dma_start(ada_sb[1], ada_w[1].rearrange("(k p) n -> p k n", p=P)).then_inc(s_cond_w, 16)
            load(0)
            load_mask3(0)
            sp.dma_start(att_sb[0][:], att_packs[0]).then_inc(s_att_w, 16)
            sp.dma_start(ssm_sb[1][:], ssm_packs[1]).then_inc(s_ssm_w, 16)
            sp.wait_ge(s_xfree, 1)
            load(1)
            with sp.Fori(0, PAIRS - 1) as p:
                for s in range(2):
                    sp.wait_ge(s_xfree, 2 * p + 2 + s)
                    load(2 * p + 2 + s)
                for s in range(2):
                    sp.wait_ge(s_m3free, 2 * p + 1 + s)
                    load_mask3(2 * p + 1 + s)
                    store(2 * p + s, s)
            sp.wait_ge(s_m3free, B - 1)
            load_mask3(B - 1)
            store(B - 2, 0)
            store(B - 1, 1)
            sp.wait_ge(s_out, 16 * B)

        @block.gpsimd
        def _(pool):
            pool.memset(neg_half[:], -0.5).then_inc(s_zero, 1)
            pool.memset(decay[:, :, :, 0:1], 0.0).then_inc(s_zero, 1)
            pool.wait_ge(s_zero, 2)
            pool.wait_ge(s_setup, 1)

            def root(var, done, k):
                pool.wait_ge(var, k)
                pool.tensor_tensor(rstd[:], var_eps[:], neg_half[:], ALU.pow).then_inc(done, 1)

            def mod_cols(b, at, n):
                return mod_all[:, bass.ds(b, 1), at:at + n].rearrange("p b m -> p (b m)")

            def attention(ai, layer, s, b):
                src = x_in if layer == 0 else x_res[s]
                if not (isinstance(ai, int) and ai == 0):
                    pool.wait_ge(a_done, ai)
                pool.tensor_copy(mod_att[:], mod_cols(b, MOD_AT[layer], 2 * DC + TT)).then_inc(a_mod, 1)
                yield from rest(ATT_STAGES["norm"])
                root(a_var, a_rstd, 2 * ai + 1)
                yield from rest(ATT_STAGES["root"] + ATT_STAGES["xn"])
                pool.wait_ge(a_xn, 2 * ai * TT + TT)
                layer_at = ATT.index(layer)
                pool.tensor_tensor(src[:], src[:], out_bias[:, layer_at:layer_at + 1, :].broadcast_to([P, TT, D]),
                                   ALU.add).then_inc(a_xb, 1)
                for stage in ("turn", "xnT", "k", "kmax", "kexp", "v", "vkeep", "qT", "qTs", "att", "y", "ynorm"):
                    yield from rest(ATT_STAGES[stage])
                root(a_var, a_rstd, 2 * ai + 2)
                for stage in ("yroot", "yn", "yturn", "hidden", "act", "out", "res"):
                    yield from rest(ATT_STAGES[stage])

            def before(pi, layer, s, b):
                yield from rest(PREP_STAGES["norm"])
                pool.wait_ge(p_var, pi + 1)
                pool.tensor_copy(mod_prep[:], mod_cols(b, MOD_AT[layer], 2 * DC)).then_inc(p_mod, 1)
                pool.memset(xpad[:, :, 0:TAPS - 1], 0.0).then_inc(p_pad, 1)
                root(p_var, p_rstd, pi + 1)
                for stage in ("root", "xn", "turn", "xnT", "in01", "in23", "z01", "z23", "u01", "u23", "x", "parts",
                              "dt01", "dt23", "soft"):
                    yield from rest(PREP_STAGES[stage])
                pool.wait_ge(p_ln, pi + 1)
                for h in range(HALVES):
                    c = slice(h * HC, (h + 1) * HC)
                    pool.tensor_tensor(dt[s][:, c], dt[s][:, c], dtu[s][:, c], ALU.add).then_inc(p_dt, 1)
                    yield from rest(PREP_STAGES["dt" if h == 0 else "dtu"] // 2)
                    pool.wait_ge(p_dt, pi * HALVES + h + 1)
                    pool.wait_ge(p_u, pi * CH + CH)
                    pool.tensor_tensor(dtu[s][:, c], dt[s][:, c], u[s][:, c], ALU.mult).then_inc(p_dtu, 1)
                    yield from rest((PREP_STAGES["dt" if h == 0 else "dtu"] + 1) // 2)

            def after(qi, layer, s, b):
                pool.tensor_copy(gate_pick[:], mod_cols(b, MOD_PICK, 1)).then_inc(o_pick, 1)
                pool.wait_ge(o_pick, qi + 1)
                pool.tensor_tensor(gate_row[:], gate_nat[:, layer - 1, :], gate_pick[0:B, :].broadcast_to([B, D]),
                                   ALU.mult).then_inc(o_row, 1)
                yield from rest(POST_TICKS)

            def scan(si, layer, s):
                def inject(k):
                    c = slice(k // N * HC, k // N * HC + HC)
                    pool.wait_ge(m_brow, si * UNITS + k + 1)
                    wait_back(pool, m_sum, si, k, STATES)
                    pool.tensor_tensor(state[:, k % STATES], dtu[s][:, c],
                                       b_rows[:, k % 2:k % 2 + 1, :].broadcast_to([P, HC, T]), ALU.mult).then_inc(m_inject, 1)

                pool.wait_ge(p_dtu, (si + 1) * HALVES)
                inject(0)
                inject(1)
                for k in range(UNITS):
                    if k + 2 < UNITS:
                        inject(k + 2)
                    if k == N + 3:
                        pool.wait_ge(m_skip, si * HALVES + 1)
                        pool.tensor_tensor(u[s][:, 0:HC], u[s][:, 0:HC], zh[s][:, 0:HC], ALU.mult).then_inc(m_half0, 1)
                    yield

            run_batches(pool, attention, before, after, scan)

        @block.scalar
        def _(act):
            act.dma_start(film_sb[3], film_w[3].rearrange("(k p) n -> p k n", p=P)).then_inc(s_cond_w, 16)
            act.dma_start(ada_sb[2], ada_w[2].rearrange("(k p) n -> p k n", p=P)).then_inc(s_cond_w, 16)
            for n, layer in enumerate(ATT):
                for r in range(2):
                    act.dma_start(qv_bias[layer][:, r * D:(r + 1) * D], att_rows[layer][r].unsqueeze(0)).then_inc(s_rows, 16)
                act.dma_start(out_bias[:, n], att_rows[layer][2].partition_broadcast(P)).then_inc(s_rows, 16)
            for n in range(2):
                act.dma_start(gate_bias[:, n], gate_rows[n].partition_broadcast(B)).then_inc(s_rows, 16)
            act.dma_start(att_sb[3][:], att_packs[3]).then_inc(s_att_w, 16)
            act.dma_start(ssm_sb[2][:], ssm_packs[2]).then_inc(s_ssm_w, 16)
            act.wait_ge(s_const, 64)
            act.activation(silu_c.rearrange("p k b -> p (k b)"), cw("cond"), ACT.Tanh, scale=0.5).then_inc(s_silu_t, 1)
            act.wait_ge(s_ssm_w, 32)
            for layer in SSM:
                act.activation(neg_a[layer][:], sw(layer, "a_log"), ACT.Exp).then_inc(s_neg_a, 1)
            act.wait_ge(s_setup, 1)

            def attention(ai, layer, s, b):
                for stage in ("norm", "root", "xn", "turn"):
                    yield from rest(ATT_STAGES[stage])
                for c in range(DC):
                    act.wait_ge(a_xT, ai * DC + c + 1)
                    act.activation(xnT[:, c, :], pa[c][:], ACT.Identity, scale=aw(layer, "norm_g")[:, c:c + 1],
                                   bias=aw(layer, "norm_b")[:, c:c + 1]).then_inc(a_xnT, 1)
                for stage in ("xnT", "k", "kmax"):
                    yield from rest(ATT_STAGES[stage])
                act.wait_ge(a_kshift, ai + 1)
                for c in range(DC):
                    act.activation(kexp[:, c, :], pb[c][:], ACT.Exp, bias=kshift[:, c:c + 1],
                                   accum_out=ksum[:, c:c + 1]).then_inc(a_kexp, 1)
                yield from rest(ATT_STAGES["kexp"])
                act.wait_ge(a_qsub, ai * 2 + 2)
                act.activation(q, q, ACT.Exp).then_inc(a_qexp, 1)
                yield from rest(ATT_STAGES["v"])
                act.wait_ge(a_mod, ai + 1)
                for t in range(TT):
                    if t % 2 == 0:
                        act.wait_ge(a_v, ai * 2 + t // 2 + 1)
                    act.activation(v[:, t, :], pb[t // 2][:, (t % 2) * D:(t % 2 + 1) * D], ACT.Copy,
                                   scale=mod_att[:, 2 * DC + t:2 * DC + t + 1]).then_inc(a_vs, 1)
                yield from rest(ATT_STAGES["vkeep"])
                for h in range(2):
                    act.wait_ge(a_kT, ai * 2 + h + 1)
                    act.activation(knat[:, 2 * h:2 * h + 2, :].rearrange("p t d -> p (t d)"), pa[h][:],
                                   ACT.Copy).then_inc(a_knat, 1)
                yield from rest(ATT_STAGES["qT"])
                for c in range(DC):
                    act.wait_ge(a_qT, ai * DC + c + 1)
                    act.activation(qT[:, c, :], pb[c][:], ACT.Copy).then_inc(a_qTs, 1)
                for stage in ("qTs", "att", "y", "ynorm", "yroot", "yn", "yturn"):
                    yield from rest(ATT_STAGES[stage])
                for c in range(DC):
                    act.wait_ge(a_yT, ai * DC + c + 1)
                    args = dict(scale=mod_att[:, c:c + 1], bias=mod_att[:, DC + c:DC + c + 1])
                    act.activation(kexp[:, c, :], pa[c][:], ACT.Identity, **args)
                    act.activation(qT[:, c, :], pa[c][:], ACT.Tanh, **args).then_inc(a_hid, 1)
                for stage in ("hidden", "act", "out", "res"):
                    yield from rest(ATT_STAGES[stage])

            def before(pi, layer, s, b):
                for stage in ("norm", "root", "xn", "turn"):
                    yield from rest(PREP_STAGES[stage])
                act.wait_ge(p_mod, pi + 1)
                for c in range(DC):
                    act.wait_ge(p_xT, pi * DC + c + 1)
                    act.activation(xnT[:, c, :], pa[c][:], ACT.Identity, scale=mod_prep[:, c:c + 1],
                                   bias=mod_prep[:, DC + c:DC + c + 1]).then_inc(p_xnT, 1)
                yield from rest(PREP_STAGES["xnT"])
                for stage, banks, first in (("in01", pb, 0), ("in23", pa, 2)):
                    yield from rest(PREP_STAGES[stage])
                    for c in range(2):
                        act.wait_ge(p_in, pi * 2 * CH + first + c + 1)
                        act.activation(xpad[:, first + c, TAPS - 1:], banks[c][:], ACT.Copy).then_inc(p_xpad, 1)
                yield from rest(PREP_STAGES["z01"])
                for c in range(2):
                    act.wait_ge(p_conv, pi * CH + c + 1)
                    act.activation(dt[s][:, c, :], u[s][:, c, :], ACT.Tanh).then_inc(p_ut, 1)
                yield from rest(PREP_STAGES["z23"])
                for c in range(2, CH):
                    act.wait_ge(p_conv, pi * CH + c + 1)
                    act.activation(dt[s][:, c, :], u[s][:, c, :], ACT.Tanh).then_inc(p_ut, 1)
                for c in range(CH):
                    z = (pb if c < 2 else pa)[c % 2]
                    act.wait_ge(p_in, pi * 2 * CH + CH + c + 1)
                    act.activation(zh[s][:, c, :], z[:], ACT.Copy, scale=0.5)
                    act.activation(zt[:, c, :], z[:], ACT.Tanh, scale=0.5).then_inc(p_z, 1)
                    if c == 1:
                        yield from rest(PREP_STAGES["u01"])
                yield from rest(PREP_STAGES["u23"])
                yield from rest(PREP_STAGES["x"])
                act.wait_ge(p_x, pi * 2 + 1)
                act.activation(dtr, pb[0][0:DTR, :], ACT.Copy).then_inc(p_dtr, 1)
                yield from rest(PREP_STAGES["parts"])
                for stage, banks, first in (("dt01", pa, 0), ("dt23", pb, 2)):
                    yield from rest(PREP_STAGES[stage])
                    for c in range(first, first + 2):
                        bias = sw(layer, "dt_b")[:, c:c + 1]
                        act.wait_ge(p_dtp, pi * CH + c + 1)
                        act.activation(dt[s][:, c, :], banks[c % 2][:], ACT.Abs, bias=bias)
                        act.activation(dtu[s][:, c, :], banks[c % 2][:], ACT.Relu, bias=bias).then_inc(p_abs, 1)
                act.wait_ge(p_abs, pi * CH + CH)
                act.activation(dt[s], dt[s], ACT.Exp, scale=-1.0).then_inc(p_exp, 1)
                act.wait_ge(p_exp, pi + 1)
                act.activation(dt[s], dt[s], ACT.Ln, bias=1.0).then_inc(p_ln, 1)
                for stage in ("soft", "dt", "dtu"):
                    yield from rest(PREP_STAGES[stage])

            def after(qi, layer, s, b):
                yield from rest(POST_STAGES["skip"])
                act.wait_ge(o_gps, qi + 1)
                act.activation(gate[:], pb[0][:, 0:D], ACT.Copy).then_inc(o_gate, 1)
                yield from rest(POST_TICKS - POST_STAGES["skip"])

            def scan(si, layer, s):
                def rows_and_decays(k):
                    act.wait_ge(m_bps, si * UNITS + k + 1)
                    wait_back(act, m_inject, si, k, 2)
                    act.activation(b_rows[:, k % 2, :], b_bank[:], ACT.Copy).then_inc(m_brow, 1)
                    if k % N == 0:
                        act.wait_ge(p_dt, si * HALVES + k // N + 1)
                    wait_back(act, m_scan, si, k, DECAYS)
                    for c in range(HC):
                        at = (k // N * HC + c) * N + k % N
                        act.activation(decay[:, k % DECAYS, c, 1:], dt[s][:, k // N * HC + c, 1:], ACT.Exp,
                                       scale=neg_a[layer][:, at:at + 1]).then_inc(m_decay, 1)

                rows_and_decays(0)
                rows_and_decays(1)
                for k in range(UNITS):
                    if k + 2 < UNITS:
                        rows_and_decays(k + 2)
                    yield

            run_batches(act, attention, before, after, scan)

        @block.vector
        def _(dve):
            pro = [0]

            def setup_link(ins):
                pro[0] += 1
                ins.then_inc(s_links, 1)
                dve.wait_ge(s_links, pro[0])

            dve.wait_ge(s_const, 64)
            dve.wait_ge(s_silu_t, 1)
            flat_c = silu_c.rearrange("p k b -> p (k b)")
            setup_link(dve.scalar_tensor_tensor(flat_c, flat_c, 1.0, cw("cond"), ALU.add, ALU.mult))
            dve.tensor_scalar(flat_c, flat_c, 0.5, None, ALU.mult).then_inc(s_silu, 1)
            keep0, keep3 = (mod_all[:, :, MOD_AT[n] + 2 * DC:MOD_AT[n] + 2 * DC + TT] for n in ATT)
            setup_link(dve.tensor_scalar(keep0, mask_i.rearrange("p (b t) -> p b t", t=TT), 1.0, None, ALU.is_equal))
            setup_link(dve.tensor_scalar(keep0, keep0, -1.0, 1.0, ALU.mult, ALU.add))
            setup_link(dve.tensor_copy(keep3, cw("keep3").rearrange("p (b t) -> p b t", t=TT)))
            setup_link(dve.tensor_copy(mod_all[:, :, MOD_PICK], ident[:, 0:B]))
            ordf = xn[:].rearrange("p t d -> p (t d)")[:, 0:T]
            setup_link(dve.tensor_copy(ordf, order_i))
            for t in range(TT):
                dve.tensor_scalar(permute[:, t, :], ordf, cw("token")[:, t:t + 1], None, ALU.is_equal)
            dve.wait_ge(s_rows, 16 * 8)
            dve.wait_ge(s_att_w, 32)
            dve.wait_ge(s_ssm_w, 32)
            for n, layer in enumerate(SSM):
                dve.tensor_scalar(half_w[layer][:], sw(layer, "conv_w"), 0.5, None, ALU.mult)
                dve.tensor_scalar(half_cb[layer][:], sw(layer, "conv_b"), 0.5, None, ALU.mult)
                dve.wait_ge(s_neg_a, n + 1)
                setup_link(dve.tensor_scalar(neg_a[layer][:], neg_a[layer][:], -1.0, None, ALU.mult))

            for n, layer in enumerate((0, 1, 2, 3)):
                dve.wait_ge(s_cond_pe, n + 1)
                is_att = layer in ATT
                m = 2 * DC if is_att else 3 * DC
                bias = aw(layer, "emb_b") if is_att else sw(layer, "ada_b")
                g, b = ((aw(layer, "film_g"), aw(layer, "film_b")) if is_att
                        else (sw(layer, "norm_g"), sw(layer, "norm_b")))
                raw = mod_raw[:, 0:m, :]
                setup_link(dve.tensor_tensor(raw, bank[n][:, 0:m * B].rearrange("p (m b) -> p m b", b=B),
                                             bias.unsqueeze(2).broadcast_to([P, m, B]), ALU.add))
                at_scale, at_shift = (0, DC) if is_att else (DC, 0)
                for c in range(DC):
                    sc, sh = raw[:, at_scale + c, :], raw[:, at_shift + c, :]
                    to_s = mod_all[:, :, MOD_AT[layer] + c]
                    to_h = mod_all[:, :, MOD_AT[layer] + DC + c]
                    setup_link(dve.tensor_scalar(to_s, sc, 1.0, g[:, c:c + 1], ALU.add, ALU.mult))
                    setup_link(dve.tensor_scalar(to_h, sc, 1.0, b[:, c:c + 1], ALU.add, ALU.mult))
                    setup_link(dve.tensor_tensor(to_h, to_h, sh, ALU.add))
                if is_att:
                    both = mod_all[:, :, MOD_AT[layer]:MOD_AT[layer] + 2 * DC]
                    setup_link(dve.tensor_scalar(both, both, 0.5, None, ALU.mult))
            for n in range(2):
                dve.wait_ge(s_cond_pe, 5 + n)
                dve.tensor_tensor(gate_nat[:, n, :], bank[4 + n][0:B, 0:D], gate_bias[:, n, :], ALU.add).then_inc(s_gate_nat, 1)
            dve.wait_ge(s_gate_nat, 2)
            dve.wait_ge(s_zero, 2)
            dve.memset(stats[:], 0.0).then_inc(s_setup, 1)
            dve.wait_ge(s_setup, 1)

            def moments(src, var, link):
                for t in range(TT):
                    ins = dve.bn_stats(stats[:, t, :], src(t))
                link(ins)
                dve.tensor_copy(var_eps[:], stats[:, :, 2])
                for t in range(TT):
                    ins = dve.bn_aggr(mv[:, t, :], stats[:, t, :])
                link(ins)
                dve.tensor_scalar(var_eps[:], mv[:, :, 1], EPS, None, ALU.add).then_inc(var, 1)

            def normed(src, root, k, done):
                dve.wait_ge(root, k)
                for t in range(TT):
                    dve.tensor_scalar(xn[:, t, :], src(t), mv[:, t, 0:1], rstd[:, t:t + 1], ALU.subtract,
                                      ALU.mult).then_inc(done, 1)

            def chain(sem_, base, length):
                count = [0]

                def link(ins):
                    count[0] += 1
                    ins.then_inc(sem_, 1)
                    dve.wait_ge(sem_, base * length + count[0])
                return link, count

            def halves(tile, h):
                return tile[:, 2 * h:2 * h + 2, :]

            def by_token(b):
                return b[:].rearrange("p (t d) -> p t d", d=D)

            def attention(ai, layer, s, b):
                heads = HEADS[ATT.index(layer)]
                width = D // heads
                link, count = chain(a_links, ai, ATT_LINKS)
                src = x_in if layer == 0 else x_res[s]
                if layer == 0:
                    dve.wait_ge(s_x, 32 * b + 32)
                    link(dve.tensor_scalar(mask_row, mrow_i, 1.0, None, ALU.is_equal))
                    dve.tensor_scalar(mask_row, mask_row, MASKED, None, ALU.mult).then_inc(a_mask, 1)
                else:
                    dve.wait_ge(s_mrow3, 16 * b + 16)
                    link(dve.tensor_scalar(mask_row, mrow3, -1.0, 1.0, ALU.mult, ALU.add))
                    dve.sem_inc(s_m3free, 1)
                    dve.tensor_scalar(mask_row, mask_row, -1000000.0, None, ALU.mult).then_inc(a_mask, 1)
                moments(lambda t: src[:, t, :], a_var, link)
                yield from rest(ATT_STAGES["norm"] + ATT_STAGES["root"])
                normed(lambda t: src[:, t, :], a_rstd, 2 * ai + 1, a_xn)
                for stage in ("xn", "turn", "xnT", "k"):
                    yield from rest(ATT_STAGES[stage])
                for c in range(DC):
                    dve.wait_ge(a_k, ai * DC + c + 1)
                    ins = dve.tensor_reduce(kmax[:, c:c + 1], pb[c][:], AX, ALU.max)
                link(ins)
                link(dve.tensor_tensor(kmax[:], kmax[:], aw(layer, "bk"), ALU.add))
                dve.tensor_tensor(kshift[:], aw(layer, "bk"), kmax[:], ALU.subtract).then_inc(a_kshift, 1)
                yield from rest(ATT_STAGES["kmax"])
                qs = qstat[:, 0:TT * heads]
                for h in range(2):
                    qsh = qs[:, h * 2 * heads:(h + 1) * 2 * heads]
                    dve.wait_ge(a_q, ai * 2 + h + 1)
                    ins = dve.tensor_reduce(qsh, pa[h][:].rearrange("p (g w) -> p g w", w=width), AX, ALU.max)
                link(ins)
                for h in range(2):
                    qsh = qs[:, h * 2 * heads:(h + 1) * 2 * heads]
                    dve.tensor_tensor(halves(q, h).rearrange("p t (g w) -> p (t g) w", w=width),
                                      pa[h][:].rearrange("p (g w) -> p g w", w=width),
                                      qsh.unsqueeze(2).broadcast_to([P, 2 * heads, width]), ALU.subtract).then_inc(a_qsub, 1)
                yield from rest(ATT_STAGES["kexp"])
                dve.wait_ge(a_kexp, ai * DC + DC)
                link(dve.reciprocal(krec[:], ksum[:]))
                for c in range(DC):
                    dve.tensor_scalar(kexp[:, c, :], kexp[:, c, :], krec[:, c:c + 1], None, ALU.mult).then_inc(a_kn, 1)
                yield from rest(ATT_STAGES["v"])
                qh = q.rearrange("p t (g w) -> p (t g) w", w=width)
                dve.wait_ge(a_qexp, ai + 1)
                link(dve.tensor_reduce(qs, qh, AX, ALU.add))
                link(dve.reciprocal(qs, qs))
                dve.tensor_tensor(qh, qh, qs.unsqueeze(2).broadcast_to([P, TT * heads, width]), ALU.mult).then_inc(a_qn, 1)
                for stage in ("vkeep", "qT", "qTs"):
                    yield from rest(ATT_STAGES[stage])
                for c in range(DC):
                    dve.wait_ge(a_att, ai * DC + c + 1)
                    dve.tensor_tensor(att[:, c, :], pa[c][:, 0:P], aw(layer, "heads"), ALU.mult).then_inc(a_atts, 1)
                yield from rest(ATT_STAGES["att"] + ATT_STAGES["y"])
                dve.wait_ge(a_y, ai * TT + TT)
                ysrc = lambda t: pb[t // 2][:, (t % 2) * D:(t % 2 + 1) * D]
                moments(ysrc, a_var, link)
                yield from rest(ATT_STAGES["ynorm"] + ATT_STAGES["yroot"])
                normed(ysrc, a_rstd, 2 * ai + 2, a_xn)
                for stage in ("yn", "yturn", "hidden"):
                    yield from rest(ATT_STAGES[stage])
                for c in range(DC):
                    dve.wait_ge(a_hid, ai * DC + c + 1)
                    dve.scalar_tensor_tensor(xnT[:, c, :], qT[:, c, :], 1.0, kexp[:, c, :], ALU.add,
                                             ALU.mult).then_inc(a_act, 1)
                yield from rest(ATT_STAGES["act"] + ATT_STAGES["out"])
                dst = x_next[s] if layer == 0 else x_res[s]
                dve.wait_ge(a_xb, ai + 1)
                for h in range(2):
                    dve.wait_ge(a_o, ai * 2 + h + 1)
                    ins = dve.tensor_tensor(halves(dst, h), by_token(pb[h]), halves(src, h), ALU.add)
                ins.then_inc(a_done, 1)
                dve.wait_ge(a_done, ai + 1)
                dve.sem_inc(s_xfree if layer == 0 else s_out_ready, 1)
                yield from rest(ATT_STAGES["res"])
                assert count[0] == ATT_LINKS, count

            def before(pi, layer, s, b):
                link, count = chain(p_links, pi, PREP_LINKS)
                src = x_next[s] if layer == 1 else x_res[s]
                moments(lambda t: src[:, t, :], p_var, link)
                yield from rest(PREP_STAGES["norm"] + PREP_STAGES["root"])
                normed(lambda t: src[:, t, :], p_rstd, pi + 1, p_xn)
                for stage in ("xn", "turn", "xnT", "in01", "in23"):
                    yield from rest(PREP_STAGES[stage])
                dve.wait_ge(p_pad, pi + 1)
                for first, stage in ((0, "z01"), (2, "z23")):
                    for k in range(TAPS):
                        for c in range(first, first + 2):
                            w = half_w[layer][:, c * TAPS + k:c * TAPS + k + 1]
                            if k == 0:
                                dve.wait_ge(p_xpad, pi * CH + c + 1)
                                ins = dve.tensor_scalar(u[s][:, c, :], xpad[:, c, 0:T], w, half_cb[layer][:, c:c + 1],
                                                        ALU.mult, ALU.add)
                            else:
                                ins = dve.scalar_tensor_tensor(u[s][:, c, :], xpad[:, c, k:k + T], w, u[s][:, c, :],
                                                               ALU.mult, ALU.add)
                                if k == TAPS - 1:
                                    ins.then_inc(p_conv, 1)
                        if k < TAPS - 1:
                            link(ins)
                    yield from rest(PREP_STAGES[stage])
                for first, stage in ((0, "u01"), (2, "u23")):
                    for c in range(first, first + 2):
                        dve.wait_ge(p_ut, pi * CH + c + 1)
                        dve.scalar_tensor_tensor(u[s][:, c, :], dt[s][:, c, :], 1.0, u[s][:, c, :], ALU.add,
                                                 ALU.mult).then_inc(p_u, 1)
                    yield from rest(PREP_STAGES[stage])
                dve.wait_ge(p_z, pi * CH + CH)
                dve.scalar_tensor_tensor(zh[s], zt, 1.0, zh[s], ALU.add, ALU.mult).then_inc(p_sz, 1)
                yield from rest(PREP_STAGES["x"])
                parts = bc_parts[s]
                dve.wait_ge(p_x, pi * 2 + 2)
                rows = pb[1][0:3 * NB, :]
                link(dve.tensor_copy(parts[:], rows))
                link(dve.tensor_tensor(bc_rest, rows, parts[:], ALU.subtract))
                dve.tensor_copy(parts[NB:2 * NB, :], bc_rest[NB:2 * NB, :])
                link(dve.tensor_copy(parts[2 * NB:, :], bc_rest[2 * NB:, :]))
                link(dve.tensor_tensor(bc_rest[2 * NB:, :], bc_rest[2 * NB:, :], parts[2 * NB:, :], ALU.subtract))
                link(dve.tensor_copy(parts[2 * NB:, :], bc_rest[2 * NB:, :]))
                dve.sem_inc(p_parts, 1)
                for stage in ("parts", "dt01", "dt23"):
                    yield from rest(PREP_STAGES[stage])
                dve.wait_ge(p_dtp, pi * CH + CH)
                if layer == 1 and not isinstance(b, int):
                    dve.wait_ge(s_out, 16 * (b - 1))
                for stage in ("soft", "dt", "dtu"):
                    yield from rest(PREP_STAGES[stage])
                assert count[0] == PREP_LINKS, count

            def skip(s, layer, h, si):
                dve.wait_ge(m_sum, si * UNITS + (h + 1) * N)
                for c in range(HC):
                    at = h * HC + c
                    ins = dve.scalar_tensor_tensor(u[s][:, at, :], u[s][:, at, :], sw(layer, "d_skip")[:, at:at + 1],
                                                   y_banks[c][:], ALU.mult, ALU.add)
                ins.then_inc(m_skip, 1)

            def after(qi, layer, s, b):
                link, count = chain(o_links, qi, POST_LINKS)
                skip(s, layer, 1, qi)
                dve.wait_ge(m_skip, qi * HALVES + 2)
                dve.tensor_tensor(u[s][:, HC:], u[s][:, HC:], zh[s][:, HC:], ALU.mult).then_inc(o_gated, 1)
                yield from rest(POST_STAGES["skip"] + POST_STAGES["out"])
                dve.wait_ge(o_gate, qi + 1)
                for h in range(2):
                    dve.wait_ge(o_o, qi * 2 + h + 1)
                    dve.tensor_tensor(halves(xn, h), by_token(pa[h]), gate[:].unsqueeze(1).broadcast_to([P, 2, D]),
                                      ALU.mult).then_inc(o_og, 1)
                if layer == 1:
                    dve.wait_ge(o_og, qi * 2 + 2)
                    link(dve.tensor_tensor(x_res[s][:], x_next[s][:], xn[:], ALU.add))
                yield from rest(POST_STAGES["gate"] + POST_STAGES["gather"])
                if layer == 2:
                    for h in range(2):
                        dve.wait_ge(o_g, (qi // 4 * 2 + qi % 4 - 2) * 2 + h + 1 if isinstance(qi, int) else (b * 2 + h + 1))
                        ins = dve.tensor_tensor(halves(x_res[s], h), by_token(pb[h]), halves(x_res[s], h), ALU.add)
                    link(ins)
                yield from rest(POST_STAGES["res"])
                assert count[0] == POST_LINKS, count

            def scan(si, layer, s):
                def step(k):
                    dve.wait_ge(m_decay, (si * UNITS + k + 1) * HC)
                    dve.wait_ge(m_inject, si * UNITS + k + 1)
                    st = state[:, k % STATES].rearrange("p c t -> p (c t)")
                    dve.tensor_tensor_scan(st, decay[:, k % DECAYS].rearrange("p c t -> p (c t)"), st, 0.0, ALU.mult,
                                           ALU.add).then_inc(m_scan, 1)

                step(0)
                for k in range(UNITS):
                    if k + 1 < UNITS:
                        step(k + 1)
                    dve.wait_ge(m_scan, si * UNITS + k + 1)
                    dve.wait_ge(m_cps, si * UNITS + k + 1)
                    st = state[:, k % STATES]
                    dve.tensor_tensor(st, st, c_bank[:].unsqueeze(1).broadcast_to([P, HC, T]), ALU.mult).then_inc(m_prod, 1)
                    if k == N + 1:
                        skip(s, layer, 0, si)
                    yield

            run_batches(dve, attention, before, after, scan)

        @block.tensor
        def _(pe):
            pe.wait_ge(s_const, 64)
            pe.wait_ge(s_silu, 1)
            pe.wait_ge(s_cond_w, 64)
            for n, layer in enumerate((0, 1, 2, 3)):
                w = film_sb[layer] if layer in ATT else ada_sb[layer]
                m = 2 * DC if layer in ATT else 3 * DC
                for c in range(m):
                    for k in range(EC):
                        ins = pe.matmul(bank[n][:, c * B:(c + 1) * B], w[:, k, c * P:(c + 1) * P], silu_c[:, k, :],
                                        start=(k == 0), stop=(k == EC - 1))
                ins.then_inc(s_cond_pe, 1)
            for n, layer in enumerate(SSM):
                for k in range(EC):
                    ins = pe.matmul(bank[4 + n][0:B, 0:D], silu_c[:, k, :], ada_sb[layer][:, k, 2 * D:3 * D],
                                    start=(k == 0), stop=(k == EC - 1))
                ins.then_inc(s_cond_pe, 1)
            pe.wait_ge(s_setup, 1)

            def turn(src, banks, done):
                for c in range(DC):
                    for t in range(TT):
                        ins = pe.transpose(banks[c][:, t * P:(t + 1) * P], src[:, t, c * P:(c + 1) * P], ident)
                    ins.then_inc(done, 1)

            def per_token(banks, weights, lhs, chunks, done, ones=None, bias=None):
                for t in range(TT):
                    dst = banks[t // 2][:, (t % 2) * D:(t % 2 + 1) * D]
                    for c in range(chunks):
                        ins = pe.matmul(dst, lhs(c, t), weights(c), start=(c == 0), stop=(c == chunks - 1 and bias is None))
                    if bias is not None:
                        ins = pe.matmul(dst, ones, bias, start=False, stop=True)
                    if t % 2:
                        ins.then_inc(done, 1)

            def attention(ai, layer, s, b):
                w = {n: aw(layer, n).rearrange("p (c n) -> p c n", c=DC) for n in ("wq", "wk", "wv", "wo")}
                normT = lambda c, t: xnT[:, c, t * P:(t + 1) * P]
                for stage in ("norm", "root", "xn"):
                    yield from rest(ATT_STAGES[stage])
                pe.wait_ge(a_xn, 2 * ai * TT + TT)
                turn(xn, pa, a_xT)
                yield from rest(ATT_STAGES["turn"] + ATT_STAGES["xnT"])
                pe.wait_ge(a_xnT, ai * DC + DC)
                pe.wait_ge(a_mask, ai + 1)
                for e in range(DC):
                    for c in range(DC):
                        pe.matmul(pb[e][:], w["wk"][:, c, e * P:(e + 1) * P], xnT[:, c, :], start=(c == 0), stop=False)
                    pe.matmul(pb[e][:], ones_row[0], mask_row, start=False, stop=True).then_inc(a_k, 1)
                per_token(pa, lambda c: w["wq"][:, c, :], normT, DC, a_q, ones_row[layer], qv_bias[layer][:, 0:D])
                for stage in ("k", "kmax", "kexp"):
                    yield from rest(ATT_STAGES[stage])
                pe.wait_ge(a_kexp, ai * DC + DC)
                per_token(pb, lambda c: w["wv"][:, c, :], normT, DC, a_v, ones_row[layer], qv_bias[layer][:, D:])
                yield from rest(ATT_STAGES["v"])
                pe.wait_ge(a_kn, ai * DC + DC)
                pe.wait_ge(a_qsub, ai * 2 + 2)
                for t in range(TT):
                    for c in range(DC):
                        ins = pe.transpose(pa[t // 2][:, (t % 2) * D + c * P:(t % 2) * D + (c + 1) * P],
                                           kexp[:, c, t * P:(t + 1) * P], ident)
                    if t % 2:
                        ins.then_inc(a_kT, 1)
                yield from rest(ATT_STAGES["vkeep"])
                pe.wait_ge(a_qn, ai + 1)
                pe.wait_ge(a_vs, ai * TT + TT)
                turn(q, pb, a_qT)
                yield from rest(ATT_STAGES["qT"])
                pe.wait_ge(a_knat, ai * 2 + 2)
                over, free = (v, knat) if layer == 0 else (knat, v)
                for c in range(DC):
                    for t in range(TT):
                        ins = pe.matmul(pa[c][:, 0:P], over[:, t, c * P:(c + 1) * P], free[:, t, c * P:(c + 1) * P],
                                        start=(t == 0), stop=(t == TT - 1))
                    ins.then_inc(a_att, 1)
                yield from rest(ATT_STAGES["qTs"] + ATT_STAGES["att"])
                pe.wait_ge(a_qTs, ai * DC + DC)
                pe.wait_ge(a_atts, ai * DC + DC)
                for t in range(TT):
                    for c in range(DC):
                        ins = pe.matmul(pb[t // 2][:, (t % 2) * D + c * P:(t % 2) * D + (c + 1) * P],
                                        qT[:, c, t * P:(t + 1) * P], att[:, c, :], start=True, stop=True)
                    ins.then_inc(a_y, 1)
                for stage in ("y", "ynorm", "yroot", "yn"):
                    yield from rest(ATT_STAGES[stage])
                pe.wait_ge(a_xn, 2 * ai * TT + 2 * TT)
                turn(xn, pa, a_yT)
                for stage in ("yturn", "hidden", "act"):
                    yield from rest(ATT_STAGES[stage])
                pe.wait_ge(a_act, ai * DC + DC)
                per_token(pb, lambda c: w["wo"][:, c, :], normT, DC, a_o)
                yield from rest(ATT_STAGES["out"] + ATT_STAGES["res"])

            def before(pi, layer, s, b):
                w_in = sw(layer, "w_in").rearrange("p (c n) -> p c n", c=DC)
                w_x = sw(layer, "w_x").rearrange("p (c n) -> p c n", c=CH)
                w_dt = sw(layer, "w_dt")[0:DTR, :]
                for stage in ("norm", "root", "xn"):
                    yield from rest(PREP_STAGES[stage])
                pe.wait_ge(p_xn, pi * TT + TT)
                if layer == 1:
                    turn(xn, pa, p_xT)
                else:
                    for c in range(DC):
                        for t in range(TT):
                            ins = pe.matmul(pa[c][:], xn[:, t, c * P:(c + 1) * P], permute[:, t, :],
                                            start=(t == 0), stop=(t == TT - 1))
                        ins.then_inc(p_xT, 1)
                yield from rest(PREP_STAGES["turn"] + PREP_STAGES["xnT"])
                pe.wait_ge(p_xnT, pi * DC + DC)

                def expand(first, banks):
                    for e in range(first, first + 2):
                        for c in range(DC):
                            ins = pe.matmul(banks[e % 2][:], w_in[:, c, e * P:(e + 1) * P], xnT[:, c, :],
                                            start=(c == 0), stop=(c == DC - 1))
                        ins.then_inc(p_in, 1)

                expand(0, pb)
                yield from rest(PREP_STAGES["in01"])
                expand(2, pa)
                yield from rest(PREP_STAGES["in23"])
                pe.wait_ge(p_xpad, pi * CH + 2)
                expand(4, pb)
                yield from rest(PREP_STAGES["z01"])
                pe.wait_ge(p_xpad, pi * CH + 4)
                expand(6, pa)
                for stage in ("z23", "u01", "u23"):
                    yield from rest(PREP_STAGES[stage])
                pe.wait_ge(p_u, pi * CH + CH)
                pe.wait_ge(p_z, pi * CH + CH)
                for c in range(CH):
                    ins = pe.matmul(pb[0][0:DTR, :], w_x[:, c, 0:DTR], u[s][:, c, :], start=(c == 0), stop=(c == CH - 1))
                ins.then_inc(p_x, 1)
                for c in range(CH):
                    ins = pe.matmul(pb[1][0:3 * NB, :], w_x[:, c, DTR:], u[s][:, c, :], start=(c == 0), stop=(c == CH - 1))
                ins.then_inc(p_x, 1)
                yield from rest(PREP_STAGES["x"])

                def steps(first, banks):
                    for c in range(first, first + 2):
                        pe.matmul(banks[c % 2][:], w_dt[:, c * P:(c + 1) * P], dtr, start=True, stop=True).then_inc(p_dtp, 1)

                yield from rest(PREP_STAGES["parts"])
                pe.wait_ge(p_dtr, pi + 1)
                steps(0, pa)
                yield from rest(PREP_STAGES["dt01"])
                pe.wait_ge(p_parts, pi + 1)
                steps(2, pb)
                for stage in ("dt23", "soft", "dt", "dtu"):
                    yield from rest(PREP_STAGES[stage])

            def after(qi, layer, s, b):
                w_out = sw(layer, "w_out").rearrange("p (c n) -> p c n", c=CH)
                yield from rest(POST_STAGES["skip"])
                pe.wait_ge(o_gated, qi + 1)
                pe.wait_ge(m_half0, qi + 1)
                pe.wait_ge(o_row, qi + 1)
                pe.matmul(pb[0][:, 0:D], ones_row8, gate_row[:], start=True, stop=True).then_inc(o_gps, 1)
                per_token(pa, lambda c: w_out[:, c, :], lambda c, t: u[s][:, c, t * P:(t + 1) * P], CH, o_o)
                yield from rest(POST_STAGES["out"] + POST_STAGES["gate"])
                if layer == 2:
                    pe.wait_ge(o_gate, qi + 1)
                    pe.wait_ge(o_og, qi * 2 + 2)
                    per_token(pb, lambda c: xn[:, c, :], lambda c, t: permute[:, c, t * P:(t + 1) * P], TT, o_g)
                yield from rest(POST_STAGES["gather"] + POST_STAGES["res"])

            def scan(si, layer, s):
                parts = bc_parts[s]

                def spread(row, dst, done):
                    pe.matmul(dst[:], sel_sb[:, row:row + 1].broadcast_to([3 * NB, P]), parts[:], start=True,
                              stop=True).then_inc(done, 1)

                def spread_b(k):
                    wait_back(pe, m_brow, si, k, 1)
                    spread(k % N, b_bank, m_bps)

                def sum_up(k):
                    pe.wait_ge(m_prod, si * UNITS + k + 1)
                    if k % N == 0 and not (isinstance(si, int) and si == 0 and k == 0):
                        pe.wait_ge(m_skip, si * HALVES + k // N)
                    for c in range(HC):
                        ins = pe.matmul(y_banks[c][:], ident, state[:, k % STATES, c, :], start=(k % N == 0),
                                        stop=(k % N == N - 1))
                    ins.then_inc(m_sum, 1)

                pe.wait_ge(p_parts, si + 1)
                spread_b(0)
                spread_b(1)
                for k in range(UNITS):
                    if k + 2 < UNITS:
                        spread_b(k + 2)
                    wait_back(pe, m_prod, si, k, 1)
                    spread(N + k % N, c_bank, m_cps)
                    if k >= 1:
                        sum_up(k - 1)
                    yield
                sum_up(UNITS - 1)

            run_batches(pe, attention, before, after, scan)


def kernel(**inputs):
    import numpy as np
    import concourse.bacc as bacc
    from concourse import mybir as mb
    from concourse.bass_utils import run_bass_kernel_spmd as run

    a = {k: np.asarray(v) for k, v in inputs.items()}

    def chunks(w):
        c = w.shape[0] // P
        return w.reshape(c, P, -1).transpose(1, 0, 2).reshape(P, -1)

    def cols(vec):
        return vec.reshape(-1, P).T

    def rows_of(w):
        full = np.zeros((P, w.shape[1]), w.dtype)
        full[:w.shape[0]] = w
        return full

    def pack(parts, names):
        return np.ascontiguousarray(np.concatenate([parts[n] for n, _ in names], axis=1))

    arrays, args = {}, {}
    nc = bacc.Bacc("TRN2", target_bir_lowering=False, num_devices=1)

    def give(name, array):
        array = np.ascontiguousarray(array)
        arrays[name] = array
        return nc.dram_tensor(name, array.shape, mb.dt.from_np(array.dtype), kind="ExternalInput").ap()

    def heads(n):
        w = np.arange(P) // (D // n)
        return (w[:, None] == w[None, :]).astype(np.float32)

    att_packs, ssm_packs, film_w, ada_w, att_rows = {}, {}, {}, {}, {}
    for n, (layer, names) in enumerate((
            (0, ("norm_scale", "norm_bias", "film_emb_W", "film_emb_b", "film_norm_scale", "film_norm_bias",
                 "film_out_W", "film_out_b")),
            (3, ("ln_w", "ln_b", "W_emb", "b_emb", "ln2_w", "ln2_b", "W_out", "b_out")))):
        g = lambda s: a[f"L{layer}_cond_{s}"]
        ng, nb, ew, eb, fg, fb, ow, ob = (g(s) for s in names)
        parts = dict(wq=chunks(g("Wq")), wk=chunks(g("Wk")), wv=chunks(g("Wv")), wo=chunks(ow), bk=cols(g("bk")),
                     norm_g=cols(ng), norm_b=cols(nb), film_g=cols(fg), film_b=cols(fb), emb_b=cols(eb),
                     heads=heads(HEADS[n]))
        att_packs[layer] = give(f"att_pack_{layer}", pack(parts, ATT_PACK))
        film_w[layer] = give(f"film_w_{layer}", ew)
        att_rows[layer] = [give(f"att_row_{layer}_{k}", r) for k, r in enumerate((g("bq"), g("bv"), ob))]
    gate_rows = []
    for layer in SSM:
        g = lambda s: a[f"L{layer}_cond_{s}"]
        if layer == 1:
            w_in, w_x, w_dt, w_out, ada = (g(s).T for s in ("in_proj_w", "x_proj_w", "dt_proj_w", "out_proj_w", "ada_w"))
            conv, dt_b, ng, nb, ab = g("conv_w"), g("dt_proj_b"), g("ln_g"), g("ln_b"), g("ada_b")
        else:
            w_in, w_x, w_dt, w_out, ada = (g(s) for s in ("W_in", "W_xp", "W_dt", "W_out", "W_ada"))
            conv, dt_b, ng, nb, ab = g("conv_w")[:, 0, :], g("b_dt"), g("gamma"), g("beta"), g("b_ada")
        parts = dict(w_in=chunks(w_in), w_x=chunks(np.concatenate([w_x] + 2 * [w_x[:, DTR:]], axis=1)), w_dt=rows_of(w_dt), w_out=chunks(w_out), conv_w=chunks(conv),
                     conv_b=cols(g("conv_b")), dt_b=cols(dt_b), a_log=chunks(g("A_log")), d_skip=cols(g("D_param")),
                     norm_g=cols(ng), norm_b=cols(nb), ada_b=cols(ab))
        ssm_packs[layer] = give(f"ssm_pack_{layer}", pack(parts, SSM_PACK))
        ada_w[layer] = give(f"ada_w_{layer}", ada)
        gate_rows.append(give(f"gate_row_{layer}", ab[2 * D:]))
    mask = a["mask_BxSx1_fk1"].reshape(B, T)
    by_tile = lambda m: m.reshape(B, TT, P).transpose(2, 0, 1).reshape(P, B * TT)
    parts = dict(ident=np.eye(P, dtype=np.float32), token=np.arange(T, dtype=np.float32).reshape(TT, P).T,
                 cond=a["cond_2048"].T.reshape(EC, P, B).transpose(1, 0, 2).reshape(P, EC * B),
                 keep3=by_tile(mask), ones=np.ones((P, P), np.float32))
    const_pack = give("const_pack", pack(parts, CONST_PACK))
    sel = np.tile(np.eye(NB), (3, 1)).astype(mb.dt.np(BF16))
    sel = give("sel", sel)
    order = give("order", a["itok_S_0_1023"])
    mask_cols = give("mask_cols", by_tile(a["mask_BxS_ik0"]))
    mask_rows0 = give("mask_rows0", a["mask_BxS_ik0"])
    mask_rows3 = give("mask_rows3", mask)
    x = give("x", a["x"])
    out = nc.dram_tensor("out", (B, T, D), mb.dt.float32, kind="ExternalOutput").ap()
    bass_cond_seq(nc, x, out, mask_cols, mask_rows0, mask_rows3, order, const_pack, sel, att_packs, ssm_packs,
                  film_w, ada_w, att_rows, gate_rows)
    r = run(nc, [arrays], core_ids=[0])
    return r.results[0]["out"]
```

```python
from contextlib import ExitStack

import concourse.bass as bass
from concourse import mybir

P = 128
B, T, D = 8, 512, 256
TT, DC = T // P, D // P
DI, CH, N = 512, 4, 16
DTR, TAPS = 64, 4
E = 512
EC = E // P
NB = 2 * N
EPS = 1e-5
MASKED = -1e30
HEADS = (16, 8)
ATT, SSM = (0, 3), (1, 2)
HALVES = 2
HC = CH // HALVES
UNITS = HALVES * N
QUAD, SUMS = 4, 3
QUADS = UNITS // QUAD
UNIT_STEPS = 2
AHEAD = 3
STATES, DECAYS, B_ROWS, C_ROWS = 4, 2, 2, 2

ALU = mybir.AluOpType
ACT = mybir.ActivationFunctionType
AX = mybir.AxisListType.X
F32, BF16, I32 = mybir.dt.float32, mybir.dt.bfloat16, mybir.dt.int32

ATT_PACK = (("wq", DC * D), ("wk", DC * D), ("wv", DC * D), ("wo", DC * D), ("bk", DC),
            ("norm_g", DC), ("norm_b", DC), ("film_g", DC), ("film_b", DC), ("emb_b", 2 * DC), ("heads", P))
SSM_PACK = (("w_in", DC * 2 * DI), ("w_x", CH * (DTR + NB)), ("w_dt", DI), ("w_out", CH * D),
            ("conv_w", CH * TAPS), ("conv_b", CH), ("dt_b", CH), ("a_log", CH * N), ("d_skip", CH),
            ("norm_g", DC), ("norm_b", DC), ("ada_b", 3 * DC))
CONST_PACK = (("ident", P), ("token", TT), ("cond", EC * B), ("keep3", B * TT), ("ones", P))


def columns(pack):
    at, out = 0, {}
    for name, n in pack:
        out[name] = (at, at + n)
        at += n
    return out, at


MOD_AT = {0: 0, 3: 2 * DC + TT, 1: 4 * DC + 2 * TT, 2: 6 * DC + 2 * TT}
MOD_PICK = 8 * DC + 2 * TT
MODS = MOD_PICK + 1
GATES_AT = 64

ATT_STAGES = dict(lead=1, norm=4, root=4, xn=3, turn=3, xnT=3, k=7, kmax=4, kexp=4, q=7, qmax=5, v=7, vkeep=4, kT=3,
                  knat=4, qT=3, qTs=4, mix=4, att=3, y=5, ynorm=4, yroot=4, yn=3, yturn=4, hidden=4, act=4, out=7, res=3)
PREP_STAGES = {layer: dict(norm=4, root=4, xn=3, turn=9 if layer == 2 else 4, xnT=3, in01=6, in23=6, z01=6, z23=6, u01=4,
                           u23=4, x=8, parts=5, dt01=5, dt23=5, soft=8, dt=8) for layer in SSM}
POST_STAGES = {layer: dict(lead=8, skip=4, out=12, gate=4, gather=11 if layer == 2 else 1, res=3) for layer in SSM}
ATT_TICKS = sum(ATT_STAGES.values())
PREP_TICKS, POST_TICKS = ({layer: sum(d.values()) for layer, d in stages.items()} for stages in (PREP_STAGES, POST_STAGES))
FINISHED = -(-(UNITS - AHEAD) * POST_TICKS[2] // (POST_TICKS[2] + PREP_TICKS[1]))
ATT_UNITS = ((12, 44), (44, 75), (75, 104), (3 * UNITS + FINISHED, 4 * UNITS))
assert ATT_UNITS[2][0] >= 2 * UNITS + FINISHED

ATT_LINKS, PREP_LINKS, POST_LINKS = 11, 12, 1

PAIRS = B // 2


def beside(units, work, ticks, also=None):
    done = 0
    for k, _ in enumerate(units):
        while done < ticks * (k + 1) // (UNIT_STEPS * (UNITS - AHEAD)):
            next(work, None)
            done += 1
        if also:
            also(k)
    for _ in work:
        pass


class Stream:

    def __init__(self, *layers):
        self.layers = [[gen, start, end, 0] for gen, start, end in layers]

    def until(self, unit):
        for layer in self.layers:
            gen, start, end, done = layer
            due = int(ATT_TICKS * min(max(unit - start, 0), end - start) / (end - start))
            for _ in range(due - done):
                next(gen, None)
            layer[3] = max(due, done)
            if unit >= end:
                for _ in gen:
                    pass

    def beside(self, slot):
        return lambda k: self.until(slot * UNITS + (k + 1) / UNIT_STEPS)


class Scan:

    def __init__(self, si, layer, s, then=None):
        self.si, self.layer, self.s, self.then = si, layer, s, then

    def at(self, k):
        if 0 <= k < UNITS:
            return self, k
        return self.then and (self.then, k - UNITS)


def one_after_another(*parts):
    for part in parts:
        yield from part


def together(a, a_ticks, b, b_ticks):
    ticks, done = max(a_ticks, b_ticks), [0, 0]
    for k in range(ticks):
        for n, (chain, own) in enumerate(((a, a_ticks), (b, b_ticks))):
            while done[n] < own * (k + 1) // ticks:
                next(chain, None)
                done[n] += 1
        yield
    for _ in one_after_another(a, b):
        pass


def run_batches(eng, att, prep, post, scan):
    def mid(p, s):
        return (one_after_another(post(4 * p + s, 1, s, 2 * p + s), prep(2 + 4 * p + s, 2, s, 2 * p + s)),
                POST_TICKS[1] + PREP_TICKS[2])

    def end(p, s):
        return (one_after_another(post(4 * p + 2 + s, 2, s, 2 * p + s), prep(4 + 4 * p + s, 1, s, 2 * p + 2 + s)),
                POST_TICKS[2] + PREP_TICKS[1])

    for _ in one_after_another(att(0, 0, 0, 0), together(prep(0, 1, 0, 0), PREP_TICKS[1], att(1, 0, 1, 1), ATT_TICKS)):
        pass
    beside(scan(Scan(0, 1, 0, Scan(1, 1, 1))), prep(1, 1, 1, 1), PREP_TICKS[1])
    with eng.Fori(0, PAIRS - 1) as p:
        at, ai = 1 + 4 * p, 2 + 4 * p
        atts = Stream((att(ai, 0, 0, 2 * p + 2), *ATT_UNITS[0]), (att(ai + 1, 0, 1, 2 * p + 3), *ATT_UNITS[1]),
                      (att(ai + 2, 3, 0, 2 * p), *ATT_UNITS[2]), (att(ai + 3, 3, 1, 2 * p + 1), *ATT_UNITS[3]))
        beside(scan(Scan(at, 1, 1, Scan(at + 1, 2, 0))), *mid(p, 0), atts.beside(0))
        beside(scan(Scan(at + 1, 2, 0, Scan(at + 2, 2, 1))), *mid(p, 1), atts.beside(1))
        beside(scan(Scan(at + 2, 2, 1, Scan(at + 3, 1, 0))), *end(p, 0), atts.beside(2))
        beside(scan(Scan(at + 3, 1, 0, Scan(at + 4, 1, 1))), *end(p, 1), atts.beside(3))
    p = PAIRS - 1
    at, ai = 1 + 4 * p, 2 + 4 * p
    beside(scan(Scan(at, 1, 1, Scan(at + 1, 2, 0))), *mid(p, 0))
    beside(scan(Scan(at + 1, 2, 0, Scan(at + 2, 2, 1))), *mid(p, 1))
    beside(scan(Scan(at + 2, 2, 1)), one_after_another(post(4 * p + 2, 2, 0, 2 * p), att(ai, 3, 0, 2 * p)),
           POST_TICKS[2] + ATT_TICKS)
    for _ in one_after_another(post(4 * p + 3, 2, 1, 2 * p + 1), att(ai + 1, 3, 1, 2 * p + 1)):
        pass


def rest(ticks):
    for _ in range(ticks):
        yield


def paced(ticks, count, steps):
    passed = 0
    for n, _ in enumerate(steps):
        while passed < min(ticks - 1, ticks * (n + 1) // count):
            passed += 1
            yield
    assert n + 1 == count, (n, count)
    yield from rest(ticks - passed)


def bass_cond_seq(nc, x, out, mask_cols, mask_rows0, mask_rows3, order, const_pack, sel, att_packs, ssm_packs,
                  film_w, ada_w, att_rows, gate_rows):
    ctx = ExitStack()
    with ctx:
        def sb(name, shape, dt=F32):
            return ctx.enter_context(nc.sbuf_tensor(name, shape, dt))

        def sem(name):
            return ctx.enter_context(nc.semaphore(name))

        bank = [ctx.enter_context(nc.psum_tensor(f"bank{k}", [P, 512], F32)) for k in range(8)]
        y_banks, b_bank, c_bank = bank[0:HC], bank[2], bank[3]
        pa, pb = bank[4:6], bank[6:8]

        catt, n_att = columns(ATT_PACK)
        cssm, n_ssm = columns(SSM_PACK)
        cconst, n_const = columns(CONST_PACK)
        att_sb = {layer: sb(f"att_pack{layer}", [P, n_att]) for layer in ATT}
        ssm_sb = {layer: sb(f"ssm_pack{layer}", [P, n_ssm]) for layer in SSM}
        const_sb = sb("const_sb", [P, n_const])
        sel_sb = sb("sel_sb", [3 * NB, NB], BF16)

        def aw(layer, name):
            return att_sb[layer][:, catt[name][0]:catt[name][1]]

        def sw(layer, name):
            return ssm_sb[layer][:, cssm[name][0]:cssm[name][1]]

        def cw(name):
            return const_sb[:, cconst[name][0]:cconst[name][1]]

        ident = cw("ident")
        ones_row, ones_row8 = {0: cw("ones")[0:1, :], 3: cw("ones")[32:33, :]}, cw("ones")[GATES_AT:GATES_AT + B, :]
        out_bias = sb("out_bias", [P, 2, D])
        rows = sb("rows", [P, T])
        qv_bias = {0: rows[0:1, :], 3: rows[32:33, :]}
        mrow_i, mrow3 = rows[64:65, :].bitcast(I32), rows[96:97, :]
        permute = sb("permute", [P, TT, T])
        neg_half = sb("neg_half", [P, TT])
        mod_all = sb("mod_all", [P, B, MODS])
        mod_att = sb("mod_att", [P, 2 * DC + TT])
        mod_prep = sb("mod_prep", [P, 2 * DC])
        gate_pick = sb("gate_pick", [P, 1])
        half_w = {layer: sb(f"half_w{layer}", [P, CH * TAPS]) for layer in SSM}
        half_cb = {layer: sb(f"half_cb{layer}", [P, CH]) for layer in SSM}
        neg_a = {layer: sb(f"neg_a{layer}", [P, CH * N]) for layer in SSM}

        kept = sb("kept", [P, 8, CH, T])
        u, zh, dt, dtu = ([kept[:, 4 * s + k] for s in range(2)] for k in range(4))
        x_next = [sb(f"x_next{s}", [P, TT, D]) for s in range(2)]
        x_res = [sb(f"x_res{s}", [P, TT, D]) for s in range(2)]
        bc_parts = [sb(f"bc_parts{s}", [3 * NB, T], BF16) for s in range(2)]

        prep_xn, prep_xnT = [dtu[s][:, 0:2].rearrange("p c (t d) -> p (c t) d", d=D) for s in range(2)], [
            dtu[s][:, 2:4] for s in range(2)]
        zt = dtu
        gated_out = [dt[s][:, 0:2].rearrange("p c (t d) -> p (c t) d", d=D) for s in range(2)]
        gate = [dt[s][:, 2, 0:D] for s in range(2)]
        on_gates = slice(GATES_AT, GATES_AT + B)
        gate_nat = sw(SSM[0], "w_dt")[on_gates, :].rearrange("p (l d) -> p l d", d=D)
        gate_row = [dt[s][on_gates, 3, 0:D] for s in range(2)]

        decay = sb("decay", [P, DECAYS, HC, T])
        state = sb("state", [P, STATES, HC, T])
        pair = sb("pair", [P, HC, T])
        b_rows = sb("b_rows", [P, B_ROWS, T])
        c_rows = sb("c_rows", [P, C_ROWS, T])

        att_norm, prep_norm = ({k: sb(f"{n}_{k}", [P, TT, w]) for k, w in (
            ("stats", 6), ("mv", 2), ("var_eps", 1), ("rstd", 1))} for n in ("att", "prep"))
        xn = sb("xn", [P, TT, D])
        xnT = sb("xnT", [P, DC, T])
        kmax, kshift, ksum, krec = (sb(n, [P, DC]) for n in ("kmax", "kshift", "ksum", "krec"))
        qstat = sb("qstat", [P, TT * 16])
        kexp = sb("kexp", [P, DC, T])
        v = sb("v", [P, TT, D])
        mask_row = kexp[0:1, 0, :]
        q = xn
        knat = kexp[:].rearrange("p c (t d) -> p (c t) d", d=D)
        qT = xnT
        att = sb("att", [P, DC, P])
        conv_in = sb("conv_in", [P, CH * (T + TAPS - 1)])
        xpad = conv_in[:].rearrange("p (c t) -> p c t", c=CH)
        dtr, bc_rest = conv_in[0:DTR, 0:T], conv_in[DTR:DTR + NB, T:2 * T]
        bc_mid = conv_in[DTR:DTR + NB, 2 * T:2 * T + T // 2].bitcast(BF16)

        order_i = kexp[:, 0, :].bitcast(I32)
        mask_i = kexp[:, 1, 0:B * TT].bitcast(I32)
        gate_bias = state[0:B, 0, 0, :].rearrange("p (l d) -> p l d", d=D)
        silu_c = xnT[:, 0, 0:EC * B].rearrange("p (k b) -> p k b", k=EC)
        mod_raw = xnT[:, 1, 0:3 * DC * B].rearrange("p (m b) -> p m b", b=B)
        flat = kept[:].rearrange("p s c t -> p (s c t)")
        film_sb = {0: flat[:, 0:EC * 2 * D], 3: flat[:, EC * 2 * D:EC * 4 * D]}
        ada_sb = {1: flat[:, EC * 4 * D:EC * 7 * D], 2: flat[:, EC * 7 * D:EC * 10 * D]}
        film_sb, ada_sb = ({n: w.rearrange("p (k n) -> p k n", k=EC) for n, w in d.items()} for d in (film_sb, ada_sb))

        s_const, s_att_w, s_ssm_w, s_cond_w, s_rows = (sem(n) for n in (
            "const_loaded", "att_weights_loaded", "ssm_weights_loaded", "cond_weights_loaded", "rows_loaded"))
        s_silu_t, s_silu, s_cond_pe, s_gate_nat, s_links, s_neg_a, s_setup, s_zero = (sem(n) for n in (
            "cond_tanh", "cond_silu", "mod_product", "gate_rows_ready", "setup_links", "neg_a_exp", "setup_done",
            "zeroed"))
        s_x, s_mrow3, s_xfree, s_m3free, s_out_ready, *s_out = (sem(n) for n in (
            "x_loaded", "mask3_loaded", "x_next_free", "mask3_free", "x_out_ready", "x_out_stored0", "x_out_stored1"))
        a_links, a_mod, a_var, a_rstd, a_xn, a_xT, a_xnT, a_xb, a_mask, a_k, a_q, a_v, a_kshift, a_kexp, a_kn, a_kT, \
            a_knat, a_qsub, a_qexp, a_qn, a_qT, a_qTs, a_vs, a_att, a_atts, a_y, a_yT, a_hid, a_act, a_o, a_done = (
                sem("a_" + n) for n in (
                    "links", "mod_ready", "variance", "rstd", "xn_ready", "xn_turned", "xnT_ready", "x_biased",
                    "mask_row", "k_product", "q_product", "v_product", "kshift", "k_exp", "k_normed", "k_turned",
                    "k_natural", "q_shifted", "q_exp", "q_normed", "q_turned", "qT_ready", "v_ready", "att_product",
                    "att_ready", "y_product", "y_turned", "hidden_tanh", "hidden_ready", "out_product", "done"))
        p_links, p_mod, p_pad, p_var, p_rstd, p_xn, p_xT, p_xnT, p_in, p_xpad, p_z, p_conv, p_ut, p_u, p_x, p_dtr, p_sz, \
            p_parts, p_dtp, p_abs, p_exp, p_ln, p_dt, p_dtu = (sem("p_" + n) for n in (
                "links", "mod_ready", "pad_zeroed", "variance", "rstd", "xn_ready", "xn_turned", "xnT_ready",
                "in_product", "conv_input", "z_ready", "conv", "u_tanh", "u_ready", "x_product", "dtr_ready", "silu_z",
                "bc_parts", "dt_product", "dt_abs", "dt_exp", "dt_log", "dt_ready", "dtu_ready"))
        m_bps, m_brow, m_cps, m_crow, m_decay, m_inject, m_scan, m_prod, m_pair, m_sum, m_skip, m_half0 = (sem("m_" + n) for n in (
            "b_spread", "b_rows", "c_spread", "c_rows", "decay_ready", "inject_ready", "scanned", "weighted", "pair_added", "summed",
            "skip_added", "first_half_gated"))
        o_links, o_pick, o_row, o_gated, o_gps, o_gate, o_o, o_og, o_g = (sem("o_" + n) for n in (
            "links", "gate_picked", "gate_row", "second_half_gated", "gate_spread", "gate_ready", "out_product",
            "out_gated", "gathered"))

        def wait_back(eng, sem_, si, k, slots, each=1):
            if not (isinstance(si, int) and si * UNITS + k < slots):
                eng.wait_ge(sem_, (si * UNITS + k + 1 - slots) * each)

        block = ctx.enter_context(nc.Block())

        @block.sync
        def _(sp):
            def load(b, s):
                sp.dma_start(x_next[s][:], x[b].rearrange("(t p) d -> p t d", p=P)).then_inc(s_x, 16)
                sp.dma_start(mrow_i, mask_rows0[bass.ds(b, 1), :]).then_inc(s_x, 16)

            def load_mask3(b):
                sp.dma_start(mrow3, mask_rows3[bass.ds(b, 1), :]).then_inc(s_mrow3, 16)

            def store(b, s):
                sp.wait_ge(s_out_ready, b + 1)
                sp.dma_start(out[b].rearrange("(t p) d -> p t d", p=P), x_res[s][:]).then_inc(s_out[s], 16)

            sp.dma_start(const_sb[:], const_pack).then_inc(s_const, 16)
            sp.dma_start(mask_i, mask_cols).then_inc(s_const, 16)
            sp.dma_start(order_i, order.partition_broadcast(P)).then_inc(s_out[0], 16)
            sp.dma_start(sel_sb[:], sel).then_inc(s_out[1], 16)
            sp.dma_start(film_sb[0], film_w[0].rearrange("(k p) n -> p k n", p=P)).then_inc(s_cond_w, 16)
            sp.dma_start(ada_sb[1], ada_w[1].rearrange("(k p) n -> p k n", p=P)).then_inc(s_cond_w, 16)
            load(0, 0)
            load_mask3(0)
            sp.dma_start(att_sb[0][:], att_packs[0]).then_inc(s_att_w, 16)
            sp.dma_start(ssm_sb[1][:], ssm_packs[1]).then_inc(s_ssm_w, 16)
            sp.wait_ge(a_mask, 1)
            load(1, 1)
            with sp.Fori(0, PAIRS - 1) as p:
                for s in range(2):
                    sp.wait_ge(s_xfree, 2 * p + 1 + s)
                    load(2 * p + 2 + s, s)
                for s in range(2):
                    sp.wait_ge(s_m3free, 2 * p + 1 + s)
                    load_mask3(2 * p + 1 + s)
                    store(2 * p + s, s)
            sp.wait_ge(s_m3free, B - 1)
            load_mask3(B - 1)
            store(B - 2, 0)
            store(B - 1, 1)
            for s in range(2):
                sp.wait_ge(s_out[s], 16 * (PAIRS + 1))

        @block.gpsimd
        def _(pool):
            pool.memset(neg_half[:], -0.5).then_inc(s_zero, 1)
            pool.memset(decay[:, :, :, 0:1], 0.0).then_inc(s_zero, 1)
            pool.wait_ge(s_zero, 2)
            pool.wait_ge(s_setup, 1)

            def root(norm, var, done, k):
                pool.wait_ge(var, k)
                pool.tensor_tensor(norm["rstd"][:, :, 0], norm["var_eps"][:, :, 0], neg_half[:], ALU.pow).then_inc(done, 1)

            def mod_cols(b, at, n):
                return mod_all[:, bass.ds(b, 1), at:at + n].rearrange("p b m -> p (b m)")

            def attention(ai, layer, s, b):
                src = x_next[s] if layer == 0 else x_res[s]
                if not (isinstance(ai, int) and ai == 0):
                    pool.wait_ge(a_done, ai)
                pool.tensor_copy(mod_att[:], mod_cols(b, MOD_AT[layer], 2 * DC + TT)).then_inc(a_mod, 1)
                yield from rest(ATT_STAGES["lead"] + ATT_STAGES["norm"])
                root(att_norm, a_var, a_rstd, 2 * ai + 1)
                yield from rest(ATT_STAGES["root"] + ATT_STAGES["xn"])
                pool.wait_ge(a_xn, 2 * ai * TT + TT)
                layer_at = ATT.index(layer)
                pool.tensor_tensor(src[:], src[:], out_bias[:, layer_at:layer_at + 1, :].broadcast_to([P, TT, D]),
                                   ALU.add).then_inc(a_xb, 1)
                for stage in ("turn", "xnT", "k", "kmax", "kexp", "q", "qmax", "v", "vkeep", "kT", "knat", "qT", "qTs", "mix",
                              "att", "y", "ynorm"):
                    yield from rest(ATT_STAGES[stage])
                root(att_norm, a_var, a_rstd, 2 * ai + 2)
                for stage in ("yroot", "yn", "yturn", "hidden", "act", "out", "res"):
                    yield from rest(ATT_STAGES[stage])

            def step_sizes(pi, s, h):
                c = slice(h * HC, (h + 1) * HC)
                pool.wait_ge(p_ln, pi * HALVES + h + 1)
                pool.tensor_tensor(dt[s][:, c], dt[s][:, c], dtu[s][:, c], ALU.add).then_inc(p_dt, 1)

            def injected(pi, s, h):
                c = slice(h * HC, (h + 1) * HC)
                pool.wait_ge(p_dt, pi * HALVES + h + 1)
                pool.wait_ge(p_u, pi * CH + CH)
                pool.tensor_tensor(dtu[s][:, c], dt[s][:, c], u[s][:, c], ALU.mult).then_inc(p_dtu, 1)

            def before(pi, layer, s, b):
                yield from rest(PREP_STAGES[layer]["norm"])
                if not (isinstance(pi, int) and pi == 0):
                    pool.wait_ge(p_dtp, pi * CH)
                pool.wait_ge(p_var, pi + 1)
                pool.tensor_copy(mod_prep[:], mod_cols(b, MOD_AT[layer], 2 * DC)).then_inc(p_mod, 1)
                pool.memset(xpad[:, :, 0:TAPS - 1], 0.0).then_inc(p_pad, 1)
                root(prep_norm, p_var, p_rstd, pi + 1)
                for stage in ("root", "xn", "turn", "xnT", "in01", "in23", "z01", "z23", "u01", "u23", "x", "parts",
                              "dt01", "dt23", "soft"):
                    yield from rest(PREP_STAGES[layer][stage])
                step_sizes(pi, s, 0)
                yield from rest(PREP_STAGES[layer]["dt"] // 2)
                injected(pi, s, 0)
                yield from rest((PREP_STAGES[layer]["dt"] + 1) // 2)

            def after(qi, layer, s, b):
                pool.tensor_copy(gate_pick[:], mod_cols(b, MOD_PICK, 1)).then_inc(o_pick, 1)
                yield from rest(POST_TICKS[layer])

            def inject(scan_, k):
                si, s = scan_.si, scan_.s
                c = slice(k // N * HC, k // N * HC + HC)
                if k % N == 0:
                    pool.wait_ge(p_dtu, si * HALVES + k // N + 1)
                pool.wait_ge(m_brow, si * UNITS + k + 1)
                if not (isinstance(si, int) and si * UNITS + k < STATES):
                    if k % QUAD < 2:
                        pool.wait_ge(m_pair, si * QUADS + k // QUAD)
                    else:
                        pool.wait_ge(m_sum, si * QUADS * SUMS + k // QUAD * SUMS + k % QUAD - 3)
                pool.tensor_tensor(state[:, k % STATES], dtu[s][:, c],
                                   b_rows[:, k % B_ROWS:k % B_ROWS + 1, :].broadcast_to([P, HC, T]),
                                   ALU.mult).then_inc(m_inject, 1)

            def add_pair(si, quad):
                pool.wait_ge(m_prod, si * UNITS + quad * QUAD + 2)
                if not (isinstance(si, int) and si * QUADS + quad == 0):
                    pool.wait_ge(m_sum, si * QUADS * SUMS + quad * SUMS - 2)
                pool.tensor_tensor(pair[:], state[:, 0], state[:, 1], ALU.add).then_inc(m_pair, 1)

            def scan(this):
                si, s = this.si, this.s
                if isinstance(si, int) and si == 0:
                    inject(this, 0)
                    inject(this, 1)
                for k in range(UNITS):
                    if k % QUAD == 2:
                        add_pair(si, k // QUAD)
                    if k == 3:
                        step_sizes(si, s, 1)
                    if k == 5:
                        injected(si, s, 1)
                    yield
                    if this.at(k + 2):
                        inject(*this.at(k + 2))
                    if k == N + 3:
                        pool.wait_ge(m_skip, si * HALVES + 1)
                        pool.tensor_tensor(u[s][:, 0:HC], u[s][:, 0:HC], zh[s][:, 0:HC], ALU.mult).then_inc(m_half0, 1)
                    yield

            run_batches(pool, attention, before, after, scan)

        @block.scalar
        def _(act):
            act.dma_start(film_sb[3], film_w[3].rearrange("(k p) n -> p k n", p=P)).then_inc(s_cond_w, 16)
            act.dma_start(ada_sb[2], ada_w[2].rearrange("(k p) n -> p k n", p=P)).then_inc(s_cond_w, 16)
            for n, layer in enumerate(ATT):
                for r in range(2):
                    act.dma_start(qv_bias[layer][:, r * D:(r + 1) * D], att_rows[layer][r].unsqueeze(0)).then_inc(s_rows, 16)
                act.dma_start(out_bias[:, n], att_rows[layer][2].partition_broadcast(P)).then_inc(s_rows, 16)
            for n in range(2):
                act.dma_start(gate_bias[:, n], gate_rows[n].partition_broadcast(B)).then_inc(s_rows, 16)
            act.dma_start(att_sb[3][:], att_packs[3]).then_inc(s_att_w, 16)
            act.dma_start(ssm_sb[2][:], ssm_packs[2]).then_inc(s_ssm_w, 16)
            act.wait_ge(s_const, 32)
            act.activation(silu_c.rearrange("p k b -> p (k b)"), cw("cond"), ACT.Tanh, scale=0.5).then_inc(s_silu_t, 1)
            act.wait_ge(s_ssm_w, 32)
            for layer in SSM:
                act.activation(neg_a[layer][:], sw(layer, "a_log"), ACT.Exp).then_inc(s_neg_a, 1)
            act.wait_ge(s_setup, 1)

            def attention(ai, layer, s, b):
                for stage in ("lead", "norm", "root", "xn", "turn"):
                    yield from rest(ATT_STAGES[stage])
                for c in range(DC):
                    act.wait_ge(a_xT, ai * DC + c + 1)
                    act.activation(xnT[:, c, :], pa[c][:], ACT.Identity, scale=aw(layer, "norm_g")[:, c:c + 1],
                                   bias=aw(layer, "norm_b")[:, c:c + 1]).then_inc(a_xnT, 1)
                for stage in ("xnT", "k", "kmax"):
                    yield from rest(ATT_STAGES[stage])
                act.wait_ge(a_kshift, ai + 1)
                for c in range(DC):
                    act.activation(kexp[:, c, :], pa[c][:], ACT.Exp, bias=kshift[:, c:c + 1],
                                   accum_out=ksum[:, c:c + 1]).then_inc(a_kexp, 1)
                for stage in ("kexp", "q", "qmax"):
                    yield from rest(ATT_STAGES[stage])
                for h in range(2):
                    act.wait_ge(a_qsub, ai * 2 + h + 1)
                    act.activation(q[:, 2 * h:2 * h + 2, :], q[:, 2 * h:2 * h + 2, :], ACT.Exp).then_inc(a_qexp, 1)
                yield from rest(ATT_STAGES["v"])
                act.wait_ge(a_mod, ai + 1)
                for t in range(TT):
                    if t % 2 == 0:
                        act.wait_ge(a_v, ai * 2 + t // 2 + 1)
                    act.activation(v[:, t, :], pa[t // 2][:, (t % 2) * D:(t % 2 + 1) * D], ACT.Copy,
                                   scale=mod_att[:, 2 * DC + t:2 * DC + t + 1]).then_inc(a_vs, 1)
                yield from rest(ATT_STAGES["vkeep"] + ATT_STAGES["kT"])
                act.wait_ge(a_kT, ai * 2 + 2)
                for h in range(2):
                    act.activation(knat[:, 2 * h:2 * h + 2, :].rearrange("p t d -> p (t d)"), pa[h][:],
                                   ACT.Copy).then_inc(a_knat, 1)
                yield from rest(ATT_STAGES["knat"] + ATT_STAGES["qT"])
                for c in range(DC):
                    act.wait_ge(a_qT, ai * DC + c + 1)
                    act.activation(qT[:, c, :], pa[c][:], ACT.Copy).then_inc(a_qTs, 1)
                for stage in ("qTs", "mix", "att", "y", "ynorm", "yroot", "yn", "yturn"):
                    yield from rest(ATT_STAGES[stage])
                for c in range(DC):
                    act.wait_ge(a_yT, ai * DC + c + 1)
                    args = dict(scale=mod_att[:, c:c + 1], bias=mod_att[:, DC + c:DC + c + 1])
                    act.activation(kexp[:, c, :], pa[c][:], ACT.Identity, **args)
                    act.activation(qT[:, c, :], pa[c][:], ACT.Tanh, **args).then_inc(a_hid, 1)
                for stage in ("hidden", "act", "out", "res"):
                    yield from rest(ATT_STAGES[stage])

            def exp_abs(pi, s, h):
                act.wait_ge(p_abs, pi * CH + (h + 1) * HC)
                act.activation(dt[s][:, h * HC:(h + 1) * HC], dt[s][:, h * HC:(h + 1) * HC], ACT.Exp,
                               scale=-1.0).then_inc(p_exp, 1)

            def log(pi, s, h):
                act.wait_ge(p_exp, pi * HALVES + h + 1)
                act.activation(dt[s][:, h * HC:(h + 1) * HC], dt[s][:, h * HC:(h + 1) * HC], ACT.Ln,
                               bias=1.0).then_inc(p_ln, 1)

            def before(pi, layer, s, b):
                for stage in ("norm", "root", "xn", "turn"):
                    yield from rest(PREP_STAGES[layer][stage])
                act.wait_ge(p_mod, pi + 1)
                for c in range(DC):
                    act.wait_ge(p_xT, pi * DC + c + 1)
                    act.activation(prep_xnT[s][:, c, :], pb[c][:], ACT.Identity, scale=mod_prep[:, c:c + 1],
                                   bias=mod_prep[:, DC + c:DC + c + 1]).then_inc(p_xnT, 1)
                yield from rest(PREP_STAGES[layer]["xnT"])
                for stage, first in (("in01", 0), ("in23", 2)):
                    yield from rest(PREP_STAGES[layer][stage])
                    for c in range(2):
                        act.wait_ge(p_in, pi * 2 * CH + first + c + 1)
                        act.activation(xpad[:, first + c, TAPS - 1:], pb[c][:], ACT.Copy).then_inc(p_xpad, 1)
                def half_z(c):
                    act.wait_ge(p_in, pi * 2 * CH + (CH + 2 if c < 2 else 2 * CH))
                    act.activation(zh[s][:, c, :], pb[c % 2][:], ACT.Copy, scale=0.5)
                    act.activation(zt[s][:, c, :], pb[c % 2][:], ACT.Tanh, scale=0.5).then_inc(p_z, 1)

                def tanh_u(c):
                    act.wait_ge(p_conv, pi * CH + c + 1)
                    act.activation(dt[s][:, c, :], u[s][:, c, :], ACT.Tanh).then_inc(p_ut, 1)

                def take(first):
                    for step, c in ((half_z, first), (half_z, first + 1), (tanh_u, first), (tanh_u, first + 1)):
                        step(c)
                        yield

                yield from rest(PREP_STAGES[layer]["z01"])
                yield from paced(PREP_STAGES[layer]["z23"], 4, take(0))
                yield from paced(PREP_STAGES[layer]["u01"], 4, take(2))
                yield from rest(PREP_STAGES[layer]["u23"])
                yield from rest(PREP_STAGES[layer]["x"])
                act.wait_ge(p_x, pi + 1)
                act.activation(dtr, pb[0][0:DTR, :], ACT.Copy).then_inc(p_dtr, 1)
                yield from rest(PREP_STAGES[layer]["parts"])
                act.wait_ge(p_sz, pi * CH + CH)
                def steps(h):
                    for c in range(h * HC, (h + 1) * HC):
                        bias = sw(layer, "dt_b")[:, c:c + 1]
                        act.wait_ge(p_dtp, pi * CH + c + 1)
                        act.activation(dt[s][:, c, :], pb[(c + 1) % 2][:], ACT.Abs, bias=bias)
                        act.activation(dtu[s][:, c, :], pb[(c + 1) % 2][:], ACT.Relu, bias=bias).then_inc(p_abs, 1)
                        yield
                    exp_abs(pi, s, h)
                    yield

                yield from rest(PREP_STAGES[layer]["dt01"])
                yield from paced(PREP_STAGES[layer]["dt23"], HC + 1, steps(0))
                yield from paced(PREP_STAGES[layer]["soft"] // 2, HC + 1, steps(1))
                log(pi, s, 0)
                yield from rest((PREP_STAGES[layer]["soft"] + 1) // 2)
                yield from rest(PREP_STAGES[layer]["dt"])

            def after(qi, layer, s, b):
                act.wait_ge(m_decay, (qi + 1) * UNITS * HC)
                act.wait_ge(o_pick, qi + 1)
                act.activation(gate_row[s], gate_nat[:, layer - 1, :], ACT.Copy, scale=gate_pick[on_gates, :]).then_inc(o_row, 1)
                yield from rest(POST_STAGES[layer]["lead"] - 2)
                act.wait_ge(o_gps, qi + 1)
                act.activation(gate[s], pb[0][:, 0:D], ACT.Copy).then_inc(o_gate, 1)
                yield from rest(POST_TICKS[layer] - POST_STAGES[layer]["lead"] + 2)

            def copy_b(scan_, k):
                act.wait_ge(m_bps, scan_.si * UNITS + k + 1)
                wait_back(act, m_inject, scan_.si, k, B_ROWS)
                act.activation(b_rows[:, k % B_ROWS, :], b_bank[:], ACT.Copy).then_inc(m_brow, 1)

            def copy_c(scan_, k):
                act.wait_ge(m_cps, scan_.si * UNITS + k + 1)
                wait_back(act, m_prod, scan_.si, k, C_ROWS)
                act.activation(c_rows[:, k % C_ROWS, :], c_bank[:], ACT.Copy).then_inc(m_crow, 1)

            def decays(scan_, k):
                si, layer, s = scan_.si, scan_.layer, scan_.s
                if k % N == 0:
                    act.wait_ge(p_dt, si * HALVES + k // N + 1)
                wait_back(act, m_scan, si, k, DECAYS)
                for c in range(HC):
                    at = (k // N * HC + c) * N + k % N
                    act.activation(decay[:, k % DECAYS, c, 1:], dt[s][:, k // N * HC + c, 1:], ACT.Exp,
                                   scale=neg_a[layer][:, at:at + 1]).then_inc(m_decay, 1)

            def scan(this):
                if isinstance(this.si, int) and this.si == 0:
                    copy_b(this, 0)
                    copy_b(this, 1)
                    decays(this, 0)
                    copy_c(this, 0)
                    decays(this, 1)
                    copy_b(this, 2)
                for k in range(UNITS):
                    if this.at(k + 2):
                        decays(*this.at(k + 2))
                    if k == 1:
                        log(this.si, this.s, 1)
                    yield
                    for ahead, step in ((1, copy_c), (AHEAD, copy_b)):
                        if this.at(k + ahead):
                            step(*this.at(k + ahead))
                    yield

            run_batches(act, attention, before, after, scan)

        @block.vector
        def _(dve):
            pro = [0]

            def setup_link(ins):
                pro[0] += 1
                ins.then_inc(s_links, 1)
                dve.wait_ge(s_links, pro[0])

            dve.wait_ge(s_const, 32)
            for s in range(2):
                dve.wait_ge(s_out[s], 16)
            dve.wait_ge(s_silu_t, 1)
            flat_c = silu_c.rearrange("p k b -> p (k b)")
            setup_link(dve.scalar_tensor_tensor(flat_c, flat_c, 1.0, cw("cond"), ALU.add, ALU.mult))
            dve.tensor_scalar(flat_c, flat_c, 0.5, None, ALU.mult).then_inc(s_silu, 1)
            keep0, keep3 = (mod_all[:, :, MOD_AT[n] + 2 * DC:MOD_AT[n] + 2 * DC + TT] for n in ATT)
            setup_link(dve.tensor_scalar(keep0, mask_i.rearrange("p (b t) -> p b t", t=TT), 1.0, None, ALU.is_equal))
            setup_link(dve.tensor_scalar(keep0, keep0, -1.0, 1.0, ALU.mult, ALU.add))
            setup_link(dve.tensor_copy(keep3, cw("keep3").rearrange("p (b t) -> p b t", t=TT)))
            setup_link(dve.tensor_copy(mod_all[:, :, MOD_PICK], ident[:, GATES_AT:GATES_AT + B]))
            ordf = xn[:].rearrange("p t d -> p (t d)")[:, 0:T]
            setup_link(dve.tensor_copy(ordf, order_i))
            for t in range(TT):
                dve.tensor_scalar(permute[:, t, :], ordf, cw("token")[:, t:t + 1], None, ALU.is_equal)
            dve.wait_ge(s_rows, 16 * 8)
            dve.wait_ge(s_att_w, 32)
            dve.wait_ge(s_ssm_w, 32)
            for n, layer in enumerate(SSM):
                dve.tensor_scalar(half_w[layer][:], sw(layer, "conv_w"), 0.5, None, ALU.mult)
                dve.tensor_scalar(half_cb[layer][:], sw(layer, "conv_b"), 0.5, None, ALU.mult)
                dve.wait_ge(s_neg_a, n + 1)
                setup_link(dve.tensor_scalar(neg_a[layer][:], neg_a[layer][:], -1.0, None, ALU.mult))

            for n, layer in enumerate((0, 1, 2, 3)):
                dve.wait_ge(s_cond_pe, n + 1)
                is_att = layer in ATT
                m = 2 * DC if is_att else 3 * DC
                bias = aw(layer, "emb_b") if is_att else sw(layer, "ada_b")
                g, b = ((aw(layer, "film_g"), aw(layer, "film_b")) if is_att
                        else (sw(layer, "norm_g"), sw(layer, "norm_b")))
                raw = mod_raw[:, 0:m, :]
                setup_link(dve.tensor_tensor(raw, bank[n][:, 0:m * B].rearrange("p (m b) -> p m b", b=B),
                                             bias.unsqueeze(2).broadcast_to([P, m, B]), ALU.add))
                at_scale, at_shift = (0, DC) if is_att else (DC, 0)
                for c in range(DC):
                    sc, sh = raw[:, at_scale + c, :], raw[:, at_shift + c, :]
                    to_s = mod_all[:, :, MOD_AT[layer] + c]
                    to_h = mod_all[:, :, MOD_AT[layer] + DC + c]
                    setup_link(dve.tensor_scalar(to_s, sc, 1.0, g[:, c:c + 1], ALU.add, ALU.mult))
                    setup_link(dve.tensor_scalar(to_h, sc, 1.0, b[:, c:c + 1], ALU.add, ALU.mult))
                    setup_link(dve.tensor_tensor(to_h, to_h, sh, ALU.add))
                if is_att:
                    both = mod_all[:, :, MOD_AT[layer]:MOD_AT[layer] + 2 * DC]
                    setup_link(dve.tensor_scalar(both, both, 0.5, None, ALU.mult))
            for n in range(2):
                dve.wait_ge(s_cond_pe, 5 + n)
                dve.tensor_tensor(gate_nat[:, n, :], bank[4 + n][0:B, 0:D], gate_bias[:, n, :], ALU.add).then_inc(s_gate_nat, 1)
            dve.wait_ge(s_gate_nat, 2)
            dve.wait_ge(s_zero, 2)
            dve.memset(prep_norm["stats"][:], 0.0)
            dve.memset(att_norm["stats"][:], 0.0).then_inc(s_setup, 1)
            dve.wait_ge(s_setup, 1)

            def moments(norm, src, var, link):
                stats, mv, var_eps = norm["stats"], norm["mv"], norm["var_eps"]
                for t in range(TT):
                    ins = dve.bn_stats(stats[:, t, :], src(t))
                link(ins)
                dve.tensor_copy(var_eps[:, :, 0], stats[:, :, 2])
                for t in range(TT):
                    ins = dve.bn_aggr(mv[:, t, :], stats[:, t, :])
                link(ins)
                dve.tensor_scalar(var_eps[:, :, 0], mv[:, :, 1], EPS, None, ALU.add).then_inc(var, 1)

            def normed(norm, src, dst, root, k, done):
                dve.wait_ge(root, k)
                for t in range(TT):
                    dve.tensor_scalar(dst[:, t, :], src(t), norm["mv"][:, t, 0:1], norm["rstd"][:, t, 0:1], ALU.subtract,
                                      ALU.mult).then_inc(done, 1)

            def chain(sem_, base, length):
                count = [0]

                def link(ins):
                    count[0] += 1
                    ins.then_inc(sem_, 1)
                    dve.wait_ge(sem_, base * length + count[0])
                return link, count

            def halves(tile, h):
                return tile[:, 2 * h:2 * h + 2, :]

            def by_token(b):
                return b[:].rearrange("p (t d) -> p t d", d=D)

            def attention(ai, layer, s, b):
                heads = HEADS[ATT.index(layer)]
                width = D // heads
                link, count = chain(a_links, ai, ATT_LINKS)
                src = x_next[s] if layer == 0 else x_res[s]
                yield from rest(ATT_STAGES["lead"])
                if layer == 0:
                    dve.wait_ge(s_x, 32 * b + 32)
                    link(dve.tensor_scalar(mask_row, mrow_i, 1.0, None, ALU.is_equal))
                    dve.tensor_scalar(mask_row, mask_row, MASKED, None, ALU.mult).then_inc(a_mask, 1)
                else:
                    dve.wait_ge(s_mrow3, 16 * b + 16)
                    link(dve.tensor_scalar(mask_row, mrow3, -1.0, 1.0, ALU.mult, ALU.add))
                    dve.sem_inc(s_m3free, 1)
                    dve.tensor_scalar(mask_row, mask_row, -1000000.0, None, ALU.mult).then_inc(a_mask, 1)
                moments(att_norm, lambda t: src[:, t, :], a_var, link)
                yield from rest(ATT_STAGES["norm"] + ATT_STAGES["root"])
                normed(att_norm, lambda t: src[:, t, :], xn, a_rstd, 2 * ai + 1, a_xn)
                for stage in ("xn", "turn", "xnT", "k"):
                    yield from rest(ATT_STAGES[stage])
                for c in range(DC):
                    dve.wait_ge(a_k, ai * DC + c + 1)
                    ins = dve.tensor_reduce(kmax[:, c:c + 1], pa[c][:], AX, ALU.max)
                link(ins)
                link(dve.tensor_tensor(kmax[:], kmax[:], aw(layer, "bk"), ALU.add))
                dve.tensor_tensor(kshift[:], aw(layer, "bk"), kmax[:], ALU.subtract).then_inc(a_kshift, 1)
                yield from rest(ATT_STAGES["kmax"] + ATT_STAGES["kexp"])
                dve.wait_ge(a_kexp, ai * DC + DC)
                link(dve.reciprocal(krec[:], ksum[:]))
                for c in range(DC):
                    dve.tensor_scalar(kexp[:, c, :], kexp[:, c, :], krec[:, c:c + 1], None, ALU.mult).then_inc(a_kn, 1)
                yield from rest(ATT_STAGES["q"])
                qs = qstat[:, 0:TT * heads]
                for h in range(2):
                    qsh = qs[:, h * 2 * heads:(h + 1) * 2 * heads]
                    dve.wait_ge(a_q, ai * 2 + h + 1)
                    ins = dve.tensor_reduce(qsh, pa[h][:].rearrange("p (g w) -> p g w", w=width), AX, ALU.max)
                link(ins)
                for h in range(2):
                    qsh = qs[:, h * 2 * heads:(h + 1) * 2 * heads]
                    dve.tensor_tensor(halves(q, h).rearrange("p t (g w) -> p (t g) w", w=width),
                                      pa[h][:].rearrange("p (g w) -> p g w", w=width),
                                      qsh.unsqueeze(2).broadcast_to([P, 2 * heads, width]), ALU.subtract).then_inc(a_qsub, 1)
                yield from rest(ATT_STAGES["qmax"] + ATT_STAGES["v"])
                qh = q[:].rearrange("p t (g w) -> p (t g) w", w=width)
                dve.wait_ge(a_qexp, ai * 2 + 2)
                link(dve.tensor_reduce(qs, qh, AX, ALU.add))
                link(dve.reciprocal(qs, qs))
                dve.tensor_tensor(qh, qh, qs.unsqueeze(2).broadcast_to([P, TT * heads, width]), ALU.mult).then_inc(a_qn, 1)
                for stage in ("vkeep", "kT", "knat", "qT", "qTs", "mix"):
                    yield from rest(ATT_STAGES[stage])
                for c in range(DC):
                    dve.wait_ge(a_att, ai * DC + c + 1)
                    dve.tensor_tensor(att[:, c, :], pa[c][:, 0:P], aw(layer, "heads"), ALU.mult).then_inc(a_atts, 1)
                yield from rest(ATT_STAGES["att"] + ATT_STAGES["y"])
                dve.wait_ge(a_y, ai * TT + TT)
                ysrc = lambda t: pa[t // 2][:, (t % 2) * D:(t % 2 + 1) * D]
                moments(att_norm, ysrc, a_var, link)
                yield from rest(ATT_STAGES["ynorm"] + ATT_STAGES["yroot"])
                normed(att_norm, ysrc, xn, a_rstd, 2 * ai + 2, a_xn)
                for stage in ("yn", "yturn", "hidden"):
                    yield from rest(ATT_STAGES[stage])
                for c in range(DC):
                    dve.wait_ge(a_hid, ai * DC + c + 1)
                    dve.scalar_tensor_tensor(xnT[:, c, :], qT[:, c, :], 1.0, kexp[:, c, :], ALU.add,
                                             ALU.mult).then_inc(a_act, 1)
                yield from rest(ATT_STAGES["act"] + ATT_STAGES["out"])
                dve.wait_ge(a_xb, ai + 1)
                for h in range(2):
                    dve.wait_ge(a_o, ai * 2 + h + 1)
                    ins = dve.tensor_tensor(halves(src, h), by_token(pa[h]), halves(src, h), ALU.add)
                ins.then_inc(a_done, 1)
                dve.wait_ge(a_done, ai + 1)
                if layer == 3:
                    dve.sem_inc(s_out_ready, 1)
                yield from rest(ATT_STAGES["res"])
                assert count[0] == ATT_LINKS, count

            def before(pi, layer, s, b):
                link, count = chain(p_links, pi, PREP_LINKS)
                src = x_next[s] if layer == 1 else x_res[s]
                moments(prep_norm, lambda t: src[:, t, :], p_var, link)
                yield from rest(PREP_STAGES[layer]["norm"] + PREP_STAGES[layer]["root"])
                normed(prep_norm, lambda t: src[:, t, :], prep_xn[s], p_rstd, pi + 1, p_xn)
                for stage in ("xn", "turn", "xnT", "in01", "in23"):
                    yield from rest(PREP_STAGES[layer][stage])
                dve.wait_ge(p_pad, pi + 1)
                def convolve(first):
                    for k in range(TAPS):
                        for c in range(first, first + 2):
                            w = half_w[layer][:, c * TAPS + k:c * TAPS + k + 1]
                            if k == 0:
                                dve.wait_ge(p_xpad, pi * CH + c + 1)
                                ins = dve.tensor_scalar(u[s][:, c, :], xpad[:, c, 0:T], w, half_cb[layer][:, c:c + 1],
                                                        ALU.mult, ALU.add)
                            else:
                                ins = dve.scalar_tensor_tensor(u[s][:, c, :], xpad[:, c, k:k + T], w, u[s][:, c, :],
                                                               ALU.mult, ALU.add)
                                if k == TAPS - 1:
                                    ins.then_inc(p_conv, 1)
                        if k < TAPS - 1:
                            link(ins)
                        yield

                yield from paced(PREP_STAGES[layer]["z01"], TAPS, convolve(0))
                yield from paced(PREP_STAGES[layer]["z23"], TAPS, convolve(2))
                for first, stage in ((0, "u01"), (2, "u23")):
                    for c in range(first, first + 2):
                        dve.wait_ge(p_ut, pi * CH + c + 1)
                        dve.scalar_tensor_tensor(u[s][:, c, :], dt[s][:, c, :], 1.0, u[s][:, c, :], ALU.add,
                                                 ALU.mult).then_inc(p_u, 1)
                    yield from rest(PREP_STAGES[layer][stage])
                def silu_z():
                    for c in range(CH):
                        dve.wait_ge(p_z, pi * CH + c + 1)
                        dve.scalar_tensor_tensor(zh[s][:, c], zt[s][:, c], 1.0, zh[s][:, c], ALU.add, ALU.mult).then_inc(p_sz, 1)
                        yield

                yield from paced(PREP_STAGES[layer]["x"], CH, silu_z())
                parts = bc_parts[s]
                dve.wait_ge(p_x, pi + 1)
                rows, part = pb[0][DTR:DTR + NB, :], lambda k: parts[k * NB:(k + 1) * NB, :]
                link(dve.tensor_copy(part(2), rows))
                link(dve.tensor_tensor(bc_rest, rows, part(2), ALU.subtract))
                link(dve.tensor_copy(bc_mid, bc_rest))
                dve.tensor_copy(part(1), bc_mid)
                link(dve.tensor_tensor(part(0), bc_rest, bc_mid, ALU.subtract))
                dve.sem_inc(p_parts, 1)
                for stage in ("parts", "dt01", "dt23"):
                    yield from rest(PREP_STAGES[layer][stage])
                for stage in ("soft", "dt"):
                    yield from rest(PREP_STAGES[layer][stage])
                assert count[0] == PREP_LINKS, count

            def skip(s, layer, h, si):
                dve.wait_ge(m_sum, (si * QUADS + (h + 1) * (N // QUAD)) * SUMS)
                for c in range(HC):
                    at = h * HC + c
                    ins = dve.scalar_tensor_tensor(u[s][:, at, :], u[s][:, at, :], sw(layer, "d_skip")[:, at:at + 1],
                                                   y_banks[c][:], ALU.mult, ALU.add)
                ins.then_inc(m_skip, 1)

            def after(qi, layer, s, b):
                link, count = chain(o_links, qi, POST_LINKS)
                yield from rest(POST_STAGES[layer]["lead"])
                skip(s, layer, 1, qi)
                dve.wait_ge(m_skip, qi * HALVES + 2)
                dve.tensor_tensor(u[s][:, HC:], u[s][:, HC:], zh[s][:, HC:], ALU.mult).then_inc(o_gated, 1)
                yield from rest(POST_STAGES[layer]["skip"] + POST_STAGES[layer]["out"])
                dve.wait_ge(o_gate, qi + 1)
                for h in range(2):
                    dve.wait_ge(o_o, qi * 2 + h + 1)
                    dve.tensor_tensor(halves(gated_out[s], h), by_token(pb[h]), gate[s].unsqueeze(1).broadcast_to([P, 2, D]),
                                      ALU.mult).then_inc(o_og, 1)
                if layer == 1:
                    dve.wait_ge(o_og, qi * 2 + 2)
                    dve.wait_ge(s_out[s], 8 * (b - s) + 16)
                    link(dve.tensor_tensor(x_res[s][:], x_next[s][:], gated_out[s], ALU.add))
                    dve.sem_inc(s_xfree, 1)
                yield from rest(POST_STAGES[layer]["gate"] + POST_STAGES[layer]["gather"])
                if layer == 2:
                    for h in range(2):
                        dve.wait_ge(o_g, (qi // 4 * 2 + qi % 4 - 2) * 2 + h + 1 if isinstance(qi, int) else (b * 2 + h + 1))
                        ins = dve.tensor_tensor(halves(x_res[s], h), by_token(pb[h]), halves(x_res[s], h), ALU.add)
                    link(ins)
                yield from rest(POST_STAGES[layer]["res"])
                assert count[0] == POST_LINKS, count

            def scan_unit(scan_, k):
                dve.wait_ge(m_decay, (scan_.si * UNITS + k + 1) * HC)
                dve.wait_ge(m_inject, scan_.si * UNITS + k + 1)
                st = state[:, k % STATES].rearrange("p c t -> p (c t)")
                dve.tensor_tensor_scan(st, decay[:, k % DECAYS].rearrange("p c t -> p (c t)"), st, 0.0, ALU.mult,
                                       ALU.add).then_inc(m_scan, 1)

            def weight(scan_, k):
                dve.wait_ge(m_scan, scan_.si * UNITS + k + 1)
                dve.wait_ge(m_crow, scan_.si * UNITS + k + 1)
                st = state[:, k % STATES]
                dve.tensor_tensor(st, st, c_rows[:, k % C_ROWS:k % C_ROWS + 1, :].broadcast_to([P, HC, T]),
                                  ALU.mult).then_inc(m_prod, 1)

            def scan(this):
                if isinstance(this.si, int) and this.si == 0:
                    scan_unit(this, 0)
                for k in range(UNITS):
                    if this.at(k + 1):
                        scan_unit(*this.at(k + 1))
                    yield
                    weight(this, k)
                    if k == N + 1:
                        skip(this.s, this.layer, 0, this.si)
                    yield

            run_batches(dve, attention, before, after, scan)

        @block.tensor
        def _(pe):
            pe.wait_ge(s_const, 32)
            pe.wait_ge(s_silu, 1)
            pe.wait_ge(s_cond_w, 64)
            for n, layer in enumerate((0, 1, 2, 3)):
                w = film_sb[layer] if layer in ATT else ada_sb[layer]
                m = 2 * DC if layer in ATT else 3 * DC
                for c in range(m):
                    for k in range(EC):
                        ins = pe.matmul(bank[n][:, c * B:(c + 1) * B], w[:, k, c * P:(c + 1) * P], silu_c[:, k, :],
                                        start=(k == 0), stop=(k == EC - 1))
                ins.then_inc(s_cond_pe, 1)
            for n, layer in enumerate(SSM):
                for k in range(EC):
                    ins = pe.matmul(bank[4 + n][0:B, 0:D], silu_c[:, k, :], ada_sb[layer][:, k, 2 * D:3 * D],
                                    start=(k == 0), stop=(k == EC - 1))
                ins.then_inc(s_cond_pe, 1)
            pe.wait_ge(s_setup, 1)

            def turn(src, banks, done):
                for c in range(DC):
                    for t in range(TT):
                        ins = pe.transpose(banks[c][:, t * P:(t + 1) * P], src[:, t, c * P:(c + 1) * P], ident)
                        if t == TT - 1:
                            ins.then_inc(done, 1)
                        yield

            def per_token(banks, weights, lhs, chunks, done, ones=None, bias=None):
                for t in range(TT):
                    dst = banks[t // 2][:, (t % 2) * D:(t % 2 + 1) * D]
                    if bias is not None:
                        pe.matmul(dst, ones, bias, start=True, stop=False)
                    for c in range(chunks):
                        ins = pe.matmul(dst, lhs(c, t), weights(c), start=(c == 0 and bias is None), stop=(c == chunks - 1))
                        if t % 2 and c == chunks - 1:
                            ins.then_inc(done, 1)
                        yield

            def attention(ai, layer, s, b):
                w = {n: aw(layer, n).rearrange("p (c n) -> p c n", c=DC) for n in ("wq", "wk", "wv", "wo")}
                normT = lambda c, t: xnT[:, c, t * P:(t + 1) * P]

                def keys():
                    for e in range(DC):
                        for c in range(DC):
                            pe.matmul(pa[e][:], w["wk"][:, c, e * P:(e + 1) * P], xnT[:, c, :], start=(c == 0), stop=False)
                            yield
                        pe.matmul(pa[e][:], ones_row[0], mask_row, start=False, stop=True).then_inc(a_k, 1)
                        yield

                def keys_back():
                    for t in range(TT):
                        for c in range(DC):
                            ins = pe.transpose(pa[t // 2][:, (t % 2) * D + c * P:(t % 2) * D + (c + 1) * P],
                                               kexp[:, c, t * P:(t + 1) * P], ident)
                            if t % 2 and c == DC - 1:
                                ins.then_inc(a_kT, 1)
                            yield

                def mix():
                    over, free = (v, knat) if layer == 0 else (knat, v)
                    for c in range(DC):
                        for t in range(TT):
                            ins = pe.matmul(pa[c][:, 0:P], over[:, t, c * P:(c + 1) * P], free[:, t, c * P:(c + 1) * P],
                                            start=(t == 0), stop=(t == TT - 1))
                            if t == TT - 1:
                                ins.then_inc(a_att, 1)
                            yield

                def mixed():
                    for t in range(TT):
                        for c in range(DC):
                            ins = pe.matmul(pa[t // 2][:, (t % 2) * D + c * P:(t % 2) * D + (c + 1) * P],
                                            qT[:, c, t * P:(t + 1) * P], att[:, c, :], start=True, stop=True)
                            if c == DC - 1:
                                ins.then_inc(a_y, 1)
                            yield

                for stage in ("lead", "norm", "root", "xn"):
                    yield from rest(ATT_STAGES[stage])
                pe.wait_ge(a_xn, 2 * ai * TT + TT)
                yield from paced(ATT_STAGES["turn"], DC * TT, turn(xn, pa, a_xT))
                yield from rest(ATT_STAGES["xnT"])
                pe.wait_ge(a_xnT, ai * DC + DC)
                pe.wait_ge(a_mask, ai + 1)
                yield from paced(ATT_STAGES["k"], DC * (DC + 1), keys())
                yield from rest(ATT_STAGES["kmax"] + ATT_STAGES["kexp"])
                pe.wait_ge(a_kexp, ai * DC + DC)
                yield from paced(ATT_STAGES["q"], DC * TT, per_token(
                    pa, lambda c: w["wq"][:, c, :], normT, DC, a_q, ones_row[layer], qv_bias[layer][:, 0:D]))
                yield from rest(ATT_STAGES["qmax"])
                pe.wait_ge(a_qsub, ai * 2 + 2)
                yield from paced(ATT_STAGES["v"], DC * TT, per_token(
                    pa, lambda c: w["wv"][:, c, :], normT, DC, a_v, ones_row[layer], qv_bias[layer][:, D:]))
                yield from rest(ATT_STAGES["vkeep"])
                pe.wait_ge(a_kn, ai * DC + DC)
                pe.wait_ge(a_vs, ai * TT + TT)
                yield from paced(ATT_STAGES["kT"], DC * TT, keys_back())
                yield from rest(ATT_STAGES["knat"])
                pe.wait_ge(a_qn, ai + 1)
                pe.wait_ge(a_knat, ai * 2 + 2)
                yield from paced(ATT_STAGES["qT"], DC * TT, turn(q, pa, a_qT))
                yield from rest(ATT_STAGES["qTs"])
                pe.wait_ge(a_qTs, ai * DC + DC)
                yield from paced(ATT_STAGES["mix"], DC * TT, mix())
                yield from rest(ATT_STAGES["att"])
                pe.wait_ge(a_atts, ai * DC + DC)
                yield from paced(ATT_STAGES["y"], DC * TT, mixed())
                for stage in ("ynorm", "yroot", "yn"):
                    yield from rest(ATT_STAGES[stage])
                pe.wait_ge(a_xn, 2 * ai * TT + 2 * TT)
                yield from paced(ATT_STAGES["yturn"], DC * TT, turn(xn, pa, a_yT))
                for stage in ("hidden", "act"):
                    yield from rest(ATT_STAGES[stage])
                pe.wait_ge(a_act, ai * DC + DC)
                yield from paced(ATT_STAGES["out"], DC * TT, per_token(pa, lambda c: w["wo"][:, c, :], normT, DC, a_o))
                yield from rest(ATT_STAGES["res"])

            def before(pi, layer, s, b):
                w_in = sw(layer, "w_in").rearrange("p (c n) -> p c n", c=DC)
                w_x = sw(layer, "w_x").rearrange("p (c n) -> p c n", c=CH)
                w_dt = sw(layer, "w_dt")[0:DTR, :]

                xn, xnT = prep_xn[s], prep_xnT[s]

                def turn_and_gather():
                    for c in range(DC):
                        for t in range(TT):
                            ins = pe.matmul(pb[c][:], xn[:, t, c * P:(c + 1) * P], permute[:, t, :],
                                            start=(t == 0), stop=(t == TT - 1))
                            if t == TT - 1:
                                ins.then_inc(p_xT, 1)
                            yield

                def expand(first, taken, count):
                    for e in range(first, first + 2):
                        if taken is not None:
                            pe.wait_ge(taken, count + e - first)
                        for c in range(DC):
                            ins = pe.matmul(pb[e % 2][:], w_in[:, c, e * P:(e + 1) * P], xnT[:, c, :],
                                            start=(c == 0), stop=(c == DC - 1))
                            if c == DC - 1:
                                ins.then_inc(p_in, 1)
                            yield

                def steps_b_c():
                    for c in range(CH):
                        ins = pe.matmul(pb[0][0:DTR + NB, :], w_x[:, c, :], u[s][:, c, :], start=(c == 0), stop=(c == CH - 1))
                        if c == CH - 1:
                            ins.then_inc(p_x, 1)
                        yield

                def steps(first):
                    for c in range(first, first + 2):
                        if c == 0:
                            pe.wait_ge(p_dtr, pi + 1)
                        elif c == 1:
                            pe.wait_ge(p_parts, pi + 1)
                        else:
                            pe.wait_ge(p_abs, pi * CH + c - 1)
                        pe.matmul(pb[(c + 1) % 2][:], w_dt[:, c * P:(c + 1) * P], dtr, start=True, stop=True).then_inc(p_dtp, 1)
                        yield

                for stage in ("norm", "root", "xn"):
                    yield from rest(PREP_STAGES[layer][stage])
                pe.wait_ge(p_xn, pi * TT + TT)
                yield from paced(PREP_STAGES[layer]["turn"], DC * TT, turn(xn, pb, p_xT) if layer == 1 else turn_and_gather())
                yield from rest(PREP_STAGES[layer]["xnT"])
                pe.wait_ge(p_xnT, pi * DC + DC)
                yield from paced(PREP_STAGES[layer]["in01"], 2 * DC, expand(0, None, 0))
                yield from rest(1)
                yield from paced(PREP_STAGES[layer]["in23"] - 1, 2 * DC, expand(2, p_xpad, pi * CH + 1))
                yield from rest(1)
                yield from paced(PREP_STAGES[layer]["z01"] - 1, 2 * DC, expand(4, p_xpad, pi * CH + 3))
                yield from rest(1)
                yield from paced(PREP_STAGES[layer]["z23"] - 1, 2 * DC, expand(6, p_z, pi * CH + 1))
                for stage in ("u01", "u23"):
                    yield from rest(PREP_STAGES[layer][stage])
                pe.wait_ge(p_u, pi * CH + CH)
                pe.wait_ge(p_z, pi * CH + CH)
                yield from paced(PREP_STAGES[layer]["x"], CH, steps_b_c())
                yield from rest(PREP_STAGES[layer]["parts"])
                yield from paced(PREP_STAGES[layer]["dt01"], 2, steps(0))
                yield from rest(1)
                yield from paced(PREP_STAGES[layer]["dt23"] - 1, 2, steps(2))
                for stage in ("soft", "dt"):
                    yield from rest(PREP_STAGES[layer][stage])

            def after(qi, layer, s, b):
                w_out = sw(layer, "w_out").rearrange("p (c n) -> p c n", c=CH)
                stages = POST_STAGES[layer]
                yield from rest(2)
                pe.wait_ge(o_row, qi + 1)
                pe.matmul(pb[0][:, 0:D], ones_row8, gate_row[s], start=True, stop=True).then_inc(o_gps, 1)
                yield from rest(stages["lead"] - 2 + stages["skip"])
                pe.wait_ge(o_gated, qi + 1)
                pe.wait_ge(m_half0, qi + 1)
                pe.wait_ge(o_gate, qi + 1)
                yield from paced(stages["out"], CH * TT, per_token(
                    pb, lambda c: w_out[:, c, :], lambda c, t: u[s][:, c, t * P:(t + 1) * P], CH, o_o))
                yield from rest(stages["gate"])
                if layer == 2:
                    pe.wait_ge(o_og, qi * 2 + 2)
                    yield from paced(stages["gather"], TT * TT, per_token(
                        pb, lambda c: gated_out[s][:, c, :], lambda c, t: permute[:, c, t * P:(t + 1) * P], TT, o_g))
                else:
                    yield from rest(stages["gather"])
                yield from rest(stages["res"])

            def spread(scan_, row, dst, done):
                pe.matmul(dst[:], sel_sb[:, row:row + 1].broadcast_to([3 * NB, P]), bc_parts[scan_.s][:], start=True,
                          stop=True).then_inc(done, 1)

            def spread_b(scan_, k):
                if k == 0:
                    pe.wait_ge(p_parts, scan_.si + 1)
                wait_back(pe, m_brow, scan_.si, k, 1)
                spread(scan_, k % N, b_bank, m_bps)

            def spread_c(scan_, k):
                wait_back(pe, m_crow, scan_.si, k, 1)
                spread(scan_, N + k % N, c_bank, m_cps)

            def sum_up(si, src, ready, count, first=False, last=False):
                pe.wait_ge(ready, count)
                for c in range(HC):
                    ins = pe.matmul(y_banks[c][:], ident, src[:, c, :], start=first, stop=last)
                ins.then_inc(m_sum, 1)

            def sum_pair(si, quad):
                first = quad % (N // QUAD) == 0
                if first and not (isinstance(si, int) and si == 0 and quad == 0):
                    pe.wait_ge(m_skip, si * HALVES + quad // (N // QUAD))
                sum_up(si, pair, m_pair, si * QUADS + quad + 1, first=first)

            def sum_unit(si, k):
                sum_up(si, state[:, k % STATES], m_prod, si * UNITS + k + 1, last=(k % N == N - 1))

            def scan(this):
                si = this.si
                if isinstance(si, int) and si == 0:
                    spread_b(this, 0)
                    spread_b(this, 1)
                    spread_c(this, 0)
                    spread_b(this, 2)
                for k in range(UNITS):
                    for ahead, step in ((1, spread_c), (AHEAD, spread_b)):
                        if this.at(k + ahead):
                            step(*this.at(k + ahead))
                    if k % QUAD == 3:
                        sum_pair(si, k // QUAD)
                    yield
                    if k % QUAD == 3 or k % QUAD == 0 and not (isinstance(si, int) and si == 0 and k == 0):
                        sum_unit(si, k - 1)
                    yield
                if not this.then:
                    sum_unit(si, UNITS - 1)

            run_batches(pe, attention, before, after, scan)


def kernel(**inputs):
    import numpy as np
    import concourse.bacc as bacc
    from concourse import mybir as mb
    from concourse.bass_utils import run_bass_kernel_spmd as run

    a = {k: np.asarray(v) for k, v in inputs.items()}

    def chunks(w):
        c = w.shape[0] // P
        return w.reshape(c, P, -1).transpose(1, 0, 2).reshape(P, -1)

    def cols(vec):
        return vec.reshape(-1, P).T

    def rows_of(w):
        full = np.zeros((P, w.shape[1]), w.dtype)
        full[:w.shape[0]] = w
        return full

    def pack(parts, names):
        return np.ascontiguousarray(np.concatenate([parts[n] for n, _ in names], axis=1))

    arrays, args = {}, {}
    nc = bacc.Bacc("TRN2", target_bir_lowering=False, num_devices=1)

    def give(name, array):
        array = np.ascontiguousarray(array)
        arrays[name] = array
        return nc.dram_tensor(name, array.shape, mb.dt.from_np(array.dtype), kind="ExternalInput").ap()

    def heads(n):
        w = np.arange(P) // (D // n)
        return (w[:, None] == w[None, :]).astype(np.float32)

    att_packs, ssm_packs, film_w, ada_w, att_rows = {}, {}, {}, {}, {}
    for n, (layer, names) in enumerate((
            (0, ("norm_scale", "norm_bias", "film_emb_W", "film_emb_b", "film_norm_scale", "film_norm_bias",
                 "film_out_W", "film_out_b")),
            (3, ("ln_w", "ln_b", "W_emb", "b_emb", "ln2_w", "ln2_b", "W_out", "b_out")))):
        g = lambda s: a[f"L{layer}_cond_{s}"]
        ng, nb, ew, eb, fg, fb, ow, ob = (g(s) for s in names)
        parts = dict(wq=chunks(g("Wq")), wk=chunks(g("Wk")), wv=chunks(g("Wv")), wo=chunks(ow), bk=cols(g("bk")),
                     norm_g=cols(ng), norm_b=cols(nb), film_g=cols(fg), film_b=cols(fb), emb_b=cols(eb),
                     heads=heads(HEADS[n]))
        att_packs[layer] = give(f"att_pack_{layer}", pack(parts, ATT_PACK))
        film_w[layer] = give(f"film_w_{layer}", ew)
        att_rows[layer] = [give(f"att_row_{layer}_{k}", r) for k, r in enumerate((g("bq"), g("bv"), ob))]
    gate_rows = []
    for layer in SSM:
        g = lambda s: a[f"L{layer}_cond_{s}"]
        if layer == 1:
            w_in, w_x, w_dt, w_out, ada = (g(s).T for s in ("in_proj_w", "x_proj_w", "dt_proj_w", "out_proj_w", "ada_w"))
            conv, dt_b, ng, nb, ab = g("conv_w"), g("dt_proj_b"), g("ln_g"), g("ln_b"), g("ada_b")
        else:
            w_in, w_x, w_dt, w_out, ada = (g(s) for s in ("W_in", "W_xp", "W_dt", "W_out", "W_ada"))
            conv, dt_b, ng, nb, ab = g("conv_w")[:, 0, :], g("b_dt"), g("gamma"), g("beta"), g("b_ada")
        parts = dict(w_in=chunks(w_in), w_x=chunks(w_x), w_dt=rows_of(w_dt), w_out=chunks(w_out), conv_w=chunks(conv),
                     conv_b=cols(g("conv_b")), dt_b=cols(dt_b), a_log=chunks(g("A_log")), d_skip=cols(g("D_param")),
                     norm_g=cols(ng), norm_b=cols(nb), ada_b=cols(ab))
        ssm_packs[layer] = give(f"ssm_pack_{layer}", pack(parts, SSM_PACK))
        ada_w[layer] = give(f"ada_w_{layer}", ada)
        gate_rows.append(give(f"gate_row_{layer}", ab[2 * D:]))
    mask = a["mask_BxSx1_fk1"].reshape(B, T)
    by_tile = lambda m: m.reshape(B, TT, P).transpose(2, 0, 1).reshape(P, B * TT)
    parts = dict(ident=np.eye(P, dtype=np.float32), token=np.arange(T, dtype=np.float32).reshape(TT, P).T,
                 cond=a["cond_2048"].T.reshape(EC, P, B).transpose(1, 0, 2).reshape(P, EC * B),
                 keep3=by_tile(mask), ones=np.ones((P, P), np.float32))
    const_pack = give("const_pack", pack(parts, CONST_PACK))
    sel = np.tile(np.eye(NB), (3, 1)).astype(mb.dt.np(BF16))
    sel = give("sel", sel)
    order = give("order", a["itok_S_0_1023"])
    mask_cols = give("mask_cols", by_tile(a["mask_BxS_ik0"]))
    mask_rows0 = give("mask_rows0", a["mask_BxS_ik0"])
    mask_rows3 = give("mask_rows3", mask)
    x = give("x", a["x"])
    out = nc.dram_tensor("out", (B, T, D), mb.dt.float32, kind="ExternalOutput").ap()
    bass_cond_seq(nc, x, out, mask_cols, mask_rows0, mask_rows3, order, const_pack, sel, att_packs, ssm_packs,
                  film_w, ada_w, att_rows, gate_rows)
    r = run(nc, [arrays], core_ids=[0])
    return r.results[0]["out"]
```
